# Optimizing a Trainium2 kernel written in Bass

```python
import numpy as np
import jax
import jax.numpy as jnp

def _softmax(x, axis=-1):
    return jax.nn.softmax(x, axis=axis)

def _gelu(x):
    return jax.nn.gelu(x, approximate=True)

def _silu(x):
    return jax.nn.silu(x)

def _sigmoid(x):
    return jax.nn.sigmoid(x)

def _layernorm(x, axis=-1, eps=1e-05):
    m = jnp.mean(x, axis=axis, keepdims=True)
    v = jnp.var(x, axis=axis, keepdims=True)
    return (x - m) / jnp.sqrt(v + eps)

def _scatter_add(tgt, idx, src, axis=0):
    return tgt.at[idx].add(src)

def _segment_sum(src, seg, n):
    return jax.ops.segment_sum(src, seg, n)
kernel_name = 'mk_xattn_ffn_d1_seqx_r2_775490'

def setup_inputs(seed: int=0):
    np.random.seed(seed)
    _w = jnp.asarray

    def _rec_inputs():
        import jax
        import jax.numpy as jnp
        _rk = jax.random.key(seed)
        x = 7.22e-05 + 1 * jax.random.normal(jax.random.fold_in(_rk, 1), (2, 2048, 512), jnp.float32)
        _lenS = 2048 - jax.random.randint(jax.random.fold_in(_rk, 7), (2,), 0, max(1, 2048 // 4) + 1, jnp.int32)
        _lenS2 = 128 - jax.random.randint(jax.random.fold_in(_rk, 8), (2,), 0, max(1, 128 // 4) + 1, jnp.int32)
        _ctx_1024P = jax.random.normal(jax.random.fold_in(_rk, 11), (2, 16, 512), jnp.float32)
        _ctx_1024c = jax.random.dirichlet(jax.random.fold_in(_rk, 511), 0.3 * jnp.ones((16,), jnp.float32), (2, 128))
        _ctx_1024t = jnp.einsum('bsk,bkd->bsd', _ctx_1024c, _ctx_1024P)
        _ctx_1024t = _ctx_1024t * jax.lax.rsqrt(jnp.mean(jnp.square(_ctx_1024t)) + 1e-12) * 0.953939
        ctx_1024 = 4.13588e-05 + 0.999923 * (_ctx_1024t + 0.3 * jax.random.normal(jax.random.fold_in(_rk, 611), (2, 128, 512), jnp.float32))
        _validS = jnp.arange(2048)[None, :] < _lenS[:, None]
        _validS2 = jnp.arange(128)[None, :] < _lenS2[:, None]
        _causal = jnp.tril(jnp.ones((2048, 2048), dtype=bool))
        mask_1xSxS2_ff0 = jnp.where(jnp.ones((1, 2048, 128), dtype=bool), 0.0, -1000000000.0).astype(jnp.float32)
        return (x, ctx_1024, mask_1xSxS2_ff0)
    x, ctx_1024, mask_1xSxS2_ff0 = _rec_inputs()

    def _L0_xattn_setup():
        import jax, jax.numpy as jnp
        import numpy as np
        B, S, D_IN, D_MODEL = (4, 1024, 512, 512)
        key = jax.random.key(seed)
        ks = jax.random.split(key, 8)
        glorot = np.sqrt(6.0 / (D_IN + D_MODEL))
        inp = {'q': jax.random.normal(ks[0], (B, S, D_IN), dtype=jnp.float32), 'k': jax.random.normal(ks[1], (B, S, D_IN), dtype=jnp.float32), 'v': jax.random.normal(ks[2], (B, S, D_IN), dtype=jnp.float32), 'mask': jnp.zeros((1, S, S), dtype=jnp.float32), 'kernel_q': jax.random.uniform(ks[3], (1, 1, D_IN, D_MODEL), jnp.float32, -glorot, glorot), 'kernel_k': jax.random.uniform(ks[4], (1, 1, D_IN, D_MODEL), jnp.float32, -glorot, glorot), 'kernel_v': jax.random.uniform(ks[5], (1, 1, D_IN, D_MODEL), jnp.float32, -glorot, glorot), 'bias_q': 0.05 * jax.random.normal(ks[6], (D_MODEL,), dtype=jnp.float32), 'bias_k': 0.05 * jax.random.normal(ks[7], (D_MODEL,), dtype=jnp.float32), 'bias_v': 0.05 * jax.random.normal(jax.random.fold_in(key, 7), (D_MODEL,), dtype=jnp.float32)}
        return inp
    _L0_xattn_all = _L0_xattn_setup()
    _L0_xattn_in = {k: v for k, v in _L0_xattn_all.items() if k in ('kernel_q', 'kernel_k', 'kernel_v', 'bias_q', 'bias_k', 'bias_v')}
    del _L0_xattn_all

    def _L0_ffn_setup():
        import jax, jax.numpy as jnp
        import numpy as np
        B, N, D, E, R, K = (4, 1024, 512, 8, 128, 2)
        key = jax.random.key(seed)
        ks = jax.random.split(key, 5)
        scale = 0.02
        return {'x': jax.random.normal(ks[0], (B, N, D), dtype=jnp.float32), 'gate_w': jax.random.normal(ks[1], (D, E), dtype=jnp.float32) * scale, 'Wu': jax.random.normal(ks[2], (E, D, R), dtype=jnp.float32) * scale, 'Wv': jax.random.normal(ks[3], (E, D, R), dtype=jnp.float32) * scale, 'Wo': jax.random.normal(ks[4], (E, R, D), dtype=jnp.float32) * scale}
    _L0_ffn_all = _L0_ffn_setup()
    _L0_ffn_in = {k: v for k, v in _L0_ffn_all.items() if k in ('gate_w', 'Wu', 'Wv', 'Wo')}
    del _L0_ffn_all
    return {'x': x, 'ctx_1024': ctx_1024, 'mask_1xSxS2_ff0': mask_1xSxS2_ff0, 'L0_xattn_kernel_q': _L0_xattn_in['kernel_q'], 'L0_xattn_kernel_k': _L0_xattn_in['kernel_k'], 'L0_xattn_kernel_v': _L0_xattn_in['kernel_v'], 'L0_xattn_bias_q': _L0_xattn_in['bias_q'], 'L0_xattn_bias_k': _L0_xattn_in['bias_k'], 'L0_xattn_bias_v': _L0_xattn_in['bias_v'], 'L0_ffn_gate_w': _L0_ffn_in['gate_w'], 'L0_ffn_Wu': _L0_ffn_in['Wu'], 'L0_ffn_Wv': _L0_ffn_in['Wv'], 'L0_ffn_Wo': _L0_ffn_in['Wo']}

def reference(x, ctx_1024, mask_1xSxS2_ff0, L0_xattn_kernel_q, L0_xattn_kernel_k, L0_xattn_kernel_v, L0_xattn_bias_q, L0_xattn_bias_k, L0_xattn_bias_v, L0_ffn_gate_w, L0_ffn_Wu, L0_ffn_Wv, L0_ffn_Wo):
    import jax
    import jax.numpy as jnp

    def _L0_xattn_ref(q, k, v, mask, kernel_q, kernel_k, kernel_v, bias_q, bias_k, bias_v):
        import jax, jax.numpy as jnp
        import numpy as np
        B, S, D_IN, D_MODEL = (4, 1024, 512, 512)
        Wq, Wk, Wv = (kernel_q[0, 0], kernel_k[0, 0], kernel_v[0, 0])
        qp = jax.nn.relu(jnp.einsum('bsd,de->bse', q, Wq) + bias_q)
        kp = jax.nn.relu(jnp.einsum('bsd,de->bse', k, Wk) + bias_k)
        vp = jax.nn.relu(jnp.einsum('bsd,de->bse', v, Wv) + bias_v)
        scores = jax.nn.relu(jnp.einsum('bqe,bke->bqk', qp, kp))
        dk = jnp.asarray(kp.shape[-1], dtype=scores.dtype)
        logits = scores / jnp.sqrt(dk) + mask
        out = jax.nn.relu(jnp.einsum('bqk,bke->bqe', logits, vp))
        return out

    def _L0_ffn_ref(x, gate_w, Wu, Wv, Wo):
        import jax, jax.numpy as jnp
        import numpy as np
        B, N, D, E, R, K = (4, 1024, 512, 8, 128, 2)
        logits = jnp.einsum('bnd,de->bne', x, gate_w)
        topv, topi = jax.lax.top_k(logits, K)
        w = jax.nn.softmax(topv, axis=-1)
        u = jnp.einsum('bnd,edr->bner', x, Wu)
        v = jnp.einsum('bnd,edr->bner', x, Wv)
        s = jax.nn.silu(u) * v
        Y = jnp.einsum('bner,erd->bned', s, Wo)
        y_sel = jnp.take_along_axis(Y, topi[..., None], axis=2)
        out = jnp.einsum('bnkd,bnk->bnd', y_sel, w)
        return out
    x = x + _L0_xattn_ref(_layernorm(x, axis=-1), ctx_1024, ctx_1024, mask_1xSxS2_ff0, L0_xattn_kernel_q, L0_xattn_kernel_k, L0_xattn_kernel_v, L0_xattn_bias_q, L0_xattn_bias_k, L0_xattn_bias_v)
    x = x + _L0_ffn_ref(_layernorm(x, axis=-1), L0_ffn_gate_w, L0_ffn_Wu, L0_ffn_Wv, L0_ffn_Wo)
    return x

_drawn_inputs = setup_inputs


def setup_inputs(seed=0):
    import zlib

    import numpy as np

    out = dict(_drawn_inputs(seed))
    spreads = {}
    factors = {'L0_xattn_bias_q': 8.0,
     'L0_xattn_bias_k': 8.0,
     'L0_ffn_gate_w': 8.0,
     'L0_ffn_Wu': 8.0,
     'L0_ffn_Wv': 8.0,
     'L0_ffn_Wo': 8.0}
    for name, (base, spread) in spreads.items():
        noise = np.random.default_rng([zlib.crc32(name.encode()), seed]).standard_normal(out[name].shape)
        drawn = base * np.exp(spread * noise) if base else spread * noise
        out[name] = jnp.asarray(drawn.astype(out[name].dtype))
    for name, factor in factors.items():
        out[name] = (out[name] * factor).astype(out[name].dtype)
    return out
```

```python
import numpy as np
import concourse.bass as bass
from concourse import mybir
from contextlib import ExitStack

F32 = mybir.dt.float32
F32R = mybir.dt.float32r
BF16 = mybir.dt.bfloat16
I32 = mybir.dt.int32
U32 = mybir.dt.uint32
ALU = mybir.AluOpType
ACT = mybir.ActivationFunctionType
AX = mybir.AxisListType

P = 128
LOG_P = 7
D = 512
DC = D // P
NBATCH, SEQ = 2, 2048
KEYS = 128
E, R = 8, 128
TOK = NBATCH * SEQ
TPB = 2
BT = TPB * P
NB = TOK // BT
NB_G = NB // NBATCH
NTILE = TOK // P
TILES_B = SEQ // P
CAP = SEQ
DUMMY = NBATCH * E * CAP
NSLOT = DUMMY + P
TILES_G = 2 * SEQ // P + E - 1
TILES = NBATCH * TILES_G
SCALE = float(np.float32(1.0) / np.sqrt(np.float32(D)))
EPS = 1e-5
HI, LO = 0, 1


def ge(eng, sem, value):
    if isinstance(value, int) and value <= 0:
        return
    eng.wait_ge(sem, value)


class Step:

    def __init__(self, j, p):
        self.j, self.p = j, p

    @property
    def n(self):
        return 2 * self.j + self.p

    def __add__(self, k):
        q = self.p + k
        return Step(self.j + q // 2, q % 2)

    def within(self, count):
        return not isinstance(self.j, int) or 0 <= self.n < count


def block_steps(eng, body):
    def straight(a, b):
        for n in range(a, b):
            body(Step(n // 2, n % 2), min(max(n // NB_G, 0), 1))

    def looped(a, b, batch):
        with eng.Fori(0, (b - a) // 2) as i:
            for p in range(2):
                body(Step(i + a // 2, p), batch)

    straight(-1, 4)
    looped(4, NB_G, 0)
    straight(NB_G, NB_G + 2)
    looped(NB_G + 2, NB - 2, 1)
    straight(NB - 2, NB + 2)


def tile_steps(eng, body):
    first = TILES_G // 2
    comb = SEQ // P
    body(Step(0, 0), None)
    body(Step(0, 1), None)
    with eng.Fori(1, first) as i:
        for p in range(2):
            body(Step(i, p), None)
    for p in range(2):
        body(Step(first, p), None)
    with eng.Fori(0, comb // 2) as i:
        for p in range(4):
            body(Step(2 * i + first + 1 + p // 2, p % 2), (i, p // 2) if p % 2 else None)
    for n in range(2 * (first + 1) + 2 * comb, TILES):
        body(Step(n // 2, n % 2), None)


def moe_block(nc, x, ctx_in, mask, kq, kk, kv, bq, bk, bv, gate_w, Wu, Wv, Wo, out):
    ctx = ExitStack()
    with ctx:
        def sb(name, shape, dt=F32):
            return ctx.enter_context(nc.sbuf_tensor(name, shape, dt))

        def bank(name):
            return ctx.enter_context(nc.psum_tensor(name, [P, 512], F32))

        def sem(name):
            return ctx.enter_context(nc.semaphore(name))

        def pair(name):
            return [sem(f"{name}{i}") for i in range(2)]

        def dram(name, shape, dt=F32):
            return nc.dram_tensor(name, shape, dt, kind="Internal").ap()

        z_dram = dram("z_dram", [TOK, D])
        x1_dram = dram("x1_dram", [TOK, D])
        y_dram = [dram(f"y_dram{g}", [TILES_G * P, D]) for g in range(NBATCH)]
        slot_token = dram("slot_token", [NSLOT, 1], I32)

        wq = sb("wq", [P, 2, DC, D], F32R)
        wuv = sb("wuv", [P, E, 2, DC, 2 * R], F32R)
        wo = sb("wo", [P, E, 2, D], F32R)
        kpT = sb("kpT", [P, 2, DC, NBATCH * KEYS], F32R)
        vp = sb("vp", [P, 2, NBATCH, D], F32R)
        qT = sb("qT", [P, 2, DC, BT], F32R)
        qpT = sb("qpT", [P, 2, DC, BT], F32R)
        lgT = sb("lgT", [P, 2, BT], F32R)
        zgT = [qT[:, h, :, :] for h in range(2)]
        sT = [lgT[:, i, :].rearrange("p (h t) -> p h t", h=2) for i in range(2)]
        xin = sb("xin", [P, 2, TPB, D])
        x1 = sb("x1", [P, TPB, D])
        xn = sb("xn", [P, TPB, D])
        z = sb("z", [P, TPB, D])
        zT = sb("zT", [P, DC, BT])
        stage = sb("stage", [P, 3 * D])
        tq = sb("tq", [P, 2, BT])
        wraw = sb("wraw", [P, 4 * D])
        mraw = sb("mraw", [P, 2, TPB, KEYS])
        tl = sb("tl", [P, BT])
        lg = sb("lg", [P, BT])
        gate_work = sb("gate_work", [P, 2, 2, R])
        sil, s_tok = gate_work[:, 0, :, :], gate_work[:, 1, :, :]
        zeros_i = gate_work[:, :, :, :].rearrange("p a b r -> p (a b r)")[:, 0:NSLOT // P].bitcast(I32)
        wk_raw = z[:, :, :].rearrange("p t d -> p (t d)")
        zg = [xn[:, i, :] for i in range(2)]
        ysb = [zT[:, 2 * i:2 * i + 2, :].rearrange("p c t -> p (c t)") for i in range(2)]
        plan_big = [wraw[:, (2 + i) * D:(2 + i) * D + 2 * TILES_B * E].rearrange("p (n e) -> p n e", e=E) for i in range(2)]
        y1g = [xin[:, 0, i, :] for i in range(2)]
        y2g = [xin[:, 1, i, :] for i in range(2)]
        xg = [x1[:, i, :] for i in range(2)]
        ctx_raw = zT[:, :, :].rearrange("p c t -> p (c t)").rearrange("p (b d) -> p b d", b=NBATCH)
        ctxT = sb("ctxT", [P, DC, NBATCH * KEYS])
        ident = sb("ident", [P, P])
        before = sb("before", [P, P], BF16)
        ones = sb("ones", [P, P], BF16)
        ones_row = sb("ones_row", [1, P])
        gw = sb("gw", [P, DC, E])
        bq_sb = sb("bq_sb", [P, DC])
        bk_sb = sb("bk_sb", [P, DC])
        bv_sb = sb("bv_sb", [1, D])
        st1 = sb("st1", [P, TPB, 6])
        mv1 = sb("mv1", [P, TPB, 2])
        rstd1 = sb("rstd1", [P, TPB])
        st2 = sb("st2", [P, TPB, 6])
        mv2 = sb("mv2", [P, TPB, 2])
        rstd2 = sb("rstd2", [P, TPB])
        nmr2 = sb("nmr2", [P, TPB])
        ve1 = sb("ve1", [P, TPB])
        ve2 = sb("ve2", [P, TPB])
        minus_half = sb("minus_half", [P, TPB])
        logT = sb("logT", [E, BT])
        logit = sb("logit", [P, TPB, E])
        top_v = sb("top_v", [P, TPB, 8])
        top_i = sb("top_i", [P, TPB, 8], U32)
        top_f = sb("top_f", [P, TPB, 2])
        iota_i = sb("iota_i", [P, TPB, 2, E], I32)
        iota_f = sb("iota_f", [P, TPB, 2, E])
        onehot = sb("onehot", [P, TPB, 2, E])
        chosen = sb("chosen", [P, TPB, E], BF16)
        base_i = sb("base_i", [P, E], I32)
        base0 = sb("base0", [P, E])
        base = sb("base", [P, E])
        pos = sb("pos", [P, TPB, E])
        posk = sb("posk", [P, TPB, 2, E])
        destf = sb("destf", [P, TPB, 2])
        dest = sb("dest", [P, 2, TPB, 2], U32)
        dest_all = sb("dest_all", [P, NTILE, 2])
        expert_all = sb("expert_all", [P, NTILE, 2])
        row_all = sb("row_all", [P, NTILE, 2], U32)
        before_e = sb("before_e", [P, E])
        shift_e = sb("shift_e", [P, E])
        shift_t = sb("shift_t", [P, TILES_B * 2])
        cidx = sb("cidx", [P, 2, 2], U32)
        gap_all = sb("gap_all", [P, NTILE])
        e_all = sb("e_all", [P, NTILE])
        den_all = sb("den_all", [P, NTILE])
        w_all = sb("w_all", [P, 2, NTILE])
        tokid = sb("tokid", [P, 2, TPB], I32)
        upto_e = sb("upto_e", [P, E, E])
        tile_i = sb("tile_i", [1, TILES_G, E], I32)
        tile_s = sb("tile_s", [1, TILES_G, E])
        cnt = sb("cnt", [P, E])
        cnt_i = sb("cnt_i", [P, E], I32)
        len_i = sb("len_i", [P, E], I32)
        length = sb("length", [P, E])
        cum = sb("cum", [P, E])
        te = TILES_G * E
        past, pastc = (wraw[0:1, i * te:(i + 1) * te].rearrange("p (t e) -> p t e", e=E) for i in range(2))
        exp_f, prev_f, off_f, row_f, over_f, row2_f = (
            wraw[0:1, 2 * te + i * TILES_G:2 * te + (i + 1) * TILES_G] for i in range(6))
        lens = wraw[:, 2 * te + 6 * TILES_G:2 * te + 6 * TILES_G + E * E].rearrange("p (a b) -> p a b", b=E)
        sched_row = sb("sched_row", [1, TILES], I32)
        sched_exp = sb("sched_exp", [1, TILES], I32)
        idx = sb("idx", [P, 2], I32)

        psT = [bank(f"psT{i}") for i in range(2)]
        psQ = [bank(f"psQ{i}") for i in range(2)]
        psS = bank("psS")
        psO = bank("psO")
        psZ = bank("psZ")
        psG = bank("psG")
        ps_out = [psO, psS]
        ps_mask = psS[:, BT:2 * BT]
        ps_log = psG[0:E, 0:BT]
        ps_logit = psG[:, BT:BT + TPB * E].rearrange("p (t e) -> p t e", e=E)
        ps_pos = psG[:, BT + 32:BT + 32 + TPB * E].rearrange("p (t e) -> p t e", e=E)
        ps_tot = psG[:, BT + 64:BT + 64 + E]
        psST = [psZ, psG]

        const_ready = sem("const_ready")
        pool_step = sem("pool_step")
        conv_ready = sem("conv_ready")
        w_loaded = {k: sem(f"load_{k}") for k in ("ctx", "wk0", "wk1", "wq", "wv", "small", "table")}
        ctxT_ready = sem("ctxT_ready")
        ctx_turned = sem("ctx_turned")
        wq_hi = sem("wq_hi")
        wq_ready = sem("wq_ready")
        k_done = sem("k_done")
        k_relu = sem("k_relu")
        k_hi = sem("k_hi")
        k_lo = sem("k_lo")
        v_done = sem("v_done")
        v_relu = sem("v_relu")
        v_hi = sem("v_hi")
        v_lo = sem("v_lo")
        x_loaded = pair("x_loaded")
        m_loaded = pair("m_loaded")
        stats1 = sem("stats1")
        rstd1_ready = sem("rstd1_ready")
        xn_ready = sem("xn_ready")
        xn_turned = sem("xn_turned")
        qT_hi = sem("qT_hi")
        qT_lo = sem("qT_lo")
        q_done = sem("q_done")
        qp_relu = sem("qp_relu")
        qp_hi = sem("qp_hi")
        qp_lo = sem("qp_lo")
        s_done = sem("s_done")
        s_relu = sem("s_relu")
        lg_step = sem("lg_step")
        o_done = sem("o_done")
        x1_ready = sem("x1_ready")
        stats2 = sem("stats2")
        rstd2_ready = sem("rstd2_ready")
        nmr2_ready = sem("nmr2_ready")
        z_ready = sem("z_ready")
        x1_stored = pair("x1_stored")
        z_stored = pair("z_stored")
        z_turned = sem("z_turned")
        zT_ready = sem("zT_ready")
        gate_done = sem("gate_done")
        logT_ready = sem("logT_ready")
        logit_turned = sem("logit_turned")
        route = sem("route")
        rank_done = sem("rank_done")
        place = sem("place")
        token_scattered = pair("token_scattered") 
        tokid_moved = sem("tokid_moved")
        stage_loaded = sem("stage_loaded")
        stage_hi = sem("stage_hi")
        stage_lo = sem("stage_lo")
        plan_aux = sem("plan_aux")
        regroup = sem("regroup")
        plan = sem("plan")
        gap_exp = sem("gap_exp")
        weight = sem("weight")
        idx_loaded = pair("idx_loaded")
        z_gathered = pair("z_gathered")
        g_turned = sem("g_turned")
        gT_hi = sem("gT_hi")
        gT_lo = sem("gT_lo")
        uv_done = sem("uv_done")
        silu_done = sem("silu_done")
        s_ready = sem("s_ready")
        s_turned = sem("s_turned")
        sT_hi = sem("sT_hi")
        sT_lo = sem("sT_lo")
        y_done = sem("y_done")
        y_ready = sem("y_ready")
        y_stored = pair("y_stored")
        cidx_ready = sem("cidx_ready")
        y1_gathered = pair("y1_gathered")
        y2_gathered = pair("y2_gathered")
        xg_loaded = pair("xg_loaded")
        comb1 = sem("comb1")
        comb2 = sem("comb2")
        out_stored = pair("out_stored")
        held = {e: sem(f"held_{e}") for e in ("pool", "dve", "act", "sp", "pe")}

        ROUTE_STEPS, PLACE_STEPS, PLAN_STEPS, SCHED_STEPS = 10, 6, 20, 14

        x_blk = x.rearrange("g (b t p) d -> (g b) p t d", t=TPB, p=P)
        x1_blk = x1_dram.rearrange("(b t p) d -> b p t d", t=TPB, p=P)
        z_blk = z_dram.rearrange("(b t p) d -> b p t d", t=TPB, p=P)
        m_blk = mask.rearrange("o (b t p) k -> (o b) p t k", t=TPB, p=P)
        x1_tile = x1_dram.rearrange("(n p) d -> n p d", p=P)
        out_tile = out.rearrange("g (n p) d -> (g n) p d", p=P)
        wu_v = Wu.rearrange("e (c p) r -> e p c r", p=P)
        wv_v = Wv.rearrange("e (c p) r -> e p c r", p=P)
        w_v = {k: w.rearrange("a b (c p) n -> p (a b c) n", p=P) for k, w in (("q", kq), ("k", kk), ("v", kv))}

        def pass_held(eng, name):
            eng.sem_inc(held[name], 1)

        block = ctx.enter_context(nc.Block())

        @block.sync
        def _(sp):
            sp.dma_start(xin[:, 0, :, :], x_blk[0]).then_inc(x_loaded[0], 16)
            sp.dma_start(ctx_raw, ctx_in.rearrange("b k d -> k b d")).then_inc(w_loaded["ctx"], 16)
            sp.dma_start(wk_raw.rearrange("p (c n) -> p c n", c=2), w_v["k"][:, 0:2, :]).then_inc(w_loaded["wk0"], 16)
            sp.dma_start(x1[:, :, :], w_v["k"][:, 2:4, :]).then_inc(w_loaded["wk1"], 16)
            with nc.allow_non_contiguous_dma("small biases"):
                sp.dma_start(bq_sb[:, :], bq.rearrange("(m p) -> p m", p=P)).then_inc(w_loaded["small"], 16)
                sp.dma_start(bk_sb[:, :], bk.rearrange("(m p) -> p m", p=P)).then_inc(w_loaded["small"], 16)
                sp.dma_start(gw[:, :, :], gate_w.rearrange("(c p) e -> p c e", p=P)).then_inc(w_loaded["small"], 16)
            sp.dma_start(bv_sb[:, :], bv.rearrange("(a n) -> a n", a=1)).then_inc(w_loaded["small"], 16)
            sp.dma_start(wraw[:, :].rearrange("p (c n) -> p c n", c=DC), w_v["q"]).then_inc(w_loaded["wq"], 16)
            sp.dma_start(stage[:, 0:3 * D].rearrange("p (c n) -> p c n", c=3), w_v["v"][:, 0:3, :]).then_inc(w_loaded["wv"], 16)
            sp.dma_start(tq[:, :, :].rearrange("p a t -> p (a t)"), w_v["v"][:, 3, :]).then_inc(w_loaded["wv"], 16)
            sp.wait_ge(const_ready, 1)
            sp.dma_start(slot_token.rearrange("(p n) o -> p (n o)", p=P), zeros_i).then_inc(w_loaded["table"], 16)

            def load_experts(e):
                uv = stage[:, 0:DC * 2 * R].rearrange("p (c h r) -> p c h r", c=DC, h=2)
                sp.dma_start(uv[:, :, 0, :], wu_v[e]).then_inc(stage_loaded, 16)
                sp.dma_start(uv[:, :, 1, :], wv_v[e]).then_inc(stage_loaded, 16)
                sp.dma_start(stage[:, 2 * D:3 * D], Wo[e]).then_inc(stage_loaded, 16)

            def body(b, batch):
                nxt, prv = b + 1, b + (-1)
                if nxt.within(NB) and not (isinstance(nxt.j, int) and nxt.n == 0):
                    ge(sp, x1_ready, 2 * (nxt.n - 2) + 2)
                    sp.dma_start(xin[:, nxt.p, :, :], x_blk[nxt.n]).then_inc(x_loaded[nxt.p], 16)
                if b.within(NB):
                    ge(sp, s_done, b.n - 1)
                    sp.dma_start(mraw[:, b.p, :, :], m_blk[b.n - batch * NB_G]).then_inc(m_loaded[b.p], 16)
                if prv.within(NB):
                    ge(sp, x1_ready, 2 * prv.n + 2)
                    sp.dma_start(x1_blk[prv.n], x1[:, :, :]).then_inc(x1_stored[prv.p], 16)
                    ge(sp, z_ready, 2 * prv.n + 2)
                    sp.dma_start(z_blk[prv.n], z[:, :, :]).then_inc(z_stored[prv.p], 16)
                if isinstance(b.j, int) and b.n == -1:
                    sp.wait_ge(v_done, 2)
                    load_experts(0)
                elif b.p == 1 and b.within(NB - 2):
                    ge(sp, stage_hi, b.n + 1)
                    ge(sp, stage_lo, b.n + 1)
                    load_experts(b.j + 1)

            block_steps(sp, body)

            def load_idx(t):
                if not t.within(TILES):
                    return
                ge(sp, z_gathered[t.p], 16 * t.j)
                pass_held(sp, "sp")
                row = sp.value_load(sched_row[0:1, bass.ds(t.n, 1)], min_val=0, max_val=DUMMY)
                sp.dma_start(idx[:, t.p:t.p + 1], slot_token[bass.ds(row, P), :]).then_inc(idx_loaded[t.p], 16)

            for q in range(2):
                sp.wait_ge(token_scattered[q], 16 * 4 * NB_G // 2)
            sp.wait_ge(plan, SCHED_STEPS)
            load_idx(Step(0, 0))
            load_idx(Step(0, 1))

            def store_out(n, q, k):
                sp.wait_ge(comb2, n + 2)
                sp.dma_start(out_tile[n], xg[q]).then_inc(out_stored[q], 16)

            def load_x1(n, q, k):
                ge(sp, out_stored[q], 16 * k)
                sp.dma_start(xg[q], x1_tile[n]).then_inc(xg_loaded[q], 16)

            y_tile = [y.rearrange("(n p) d -> n p d", p=P) for y in y_dram]

            def tile_body(t, comb, g):
                load_idx(t + 2)
                if comb is not None:
                    i, q = comb
                    load_x1(2 * i + q, q, i)
                sp.wait_ge(y_ready, t.n + 1)
                sp.dma_start(y_tile[g][t.n - g * TILES_G], ysb[t.p]).then_inc(y_stored[t.p], 16)
                if comb is not None:
                    store_out(2 * i + q, q, i)

            first = TILES_G // 2
            with sp.Fori(0, first - 1) as i:
                for p in range(2):
                    tile_body(Step(i, p), None, 0)
            for q in range(2):
                sp.wait_ge(token_scattered[q], 16 * 4 * NB // 2)
            sp.wait_ge(plan, PLAN_STEPS + SCHED_STEPS)
            for n in range(2 * first - 2, 2 * first + 2):
                tile_body(Step(n // 2, n % 2), None, n // TILES_G)
            with sp.Fori(0, SEQ // P // 2) as i:
                for p in range(4):
                    tile_body(Step(2 * i + first + 1 + p // 2, p % 2), (i, p // 2) if p % 2 else None, 1)
            for n in range(2 * (first + 1) + 2 * (SEQ // P), TILES):
                tile_body(Step(n // 2, n % 2), None, n // TILES_G)
            half = SEQ // P // 2
            with sp.Fori(half, 2 * half) as i:
                for q in range(2):
                    load_x1(2 * i + q, q, i)
                for q in range(2):
                    store_out(2 * i + q, q, i)
            for q in range(2):
                sp.wait_ge(out_stored[q], 16 * NTILE // 2)
                sp.wait_ge(y_stored[q], 16 * TILES // 2)
                sp.wait_ge(x1_stored[q], 16 * NB // 2)
                sp.wait_ge(z_stored[q], 16 * NB // 2)

        @block.gpsimd
        def _(pool):
            nc.gpsimd.memset(zeros_i, 0).then_inc(const_ready, 1)
            nc.gpsimd.memset(ident[:, :], 0.0).then_inc(pool_step, 1)
            nc.gpsimd.memset(before[:, :], 1.0).then_inc(pool_step, 1)
            nc.gpsimd.memset(upto_e[:, :, :], 1.0).then_inc(pool_step, 1)
            pool.wait_ge(pool_step, 3)
            nc.gpsimd.affine_select(out=ident[:, :], in_=ident[:, :], compare_op=ALU.not_equal, fill=1.0,
                                    base=0, pattern=[[-1, P]], channel_multiplier=1).then_inc(const_ready, 1)
            nc.gpsimd.affine_select(out=before[:, :], in_=before[:, :], compare_op=ALU.is_gt, fill=0.0,
                                    base=0, pattern=[[1, P]], channel_multiplier=-1).then_inc(const_ready, 1)
            nc.gpsimd.affine_select(out=upto_e[:, :, :], in_=upto_e[:, :, :], compare_op=ALU.is_ge, fill=0.0,
                                    base=0, pattern=[[1, E], [-1, E]], channel_multiplier=0).then_inc(const_ready, 1)
            nc.gpsimd.memset(ones[:, :], 1.0).then_inc(const_ready, 1)
            nc.gpsimd.memset(ones_row[:, :], 1.0).then_inc(const_ready, 1)
            nc.gpsimd.memset(minus_half[:, :], -0.5).then_inc(const_ready, 1)
            nc.gpsimd.iota(iota_i[:, :, :, :], [[0, TPB], [0, 2], [1, E]], base=0, channel_multiplier=0).then_inc(const_ready, 1)
            nc.gpsimd.iota(base_i[:, :], [[CAP, E]], base=0, channel_multiplier=0).then_inc(const_ready, 1)
            nc.gpsimd.iota(tile_i[:, :, :], [[P, TILES_G], [0, E]], base=0, channel_multiplier=0).then_inc(const_ready, 1)
            for q in range(2):
                nc.gpsimd.iota(tokid[:, q, :], [[P, TPB]], base=q * BT, channel_multiplier=1).then_inc(tokid_moved, 1)

            def body(b, batch):
                prv, nxt, old = b + (-1), b + 1, b + (-2)
                if prv.within(NB):
                    ge(pool, stats2, 5 * prv.n + 5)
                    ge(pool, z_ready, 2 * prv.n)
                    nc.gpsimd.tensor_tensor(rstd2[:, :], ve2[:, :], minus_half[:, :], ALU.pow).then_inc(rstd2_ready, 1)
                if nxt.within(NB):
                    ge(pool, stats1, 5 * nxt.n + 5)
                    ge(pool, xn_ready, 2 * nxt.n)
                    nc.gpsimd.tensor_tensor(rstd1[:, :], ve1[:, :], minus_half[:, :], ALU.pow).then_inc(rstd1_ready, 1)
                if old.within(NB):
                    if isinstance(old.j, int) and old.n == 0:
                        pool.wait_ge(w_loaded["table"], 16)
                    ge(pool, place, PLACE_STEPS * old.n + 5)
                    ge(pool, tokid_moved, old.n + 1)
                    pass_held(pool, "pool")
                    for t in range(TPB):
                        for k in range(2):
                            pool.indirect_dma_start(
                                out=slot_token, out_offset=bass.IndirectOffsetOnAxis(ap=dest[:, old.p, t, k:k + 1], axis=0),
                                in_=tokid[:, old.p, t:t + 1], in_offset=None).then_inc(token_scattered[old.p], 16)
                if (b + (-3)).within(NB):
                    o = b + (-3)
                    ge(pool, token_scattered[o.p], 16 * 4 * (o.j + 1))
                    pass_held(pool, "pool")
                    nc.gpsimd.tensor_scalar(tokid[:, o.p, :], tokid[:, o.p, :], 2 * BT, None, ALU.add).then_inc(tokid_moved, 1)

            block_steps(pool, body)

            def gather(t):
                if not t.within(TILES):
                    return
                ge(pool, idx_loaded[t.p], 16 * (t.j + 1))
                ge(pool, g_turned, t.n - 1)
                pass_held(pool, "pool")
                pool.indirect_dma_start(out=zg[t.p], out_offset=None, in_=z_dram,
                                        in_offset=bass.IndirectOffsetOnAxis(ap=idx[:, t.p:t.p + 1], axis=0)
                                        ).then_inc(z_gathered[t.p], 16)

            def gather_y(n, q, k, g):
                ge(pool, cidx_ready, n + 1)
                ge(pool, comb2, n)
                pass_held(pool, "pool")
                for kk_, (buf, s) in enumerate(((y1g[q], y1_gathered[q]), (y2g[q], y2_gathered[q]))):
                    pool.indirect_dma_start(out=buf, out_offset=None, in_=y_dram[g],
                                            in_offset=bass.IndirectOffsetOnAxis(ap=cidx[:, q, kk_:kk_ + 1], axis=0)
                                            ).then_inc(s, 16)

            for q in range(2):
                pool.wait_ge(z_stored[q], 16 * NB // 2)
            pool.wait_ge(xn_turned, 2 * NB)
            gather(Step(0, 0))
            gather(Step(0, 1))

            def tile_body(t, comb):
                gather(t + 2)
                if comb is not None:
                    i, q = comb
                    gather_y(2 * i + q, q, i, 0)

            first = TILES_G // 2
            with pool.Fori(0, first) as i:
                for p in range(2):
                    tile_body(Step(i, p), None)
            for p in range(2):
                tile_body(Step(first, p), None)
            pool.wait_ge(y_stored[0], 16 * (first + 1))
            pool.wait_ge(y_stored[1], 16 * first)
            with pool.Fori(0, SEQ // P // 2) as i:
                for p in range(4):
                    tile_body(Step(2 * i + first + 1 + p // 2, p % 2), (i, p // 2) if p % 2 else None)
            for n in range(2 * (first + 1) + 2 * (SEQ // P), TILES):
                tile_body(Step(n // 2, n % 2), None)
            for q in range(2):
                pool.wait_ge(y_stored[q], 16 * TILES // 2)
            half = SEQ // P // 2
            with pool.Fori(half, 2 * half) as i:
                for q in range(2):
                    gather_y(2 * i + q, q, i, 1)

        @block.scalar
        def _(act):
            def copy(o, i, s):
                nc.scalar.activation(o, i, ACT.Copy).then_inc(s, 1)

            for g in range(NBATCH):
                act.wait_ge(ctx_turned, g + 1)
                copy(ctxT[:, :, g * KEYS:(g + 1) * KEYS], psT[g][:, :].rearrange("p (c k) -> p c k", c=DC), ctxT_ready)
            act.wait_ge(w_loaded["wq"], 16)
            for c in range(DC):
                copy(wq[:, HI, c, :], wraw[:, c * D:(c + 1) * D], wq_hi)
            act.wait_ge(w_loaded["small"], 64)
            for m in range(DC):
                act.wait_ge(k_done, m + 1)
                dst = lg if m % 2 == 0 else tl
                ge(act, k_lo, m - 1)
                nc.scalar.activation(dst[:, :], psQ[m % 2][:, 0:BT], ACT.Relu,
                                     bias=bk_sb[:, m:m + 1]).then_inc(k_relu, 1)
                act.wait_ge(k_relu, m + 1)
                copy(kpT[:, HI, m, :], dst[:, :], k_hi)
            for g in range(NBATCH):
                act.wait_ge(v_done, g + 1)
                act.wait_ge(k_done, DC)
                nc.scalar.activation(z[:, g, :], ps_out[g][:, :], ACT.Relu).then_inc(v_relu, 1)
                act.wait_ge(v_relu, g + 1)
                copy(vp[:, HI, g, :], z[:, g, :], v_hi)

            def body(b, batch):
                nxt, prv = b + 1, b + (-1)

                def queries(m):
                    ge(act, q_done, 4 * b.n + m + 1)
                    ge(act, qp_lo, 4 * b.n + m - 1)
                    nc.scalar.activation(tq[:, m % 2, :], psQ[m % 2][:, 0:BT], ACT.Relu,
                                         bias=bq_sb[:, m:m + 1]).then_inc(qp_relu, 1)
                    ge(act, qp_relu, 4 * b.n + m + 1)
                    ge(act, s_done, b.n)
                    copy(qpT[:, HI, m, :], tq[:, m % 2, :], qp_hi)

                def turned_z(t):
                    ge(act, z_turned, 2 * prv.n + t + 1)
                    ge(act, gate_done, prv.n)
                    copy(zT[:, :, t * P:(t + 1) * P], psZ[:, :].rearrange("p (c k) -> p c k", c=DC), zT_ready)

                if b.within(NB):
                    queries(0)
                    queries(1)
                if prv.within(NB):
                    for t in range(TPB):
                        if t == 0:
                            ge(act, nmr2_ready, prv.n + 1)
                            ge(act, z_turned, 2 * prv.n)
                            if (prv + (-1)).within(NB):
                                last = prv + (-1)
                                ge(act, z_stored[last.p], 16 * (last.j + 1))
                        nc.scalar.activation(z[:, t, :], x1[:, t, :], ACT.Identity, bias=nmr2[:, t:t + 1],
                                             scale=rstd2[:, t:t + 1]).then_inc(z_ready, 1)
                if b.within(NB):
                    queries(2)
                    queries(3)
                if prv.within(NB):
                    turned_z(0)
                if b.within(NB):
                    ge(act, s_done, b.n + 1)
                    ge(act, lg_step, 3 * b.n)
                    nc.scalar.activation(tl[:, :], psS[:, 0:BT], ACT.Relu, scale=SCALE).then_inc(s_relu, 1)
                if prv.within(NB):
                    turned_z(1)
                if nxt.within(NB):
                    for t in range(TPB):
                        ge(act, xn_turned, 2 * nxt.n + t + 1)
                        ge(act, q_done, 4 * nxt.n)
                        copy(qT[:, HI, :, t * P:(t + 1) * P], psT[t][:, :].rearrange("p (c k) -> p c k", c=DC), qT_hi)
                if b.within(NB):
                    ge(act, stage_loaded, 48 * (b.j + 1))
                    pass_held(act, "act")
                    if b.p == 0:
                        copy(wuv[:, b.j, HI, :, :].rearrange("p c n -> p (c n)") if isinstance(b.j, int)
                             else wuv[:, bass.ds(b.j, 1), HI, :, :].rearrange("p e c n -> p (e c n)"), stage[:, 0:2 * D], stage_hi)
                    else:
                        copy(wo[:, b.j, HI, :] if isinstance(b.j, int)
                             else wo[:, bass.ds(b.j, 1), HI, :].rearrange("p e n -> p (e n)"), stage[:, 2 * D:3 * D], stage_hi)
                if prv.within(NB):
                    ge(act, gate_done, prv.n + 1)
                    ge(act, logit_turned, prv.n)
                    copy(logT[:, :], ps_log, logT_ready)

            block_steps(act, body)
            act.wait_ge(route, ROUTE_STEPS * NB)
            nc.scalar.activation(e_all[:, :], gap_all[:, :], ACT.Exp).then_inc(gap_exp, 1)

            def turned_g(t):
                ge(act, g_turned, t.n + 1)
                ge(act, uv_done, t.n - 1)
                copy(zgT[t.p][:, :, 0:P], psT[t.p][:, :].rearrange("p (c k) -> p c k", c=DC), gT_hi)

            def turned_s(t):
                ge(act, s_turned, t.n + 1)
                ge(act, y_done, t.n - 1)
                copy(sT[t.p][:, HI, :], psST[t.p][:, 0:P], sT_hi)

            def take_y(t):
                ge(act, y_done, t.n + 1)
                if not isinstance(t.j, int) or t.n >= 2:
                    ge(act, y_stored[t.p], 16 * t.j)
                copy(ysb[t.p], ps_out[t.p][:, :], y_ready)

            turned_g(Step(0, 0))

            def tile_body(t, comb, last=False):
                ge(act, uv_done, t.n + 1)
                ge(act, s_ready, t.n - 1)
                nc.scalar.activation(sil[:, t.p, :], psQ[t.p][:, 0:R], ACT.Silu).then_inc(silu_done, 1)
                if (t + 1).within(TILES):
                    turned_g(t + 1)
                if (t + (-1)).within(TILES):
                    take_y(t + (-1))
                turned_s(t)

            tile_body(Step(0, 0), None)
            tile_body(Step(0, 1), None)
            with act.Fori(1, TILES // 2 - 1) as i:
                for p in range(2):
                    tile_body(Step(i, p), None)
            tile_body(Step(TILES // 2 - 1, 0), None)
            tile_body(Step(TILES // 2 - 1, 1), None)
            take_y(Step(TILES // 2 - 1, 1))

        @block.vector
        def _(dve):
            def sub(o, a, b, s):
                nc.vector.tensor_tensor(o, a, b, ALU.subtract).then_inc(s, 1)

            def stats(src, st, mv, t, s, n):
                nc.vector.bn_stats(st[:, t, :], src).then_inc(s, 1)
                ge(dve, s, n)
                pass_held(dve, "dve")
                nc.vector.bn_aggr(mv[:, t, :], st[:, t, :]).then_inc(s, 1)

            def variance(mv, ve, s, n):
                ge(dve, s, n)
                nc.vector.tensor_scalar(ve[:, :], mv[:, :, 1], EPS, None, ALU.add).then_inc(s, 1)

            dve.sem_inc(comb2, 1)
            dve.wait_ge(const_ready, 10)
            nc.vector.tensor_copy(iota_f[:, :, :, :], iota_i[:, :, :, :]).then_inc(conv_ready, 1)
            nc.vector.tensor_copy(base0[:, :], base_i[:, :]).then_inc(conv_ready, 1)
            nc.vector.tensor_copy(base[:, :], base_i[:, :]).then_inc(conv_ready, 1)
            nc.vector.tensor_copy(tile_s[:, :, :], tile_i[:, :, :]).then_inc(conv_ready, 1)
            dve.wait_ge(conv_ready, 4)

            def setup_splits():
                for c in range(DC):
                    dve.wait_ge(wq_hi, c + 1)
                    sub(wq[:, LO, c, :], wraw[:, c * D:(c + 1) * D], wq[:, HI, c, :], wq_ready)
                for m in range(DC):
                    dve.wait_ge(k_hi, m + 1)
                    sub(kpT[:, LO, m, :], (lg if m % 2 == 0 else tl)[:, :], kpT[:, HI, m, :], k_lo)
                for g in range(NBATCH):
                    dve.wait_ge(v_hi, g + 1)
                    sub(vp[:, LO, g, :], z[:, g, :], vp[:, HI, g, :], v_lo)

            def make_plan(g):
                n0 = PLAN_STEPS * g
                cols = slice(g * TILES_G, (g + 1) * TILES_G)
                step = [n0]

                def link(ins):
                    ins.then_inc(plan, 1)
                    step[0] += 1
                    dve.wait_ge(plan, step[0])

                start = float(g * E * CAP)
                link(nc.vector.scalar_tensor_tensor(cnt[:, :], base[:, :], P - 1 - start, base0[:, :], ALU.add, ALU.subtract))
                link(nc.vector.tensor_copy(cnt_i[:, :], cnt[:, :]))
                link(nc.vector.tensor_scalar(len_i[:, :], cnt_i[:, :], LOG_P, LOG_P,
                                             ALU.logical_shift_right, ALU.logical_shift_left))
                link(nc.vector.tensor_copy(length[:, :], len_i[:, :]))
                link(nc.vector.tensor_tensor(lens, upto_e[:, :, :],
                                             length[:, :].unsqueeze(1).broadcast_to([P, E, E]), ALU.mult))
                link(nc.vector.tensor_reduce(cum[:, :], lens, AX.X, ALU.add))
                cum_b = cum[0:1, :].unsqueeze(1).broadcast_to([1, TILES_G, E])
                link(nc.vector.tensor_tensor(past, cum_b, tile_s[:, :, :], ALU.is_le))
                link(nc.vector.tensor_tensor(pastc, past, cum_b, ALU.mult))
                link(nc.vector.tensor_reduce(exp_f, past, AX.X, ALU.add))
                link(nc.vector.tensor_reduce(prev_f, pastc, AX.X, ALU.max))
                link(nc.vector.tensor_tensor(off_f, tile_s[:, :, 0], prev_f, ALU.subtract))
                link(nc.vector.scalar_tensor_tensor(row_f, exp_f, float(CAP), off_f, ALU.mult, ALU.add))
                nc.vector.tensor_scalar(over_f, exp_f, float(E), float(DUMMY), ALU.is_ge, ALU.mult).then_inc(plan_aux, 1)
                dve.wait_ge(plan_aux, 4 * g + 1)
                nc.vector.scalar_tensor_tensor(row2_f, row_f, start, over_f, ALU.add, ALU.add).then_inc(plan_aux, 1)
                dve.wait_ge(plan_aux, 4 * g + 2)
                nc.vector.tensor_scalar(row_f, row2_f, float(DUMMY), None, ALU.min).then_inc(plan_aux, 1)
                nc.vector.tensor_scalar(off_f, exp_f, float(E - 1), None, ALU.min).then_inc(plan_aux, 1)
                dve.wait_ge(plan_aux, 4 * g + 4)
                link(nc.vector.tensor_copy(sched_row[:, cols], row_f))
                link(nc.vector.tensor_copy(sched_exp[:, cols], off_f))
                ex = expert_all[:, g * TILES_B:(g + 1) * TILES_B, :].rearrange("p n k -> p (n k)")
                sl = dest_all[:, g * TILES_B:(g + 1) * TILES_B, :].rearrange("p n k -> p (n k)")
                rw = row_all[:, g * TILES_B:(g + 1) * TILES_B, :].rearrange("p n k -> p (n k)")
                wide = [P, 2 * TILES_B, E]
                link(nc.vector.tensor_tensor(before_e[:, :], cum[:, :], length[:, :], ALU.subtract))
                link(nc.vector.scalar_tensor_tensor(shift_e[:, :], before_e[:, :], -start, base0[:, :], ALU.add, ALU.subtract))
                link(nc.vector.tensor_tensor(plan_big[0], iota_f[:, 0, 0, :].unsqueeze(1).broadcast_to(wide),
                                             ex.unsqueeze(2).broadcast_to(wide), ALU.is_equal))
                link(nc.vector.tensor_tensor(plan_big[1], plan_big[0], shift_e[:, :].unsqueeze(1).broadcast_to(wide), ALU.mult))
                link(nc.vector.tensor_reduce(shift_t[:, :], plan_big[1], AX.X, ALU.add))
                link(nc.vector.tensor_tensor(rw, sl, shift_t[:, :], ALU.add))

            def add_attention(b):
                for t in range(TPB):
                    ge(dve, o_done, 2 * b.n + t + 1)
                    if t == 0:
                        ge(dve, z_ready, 2 * b.n)
                        last = b + (-1)
                        if last.within(NB):
                            ge(dve, x1_stored[last.p], 16 * (last.j + 1))
                    nc.vector.scalar_tensor_tensor(x1[:, t, :], ps_out[t][:, :], 0.0, xin[:, b.p, t, :],
                                                   ALU.max, ALU.add).then_inc(x1_ready, 1)
                ge(dve, rstd2_ready, b.n)
                for t in range(TPB):
                    ge(dve, x1_ready, 2 * b.n + t + 1)
                    stats(x1[:, t, :], st2, mv2, t, stats2, 5 * b.n + 2 * t + 1)
                variance(mv2, ve2, stats2, 5 * b.n + 4)

            def shift2(b):
                ge(dve, rstd2_ready, b.n + 1)
                nc.vector.scalar_tensor_tensor(nmr2[:, :], mv2[:, :, 0], -1.0, rstd2[:, :],
                                               ALU.mult, ALU.mult).then_inc(nmr2_ready, 1)

            def norm1(b):
                ge(dve, x_loaded[b.p], 16 * (b.j + 1))
                ge(dve, rstd1_ready, b.n)
                for t in range(TPB):
                    stats(xin[:, b.p, t, :], st1, mv1, t, stats1, 5 * b.n + 2 * t + 1)
                variance(mv1, ve1, stats1, 5 * b.n + 4)

            def norm1_apply(b):
                ge(dve, rstd1_ready, b.n + 1)
                ge(dve, xn_turned, 2 * b.n)
                for t in range(TPB):
                    nc.vector.tensor_scalar(xn[:, t, :], xin[:, b.p, t, :], mv1[:, t, 0:1], rstd1[:, t:t + 1],
                                            ALU.subtract, ALU.mult).then_inc(xn_ready, 1)

            def choose(b):
                n = ROUTE_STEPS * b.n
                ge(dve, logit_turned, b.n + 1)
                nc.vector.tensor_copy(logit[:, :, :], ps_logit).then_inc(route, 1)
                ge(dve, route, n + 1)
                pass_held(dve, "dve")
                for t in range(TPB):
                    nc.vector.max(top_v[:, t, :], logit[:, t, :]).then_inc(route, 1)
                ge(dve, route, n + 3)
                pass_held(dve, "dve")
                for t in range(TPB):
                    nc.vector.max_index(top_i[:, t, :], top_v[:, t, :], logit[:, t, :]).then_inc(route, 1)
                gap = (gap_all[:, 2 * b.n:2 * b.n + 2] if isinstance(b.j, int) else gap_all[:, bass.ds(b.n * 2, 2)])
                nc.vector.tensor_tensor(gap, top_v[:, :, 1], top_v[:, :, 0], ALU.subtract).then_inc(route, 1)
                ge(dve, route, n + 5)
                nc.vector.tensor_copy(top_f[:, :, :], top_i[:, :, 0:2]).then_inc(route, 1)
                ge(dve, route, n + 7)
                nc.vector.tensor_tensor(onehot[:, :, :, :], iota_f[:, :, :, :],
                                        top_f[:, :, :].unsqueeze(3).broadcast_to([P, TPB, 2, E]), ALU.is_equal).then_inc(route, 1)
                ge(dve, route, n + 8)
                ge(dve, rank_done, b.n)
                nc.vector.tensor_tensor(chosen[:, :, :], onehot[:, :, 0, :], onehot[:, :, 1, :], ALU.add).then_inc(route, 1)
                ea = (expert_all[:, 2 * b.n:2 * b.n + 2, :] if isinstance(b.j, int)
                      else expert_all[:, bass.ds(b.n * 2, 2), :])
                pass_held(dve, "dve")
                nc.vector.tensor_copy(ea, top_f[:, :, :]).then_inc(route, 1)

            def place_tokens(b):
                n = PLACE_STEPS * b.n
                ge(dve, rank_done, b.n + 1)
                nc.vector.tensor_tensor(pos[:, :, :], ps_pos, base[:, :].unsqueeze(1).broadcast_to([P, TPB, E]),
                                        ALU.add).then_inc(place, 1)
                ge(dve, place, n + 1)
                nc.vector.tensor_tensor(posk[:, :, :, :], onehot[:, :, :, :],
                                        pos[:, :, :].unsqueeze(2).broadcast_to([P, TPB, 2, E]), ALU.mult).then_inc(place, 1)
                nc.vector.tensor_tensor(base[:, :], base[:, :], ps_tot, ALU.add).then_inc(place, 1)
                ge(dve, place, n + 3)
                nc.vector.tensor_reduce(destf[:, :, :], posk[:, :, :, :], AX.X, ALU.add).then_inc(place, 1)
                ge(dve, place, n + 4)
                g2 = b + (-2)
                if g2.within(NB):
                    ge(dve, token_scattered[b.p], 16 * 4 * (g2.j + 1))
                nc.vector.tensor_copy(dest[:, b.p, :, :], destf[:, :, :]).then_inc(place, 1)
                da = (dest_all[:, 2 * b.n:2 * b.n + 2, :] if isinstance(b.j, int) else dest_all[:, bass.ds(b.n * 2, 2), :])
                pass_held(dve, "dve")
                nc.vector.tensor_copy(da, destf[:, :, :]).then_inc(place, 1)
                if isinstance(b.j, int) and b.n % NB_G == NB_G - 1:
                    dve.wait_ge(place, n + PLACE_STEPS)
                    dve.wait_ge(route, ROUTE_STEPS * (b.n + 1))
                    make_plan(b.n // NB_G)
                    if b.n == NB_G - 1:
                        nc.vector.tensor_scalar(base[:, :], base0[:, :], float(E * CAP), None, ALU.add).then_inc(regroup, 1)
                        dve.wait_ge(regroup, 1)

            def body(b, batch):
                nxt, prv, old = b + 1, b + (-1), b + (-2)
                if prv.within(NB):
                    add_attention(prv)

                def low(m):
                    ge(dve, qp_hi, 4 * b.n + m + 1)
                    ge(dve, s_done, b.n)
                    sub(qpT[:, LO, m, :], tq[:, m % 2, :], qpT[:, HI, m, :], qp_lo)

                if b.within(NB):
                    low(0)
                if prv.within(NB):
                    shift2(prv)
                if b.within(NB):
                    low(1)
                if old.within(NB):
                    choose(old)
                if b.within(NB):
                    low(2)
                if nxt.within(NB):
                    norm1(nxt)
                if b.within(NB):
                    low(3)
                if nxt.within(NB):
                    norm1_apply(nxt)
                if isinstance(b.j, int) and b.n == -1:
                    setup_splits()
                if old.within(NB):
                    place_tokens(old)
                if b.within(NB):
                    n = 3 * b.n
                    ge(dve, s_relu, b.n + 1)
                    nc.vector.tensor_tensor(lg[:, :], tl[:, :], ps_mask, ALU.add).then_inc(lg_step, 1)
                    ge(dve, lg_step, n + 1)
                    ge(dve, o_done, 2 * b.n)
                    nc.vector.tensor_copy(lgT[:, HI, :], lg[:, :]).then_inc(lg_step, 1)
                    ge(dve, lg_step, n + 2)
                    sub(lgT[:, LO, :], lg[:, :], lgT[:, HI, :], lg_step)
                if nxt.within(NB):
                    for t in range(TPB):
                        ge(dve, qT_hi, 2 * nxt.n + t + 1)
                        ge(dve, q_done, 4 * nxt.n)
                        sub(qT[:, LO, :, t * P:(t + 1) * P], psT[t][:, :].rearrange("p (c k) -> p c k", c=DC),
                            qT[:, HI, :, t * P:(t + 1) * P], qT_lo)
                if b.within(NB):
                    ge(dve, stage_hi, b.n + 1)
                    if b.p == 0:
                        v = [wuv[:, b.j, h, :, :].rearrange("p c n -> p (c n)") if isinstance(b.j, int)
                             else wuv[:, bass.ds(b.j, 1), h, :, :].rearrange("p e c n -> p (e c n)") for h in (HI, LO)]
                        sub(v[LO], stage[:, 0:2 * D], v[HI], stage_lo)
                    else:
                        v = [wo[:, b.j, h, :] if isinstance(b.j, int)
                             else wo[:, bass.ds(b.j, 1), h, :].rearrange("p e n -> p (e n)") for h in (HI, LO)]
                        sub(v[LO], stage[:, 2 * D:3 * D], v[HI], stage_lo)

            block_steps(dve, body)
            dve.wait_ge(gap_exp, 1)
            nc.vector.tensor_scalar(den_all[:, :], e_all[:, :], 1.0, None, ALU.add).then_inc(weight, 1)
            dve.wait_ge(weight, 1)
            nc.vector.reciprocal(w_all[:, 0, :], den_all[:, :]).then_inc(weight, 1)
            dve.wait_ge(weight, 2)
            nc.vector.tensor_tensor(w_all[:, 1, :], e_all[:, :], w_all[:, 0, :], ALU.mult).then_inc(weight, 1)
            dve.wait_ge(weight, 3)

            def turned_g(t):
                ge(dve, gT_hi, t.n + 1)
                ge(dve, uv_done, t.n - 1)
                sub(zgT[t.p][:, :, P:2 * P], psT[t.p][:, :].rearrange("p (c k) -> p c k", c=DC),
                    zgT[t.p][:, :, 0:P], gT_lo)

            def take_idx(n, q):
                if isinstance(n, int):
                    src = row_all[:, n, :]
                else:
                    src = row_all[:, bass.ds(n, 1), :].rearrange("p n k -> p (n k)")
                nc.vector.tensor_copy(cidx[:, q, :], src).then_inc(cidx_ready, 1)

            def combine(n, q, k):
                w = [w_all[:, j, bass.ds(n, 1)] for j in range(2)]
                ge(dve, xg_loaded[q], 16 * (k + 1))
                ge(dve, y1_gathered[q], 16 * (k + 1))
                nc.vector.scalar_tensor_tensor(y1g[q], y1g[q], w[0], xg[q], ALU.mult, ALU.add).then_inc(comb1, 1)
                ge(dve, y2_gathered[q], 16 * (k + 1))
                ge(dve, comb1, n + 1)
                nc.vector.scalar_tensor_tensor(xg[q], y2g[q], w[1], y1g[q], ALU.mult, ALU.add).then_inc(comb2, 1)

            turned_g(Step(0, 0))

            def tile_body(t, comb):
                if comb is not None:
                    i, q = comb
                    ge(dve, y1_gathered[q], 16 * i)
                    ge(dve, y2_gathered[q], 16 * i)
                    pass_held(dve, "dve")
                    take_idx(2 * i + q, q)
                ge(dve, silu_done, t.n + 1)
                ge(dve, s_turned, t.n - 1)
                nc.vector.tensor_tensor(s_tok[:, t.p, :], sil[:, t.p, :], psQ[t.p][:, R:2 * R], ALU.mult).then_inc(s_ready, 1)
                if (t + 1).within(TILES):
                    turned_g(t + 1)
                ge(dve, sT_hi, t.n + 1)
                ge(dve, y_done, t.n - 1)
                sub(sT[t.p][:, LO, :], psST[t.p][:, 0:P], sT[t.p][:, HI, :], sT_lo)
                if comb is not None:
                    combine(2 * i + q, q, i)

            tile_steps(dve, tile_body)
            half = SEQ // P // 2
            with dve.Fori(half, 2 * half) as i:
                for q in range(2):
                    ge(dve, y1_gathered[q], 16 * i)
                    ge(dve, y2_gathered[q], 16 * i)
                    pass_held(dve, "dve")
                    take_idx(2 * i + q, q)
                for q in range(2):
                    combine(2 * i + q, q, i)

        @block.tensor
        def _(pe):
            def turn(o, i, n=P):
                return pe.transpose(o, i, ident[0:n, 0:n])

            def three(o, w, a, first, last):
                pe.matmul(o, w[LO], a[HI], start=first, stop=False)
                pe.matmul(o, w[HI], a[LO], start=False, stop=False)
                return pe.matmul(o, w[HI], a[HI], start=False, stop=last)

            pe.wait_ge(const_ready, 10)
            pe.wait_ge(w_loaded["ctx"], 16)
            for g in range(NBATCH):
                for c in range(DC):
                    ins = turn(psT[g][:, c * P:(c + 1) * P], ctx_raw[:, g, c * P:(c + 1) * P])
                ins.then_inc(ctx_turned, 1)
            pe.wait_ge(ctxT_ready, 2)
            pe.wait_ge(w_loaded["wk0"], 16)
            pe.wait_ge(w_loaded["wk1"], 16)
            for m in range(DC):
                ge(pe, k_relu, m - 1)
                for c in range(DC):
                    w = z if c < 2 else x1
                    ins = pe.matmul(psQ[m % 2][:, 0:BT], w[:, c % 2, m * P:(m + 1) * P],
                                    ctxT[:, c, :], start=(c == 0), stop=(c == DC - 1))
                ins.then_inc(k_done, 1)
            pe.wait_ge(w_loaded["wv"], 32)
            pe.wait_ge(w_loaded["small"], 64)
            for g in range(NBATCH):
                pe.matmul(ps_out[g][:, :], ones_row[:, :], bv_sb[:, :], start=True, stop=False)
                for c in range(DC):
                    w = stage[:, c * D:(c + 1) * D] if c < 3 else tq[:, :, :].rearrange("p a t -> p (a t)")
                    ins = pe.matmul(ps_out[g][:, :], ctxT[:, c, g * KEYS:(g + 1) * KEYS], w, start=False, stop=(c == DC - 1))
                ins.then_inc(v_done, 1)

            def queries(b):
                ge(pe, qT_lo, 2 * b.n + 2)
                if isinstance(b.j, int) and b.n == 0:
                    pe.wait_ge(wq_ready, DC)
                    pe.wait_ge(k_relu, DC)
                for m in range(DC):
                    ge(pe, qp_relu, 4 * b.n + m - 1)
                    for c in range(DC):
                        ins = three(psQ[m % 2][:, 0:BT],
                                    [wq[:, h, c, m * P:(m + 1) * P] for h in range(2)],
                                    [qT[:, h, c, :] for h in range(2)], c == 0, c == DC - 1)
                    ins.then_inc(q_done, 1)

            def ranks(b):
                ge(pe, route, ROUTE_STEPS * b.n + 9)
                ge(pe, place, PLACE_STEPS * (b.n - 1) + 3)
                for t in range(TPB):
                    for u in range(t):
                        pe.matmul(ps_pos[:, t, :], ones[:, :], chosen[:, u, :], start=(u == 0), stop=False)
                    pe.matmul(ps_pos[:, t, :], before[:, :], chosen[:, t, :], start=(t == 0), stop=True)
                for t in range(TPB):
                    ins = pe.matmul(ps_tot, ones[:, :], chosen[:, t, :], start=(t == 0), stop=(t == TPB - 1))
                ins.then_inc(rank_done, 1)

            def turn_z(b, t):
                ge(pe, z_ready, 2 * b.n + t + 1)
                ge(pe, zT_ready, 2 * b.n + t)
                for c in range(DC):
                    ins = turn(psZ[:, c * P:(c + 1) * P], z[:, t, c * P:(c + 1) * P])
                ins.then_inc(z_turned, 1)

            def scores(b, batch):
                ge(pe, m_loaded[b.p], 16 * (b.j + 1))
                ge(pe, x1_ready, 2 * b.n)
                if isinstance(b.j, int) and b.n == 0:
                    pe.wait_ge(k_lo, DC)
                    pe.wait_ge(v_relu, 2)
                for t in range(TPB):
                    turn(ps_mask[:, t * P:(t + 1) * P], mraw[:, b.p, t, :])
                ge(pe, qp_lo, 4 * b.n + 4)
                for c in range(DC):
                    ins = three(psS[:, 0:BT], [kpT[:, h, c, batch * KEYS:(batch + 1) * KEYS] for h in range(2)],
                                [qpT[:, h, c, :] for h in range(2)], c == 0, c == DC - 1)
                ins.then_inc(s_done, 1)

            def turn_x(b):
                ge(pe, xn_ready, 2 * b.n + 2)
                ge(pe, qT_lo, 2 * b.n)
                for t in range(TPB):
                    for c in range(DC):
                        ins = turn(psT[t][:, c * P:(c + 1) * P], xn[:, t, c * P:(c + 1) * P])
                    ins.then_inc(xn_turned, 1)

            def gates(b):
                ge(pe, zT_ready, 2 * b.n + 2)
                ge(pe, logT_ready, b.n)
                ge(pe, place, PLACE_STEPS * (b.n - 1) + 3)
                for c in range(DC):
                    ins = pe.matmul(ps_log, gw[:, c, :], zT[:, c, :], start=(c == 0), stop=(c == DC - 1))
                ins.then_inc(gate_done, 1)

            def attend(b, batch):
                ge(pe, lg_step, 3 * b.n + 3)
                ge(pe, x1_ready, 2 * b.n)
                if isinstance(b.j, int) and b.n == 0:
                    pe.wait_ge(v_lo, 2)
                for t in range(TPB):
                    three(ps_out[t][:, :], [lgT[:, h, t * P:(t + 1) * P] for h in range(2)],
                          [vp[:, h, batch, :] for h in range(2)], True, True).then_inc(o_done, 1)

            def turn_logits(b):
                ge(pe, logT_ready, b.n + 1)
                ge(pe, route, ROUTE_STEPS * (b.n - 1) + 1)
                pass_held(pe, "pe")
                for t in range(TPB):
                    ins = turn(ps_logit[:, t, :], logT[:, t * P:(t + 1) * P], E)
                ins.then_inc(logit_turned, 1)

            def body(b, batch):
                nxt, prv, old = b + 1, b + (-1), b + (-2)
                if b.within(NB):
                    queries(b)
                if old.within(NB):
                    ranks(old)
                if prv.within(NB):
                    turn_z(prv, 0)
                if b.within(NB):
                    scores(b, batch)
                if prv.within(NB):
                    turn_z(prv, 1)
                if nxt.within(NB):
                    turn_x(nxt)
                if prv.within(NB):
                    gates(prv)
                if b.within(NB):
                    attend(b, batch)
                if prv.within(NB):
                    turn_logits(prv)

            block_steps(pe, body)

            def turn_g(t):
                ge(pe, z_gathered[t.p], 16 * (t.j + 1))
                ge(pe, gT_lo, t.n - 1)
                for c in range(DC):
                    ins = turn(psT[t.p][:, c * P:(c + 1) * P], zg[t.p][:, c * P:(c + 1) * P])
                ins.then_inc(g_turned, 1)

            def expert(t):
                return pe.value_load(sched_exp[0:1, bass.ds(t.n, 1)], min_val=0, max_val=E - 1)

            def up(t):
                e = expert(t)
                ge(pe, gT_lo, t.n + 1)
                ge(pe, s_ready, t.n - 1)
                for c in range(DC):
                    w = [wuv[:, bass.ds(e, 1), h, c, :].rearrange("p e n -> p (e n)") for h in range(2)]
                    a = [zgT[t.p][:, c, h * P:(h + 1) * P] for h in range(2)]
                    ins = three(psQ[t.p][:, 0:2 * R], a, w, c == 0, c == DC - 1)
                ins.then_inc(uv_done, 1)

            def down(t):
                e = expert(t)
                ge(pe, sT_lo, t.n + 1)
                ge(pe, y_ready, t.n - 1)
                w = [wo[:, bass.ds(e, 1), h, :].rearrange("p e n -> p (e n)") for h in range(2)]
                three(ps_out[t.p][:, :], [sT[t.p][:, h, :] for h in range(2)], w, True, True).then_inc(y_done, 1)

            def turn_s(t):
                ge(pe, s_ready, t.n + 1)
                ge(pe, sT_lo, t.n - 1)
                turn(psST[t.p][:, 0:P], s_tok[:, t.p, :]).then_inc(s_turned, 1)

            pe.wait_ge(place, PLACE_STEPS * NB)
            pe.wait_ge(stage_lo, NB)
            pe.wait_ge(x1_ready, 2 * NB)
            turn_g(Step(0, 0))

            def tile_body(t):
                up(t)
                if (t + 1).within(TILES):
                    turn_g(t + 1)
                if (t + (-1)).within(TILES):
                    down(t + (-1))
                turn_s(t)

            tile_body(Step(0, 0))
            tile_body(Step(0, 1))
            with pe.Fori(1, TILES_G // 2) as i:
                for p in range(2):
                    tile_body(Step(i, p))
            pe.wait_ge(plan, PLAN_STEPS + SCHED_STEPS)
            with pe.Fori(TILES_G // 2, TILES // 2 - 1) as i:
                for p in range(2):
                    tile_body(Step(i, p))
            tile_body(Step(TILES // 2 - 1, 0))
            tile_body(Step(TILES // 2 - 1, 1))
            down(Step(TILES // 2 - 1, 1))


_INS = ['x', 'ctx_1024', 'mask_1xSxS2_ff0', 'L0_xattn_kernel_q', 'L0_xattn_kernel_k', 'L0_xattn_kernel_v',
        'L0_xattn_bias_q', 'L0_xattn_bias_k', 'L0_xattn_bias_v', 'L0_ffn_gate_w', 'L0_ffn_Wu', 'L0_ffn_Wv', 'L0_ffn_Wo']
_OUTS = [((NBATCH, SEQ, D), 'float32')]


def kernel(**inputs):
    import numpy as _np
    import concourse.bacc as _bacc
    from concourse import mybir as _mybir
    from concourse.bass_utils import run_bass_kernel_spmd as _run

    nc = _bacc.Bacc("TRN2", target_bir_lowering=False, num_devices=1)
    arrays, args = {}, []
    for name in _INS:
        a = _np.ascontiguousarray(inputs[name])
        arrays[f"in_{name}_dram"] = a
        args.append(nc.dram_tensor(f"in_{name}_dram", a.shape, _mybir.dt.from_np(a.dtype), kind="ExternalInput").ap())
    for i, (shape, dtype) in enumerate(_OUTS):
        dt = _mybir.dt.from_np(_np.dtype(dtype))
        args.append(nc.dram_tensor(f"out_{i}_dram", shape, dt, kind="ExternalOutput").ap())
    moe_block(nc, *args)
    r = _run(nc, [arrays], core_ids=[0])
    return r.results[0]["out_0_dram"]
```

```python
import numpy as np
import concourse.bass as bass
from concourse import mybir
from contextlib import ExitStack

F32 = mybir.dt.float32
F32R = mybir.dt.float32r
BF16 = mybir.dt.bfloat16
I32 = mybir.dt.int32
U32 = mybir.dt.uint32
ALU = mybir.AluOpType
ACT = mybir.ActivationFunctionType
AX = mybir.AxisListType

P = 128
LOG_P = 7
D = 512
DC = D // P
NBATCH, SEQ = 2, 2048
KEYS = 128
E, R = 8, 128
TOK = NBATCH * SEQ
TPB = 2
BT = TPB * P
NB = TOK // BT
NB_G = NB // NBATCH
NTILE = TOK // P
TILES_B = SEQ // P
CAP = SEQ
DUMMY = NBATCH * E * CAP
NSLOT = DUMMY + P
TILES_G = 2 * SEQ // P + E - 1
TILES = NBATCH * TILES_G
SCALE = float(np.float32(1.0) / np.sqrt(np.float32(D)))
EPS = 1e-5
HI, LO = 0, 1


def ge(eng, sem, value):
    if isinstance(value, int) and value <= 0:
        return
    eng.wait_ge(sem, value)


class Step:

    def __init__(self, j, p):
        self.j, self.p = j, p

    @property
    def n(self):
        return 2 * self.j + self.p

    def __add__(self, k):
        q = self.p + k
        return Step(self.j + q // 2, q % 2)

    def within(self, count):
        return not isinstance(self.j, int) or 0 <= self.n < count


def block_steps(eng, body):
    def straight(a, b):
        for n in range(a, b):
            body(Step(n // 2, n % 2), min(max(n // NB_G, 0), 1))

    def looped(a, b, batch):
        with eng.Fori(0, (b - a) // 2) as i:
            for p in range(2):
                body(Step(i + a // 2, p), batch)

    straight(-1, 4)
    looped(4, NB_G, 0)
    straight(NB_G, NB_G + 2)
    looped(NB_G + 2, NB - 2, 1)
    straight(NB - 2, NB + 2)


def tile_steps(eng, body):
    first = TILES_G // 2
    comb = SEQ // P
    body(Step(0, 0), None)
    body(Step(0, 1), None)
    with eng.Fori(1, first) as i:
        for p in range(2):
            body(Step(i, p), None)
    for p in range(2):
        body(Step(first, p), None)
    with eng.Fori(0, comb // 2) as i:
        for p in range(4):
            body(Step(2 * i + first + 1 + p // 2, p % 2), (i, p // 2) if p % 2 else None)
    for n in range(2 * (first + 1) + 2 * comb, TILES):
        body(Step(n // 2, n % 2), None)


def moe_block(nc, x, ctx_in, mask, kq, kk, kv, bq, bk, bv, gate_w, Wu, Wv, Wo, out):
    ctx = ExitStack()
    with ctx:
        def sb(name, shape, dt=F32):
            return ctx.enter_context(nc.sbuf_tensor(name, shape, dt))

        def bank(name):
            return ctx.enter_context(nc.psum_tensor(name, [P, 512], F32))

        def sem(name):
            return ctx.enter_context(nc.semaphore(name))

        def pair(name):
            return [sem(f"{name}{i}") for i in range(2)]

        def dram(name, shape, dt=F32):
            return nc.dram_tensor(name, shape, dt, kind="Internal").ap()

        z_dram = dram("z_dram", [TOK, D])
        x1_dram = dram("x1_dram", [TOK, D])
        y_dram = [dram(f"y_dram{g}", [TILES_G * P, D]) for g in range(NBATCH)]
        slot_token = dram("slot_token", [NSLOT, 1], I32)

        wq = sb("wq", [P, 2, DC, D], F32R)
        wuv = sb("wuv", [P, E, 2, DC * 2 * R], F32R)
        wo = sb("wo", [P, E, 2, D], F32R)
        kpT = sb("kpT", [P, 2, DC, NBATCH * KEYS], F32R)
        vp = sb("vp", [P, 2, NBATCH, D], F32R)
        qT = sb("qT", [P, 2, DC, BT], F32R)
        qpT = sb("qpT", [P, 2, DC, BT], F32R)
        lgT = sb("lgT", [P, 2, BT], F32R)
        zgT = [qT[:, h, :, :] for h in range(2)]
        sT = [lgT[:, i, :].rearrange("p (h t) -> p h t", h=2) for i in range(2)]
        xin = sb("xin", [P, 2, TPB, D])
        x1 = sb("x1", [P, TPB, D])
        xn = sb("xn", [P, TPB, D])
        z = sb("z", [P, TPB, D])
        zT = sb("zT", [P, DC, BT])
        stage = sb("stage", [P, 3 * D])
        tq = sb("tq", [P, 2, BT])
        wraw = sb("wraw", [P, 4 * D])
        mraw = sb("mraw", [P, 2, TPB, KEYS])
        tl = sb("tl", [P, BT])
        lg = sb("lg", [P, BT])
        gate_work = sb("gate_work", [P, 2, 2, R])
        sil, s_tok = gate_work[:, 0, :, :], gate_work[:, 1, :, :]
        zeros_i = gate_work[:, :, :, :].rearrange("p a b r -> p (a b r)")[:, 0:NSLOT // P].bitcast(I32)
        wk_raw = z[:, :, :].rearrange("p t d -> p (t d)")
        zg = [xn[:, i, :] for i in range(2)]
        ysb = [zT[:, 2 * i:2 * i + 2, :].rearrange("p c t -> p (c t)") for i in range(2)]
        plan_big = [wraw[:, (2 + i) * D:(2 + i) * D + 2 * TILES_B * E].rearrange("p (n e) -> p n e", e=E) for i in range(2)]
        y1g = [xin[:, 0, i, :] for i in range(2)] + [wraw[:, i * D:(i + 1) * D] for i in range(2)]
        y2g = [xin[:, 1, i, :] for i in range(2)] + [wraw[:, (2 + i) * D:(3 + i) * D] for i in range(2)]
        xg = [x1[:, i, :] for i in range(2)] + [z[:, i, :] for i in range(2)]
        ctx_raw = zT[:, :, :].rearrange("p c t -> p (c t)").rearrange("p (b d) -> p b d", b=NBATCH)
        ctxT = sb("ctxT", [P, DC, NBATCH * KEYS])
        ident = sb("ident", [P, P])
        before = sb("before", [P, P], BF16)
        ones = sb("ones", [P, P], BF16)
        ones_row = sb("ones_row", [1, P])
        gw = sb("gw", [P, DC, E])
        bq_sb = sb("bq_sb", [P, DC])
        bk_sb = sb("bk_sb", [P, DC])
        bv_sb = sb("bv_sb", [1, D])
        st1 = sb("st1", [P, TPB, 6])
        mv1 = sb("mv1", [P, TPB, 2])
        rstd1 = sb("rstd1", [P, TPB])
        st2 = sb("st2", [P, TPB, 6])
        mv2 = sb("mv2", [P, TPB, 2])
        rstd2 = sb("rstd2", [P, TPB])
        nmr1 = sb("nmr1", [P, TPB])
        nmr2 = sb("nmr2", [P, TPB])
        ve1 = sb("ve1", [P, TPB])
        ve2 = sb("ve2", [P, TPB])
        minus_half = sb("minus_half", [P, TPB])
        logT = sb("logT", [E, BT])
        logit = sb("logit", [P, TPB, E])
        top_v = sb("top_v", [P, TPB, 8])
        top_i = sb("top_i", [P, TPB, 8], U32)
        top_f = sb("top_f", [P, TPB, 2])
        iota_i = sb("iota_i", [P, TPB, 2, E], I32)
        iota_f = sb("iota_f", [P, TPB, 2, E])
        onehot = sb("onehot", [P, TPB, 2, E])
        chosen = sb("chosen", [P, TPB, E], BF16)
        base_i = sb("base_i", [P, E], I32)
        base0 = sb("base0", [P, E])
        base = sb("base", [P, E])
        pos = sb("pos", [P, TPB, E])
        posk = sb("posk", [P, TPB, 2, E])
        destf = sb("destf", [P, TPB, 2])
        dest = sb("dest", [P, 2, TPB, 2], U32)
        dest_all = sb("dest_all", [P, NTILE, 2])
        expert_all = sb("expert_all", [P, NTILE, 2])
        row_all = sb("row_all", [P, NTILE, 2], U32)
        before_e = sb("before_e", [P, E])
        shift_e = sb("shift_e", [P, E])
        shift_t = sb("shift_t", [P, TILES_B * 2])
        cidx = sb("cidx", [P, 4, 2], U32)
        gap_all = sb("gap_all", [P, NTILE])
        e_all = sb("e_all", [P, NTILE])
        den_all = sb("den_all", [P, NTILE])
        w_all = sb("w_all", [P, 2, NTILE])
        tokid = sb("tokid", [P, 2, TPB], I32)
        upto_e = sb("upto_e", [P, E, E])
        tile_i = sb("tile_i", [P, 1], I32)
        tile_s = sb("tile_s", [P, 1])
        cnt = sb("cnt", [P, E])
        cnt_i = sb("cnt_i", [P, E], I32)
        len_i = sb("len_i", [P, E], I32)
        length = sb("length", [P, E])
        cum = sb("cum", [P, E])
        past = sb("past", [P, E])
        pastc = sb("pastc", [P, E])
        exp_f, prev_f, off_f, row_f, over_f, row2_f = (sb(f"plan{i}", [P, 1]) for i in range(6))
        expc_f = sb("expc_f", [P, NBATCH])
        lens = sb("lens", [P, E, E])
        table_row = sb("table_row", [P, NBATCH], U32)
        slot_rows = sb("slot_rows", [P, P], I32)
        slot_rows_f = sb("slot_rows_f", [P, P])
        idx_all = [sb(f"idx_all{g}", [P, TILES_G], U32) for g in range(NBATCH)]
        sched_exp = sb("sched_exp", [1, TILES], I32)
        idx = sb("idx", [P, 2], U32)

        psT = [bank(f"psT{i}") for i in range(2)]
        psQ = [bank(f"psQ{i}") for i in range(2)]
        psS = bank("psS")
        psO = bank("psO")
        psZ = bank("psZ")
        psG = bank("psG")
        ps_out = [psO, psS]
        ps_mask = psS[:, BT:2 * BT]
        ps_log = psG[0:E, 0:BT]
        ps_logit = psG[:, BT:BT + TPB * E].rearrange("p (t e) -> p t e", e=E)
        ps_pos = psG[:, BT + 32:BT + 32 + TPB * E].rearrange("p (t e) -> p t e", e=E)
        ps_tot = psG[:, BT + 64:BT + 64 + E]
        psST = psZ

        const_ready = sem("const_ready")
        pool_step = sem("pool_step")
        conv_ready = sem("conv_ready")
        w_loaded = {k: sem(f"load_{k}") for k in ("ctx", "wk0", "wk1", "wq", "wv", "small", "table")}
        ctxT_ready = sem("ctxT_ready")
        ctx_turned = sem("ctx_turned")
        wq_hi = sem("wq_hi")
        wq_ready = sem("wq_ready")
        k_done = sem("k_done")
        k_relu = sem("k_relu")
        k_hi = sem("k_hi")
        k_lo = sem("k_lo")
        v_done = sem("v_done")
        v_relu = sem("v_relu")
        v_hi = sem("v_hi")
        v_lo = sem("v_lo")
        x_loaded = pair("x_loaded")
        m_loaded = pair("m_loaded")
        stats1 = sem("stats1")
        rstd1_ready = sem("rstd1_ready")
        xn_ready = sem("xn_ready")
        xn_turned = sem("xn_turned")
        qT_hi = sem("qT_hi")
        qT_lo = sem("qT_lo")
        q_done = sem("q_done")
        qp_relu = sem("qp_relu")
        qp_hi = sem("qp_hi")
        qp_lo = sem("qp_lo")
        s_done = sem("s_done")
        s_relu = sem("s_relu")
        lg_step = sem("lg_step")
        o_done = sem("o_done")
        x1_ready = sem("x1_ready")
        stats2 = sem("stats2")
        rstd2_ready = sem("rstd2_ready")
        nmr2_ready = sem("nmr2_ready")
        z_ready = sem("z_ready")
        x1_stored = pair("x1_stored")
        z_stored = pair("z_stored")
        z_turned = sem("z_turned")
        zT_ready = sem("zT_ready")
        gate_done = sem("gate_done")
        logT_ready = sem("logT_ready")
        logit_turned = sem("logit_turned")
        route = sem("route")
        rank_done = sem("rank_done")
        place = sem("place")
        token_scattered = pair("token_scattered") 
        tokid_moved = sem("tokid_moved")
        stage_loaded = sem("stage_loaded")
        stage_hi = sem("stage_hi")
        stage_lo = sem("stage_lo")
        rows_gathered = sem("rows_gathered")
        rows_float = sem("rows_float")
        rows_turned = sem("rows_turned")
        sched_ready = sem("sched_ready")
        idx_ready = sem("idx_ready")
        nmr1_ready = sem("nmr1_ready")
        regroup = sem("regroup")
        plan = sem("plan")
        gap_exp = sem("gap_exp")
        weight = sem("weight")
        z_gathered = pair("z_gathered")
        g_turned = sem("g_turned")
        gT_hi = sem("gT_hi")
        gT_lo = sem("gT_lo")
        uv_done = sem("uv_done")
        silu_done = sem("silu_done")
        s_ready = sem("s_ready")
        s_turned = sem("s_turned")
        sT_hi = sem("sT_hi")
        sT_lo = sem("sT_lo")
        y_done = sem("y_done")
        y_ready = sem("y_ready")
        y_stored = pair("y_stored")
        cidx_ready = sem("cidx_ready")
        y1_gathered = [sem(f"y1_gathered{i}") for i in range(4)]
        y2_gathered = [sem(f"y2_gathered{i}") for i in range(4)]
        xg_loaded = [sem(f"xg_loaded{i}") for i in range(4)]
        comb1 = sem("comb1")
        comb2 = sem("comb2")
        out_stored = [sem(f"out_stored{i}") for i in range(4)]
        held = {e: sem(f"held_{e}") for e in ("pool", "dve", "act", "sp", "pe")}

        ROUTE_STEPS, PLACE_STEPS, PLAN_STEPS, SCHED_STEPS = 10, 6, 22, 16

        x_blk = x.rearrange("g (b t p) d -> (g b) p t d", t=TPB, p=P)
        x1_blk = x1_dram.rearrange("(b t p) d -> b p t d", t=TPB, p=P)
        z_blk = z_dram.rearrange("(b t p) d -> b p t d", t=TPB, p=P)
        m_blk = mask.rearrange("o (b t p) k -> (o b) p t k", t=TPB, p=P)
        x1_tile = x1_dram.rearrange("(n p) d -> n p d", p=P)
        out_tile = out.rearrange("g (n p) d -> (g n) p d", p=P)
        wu_v = Wu.rearrange("e (c p) r -> e p c r", p=P)
        wv_v = Wv.rearrange("e (c p) r -> e p c r", p=P)
        w_v = {k: w.rearrange("a b (c p) n -> p (a b c) n", p=P) for k, w in (("q", kq), ("k", kk), ("v", kv))}

        def used(q):
            return TILES_B // 2 if q < 2 else 0

        def pass_held(eng, name):
            eng.sem_inc(held[name], 1)

        def expert_parts(b):
            def uv(lo, hi):
                if isinstance(b.j, int):
                    return lambda h: wuv[:, b.j, h, lo:hi]
                return lambda h: wuv[:, bass.ds(b.j, 1), h, lo:hi].rearrange("p e n -> p (e n)")

            def o(h):
                if isinstance(b.j, int):
                    return wo[:, b.j, h, :]
                return wo[:, bass.ds(b.j, 1), h, :].rearrange("p e n -> p (e n)")

            cut = 3 * D // 2
            if b.p == 0:
                return [(uv(0, cut), stage[:, 0:cut])]
            return [(uv(cut, 2 * D), stage[:, cut:2 * D]), (o, stage[:, 2 * D:3 * D])]

        block = ctx.enter_context(nc.Block())

        @block.sync
        def _(sp):
            for q in range(4):
                sp.sem_inc(out_stored[q], 16)
            sp.dma_start(xin[:, 0, :, :], x_blk[0]).then_inc(x_loaded[0], 16)
            sp.dma_start(ctx_raw, ctx_in.rearrange("b k d -> k b d")).then_inc(w_loaded["ctx"], 16)
            sp.dma_start(wk_raw.rearrange("p (c n) -> p c n", c=2), w_v["k"][:, 0:2, :]).then_inc(w_loaded["wk0"], 16)
            sp.dma_start(x1[:, :, :], w_v["k"][:, 2:4, :]).then_inc(w_loaded["wk1"], 16)
            with nc.allow_non_contiguous_dma("small biases"):
                sp.dma_start(bq_sb[:, :], bq.rearrange("(m p) -> p m", p=P)).then_inc(w_loaded["small"], 16)
                sp.dma_start(bk_sb[:, :], bk.rearrange("(m p) -> p m", p=P)).then_inc(w_loaded["small"], 16)
                sp.dma_start(gw[:, :, :], gate_w.rearrange("(c p) e -> p c e", p=P)).then_inc(w_loaded["small"], 16)
            sp.dma_start(bv_sb[:, :], bv.rearrange("(a n) -> a n", a=1)).then_inc(w_loaded["small"], 16)
            sp.dma_start(wraw[:, :].rearrange("p (c n) -> p c n", c=DC), w_v["q"]).then_inc(w_loaded["wq"], 16)
            sp.dma_start(stage[:, 0:3 * D].rearrange("p (c n) -> p c n", c=3), w_v["v"][:, 0:3, :]).then_inc(w_loaded["wv"], 16)
            sp.dma_start(tq[:, :, :].rearrange("p a t -> p (a t)"), w_v["v"][:, 3, :]).then_inc(w_loaded["wv"], 16)
            sp.wait_ge(const_ready, 1)
            sp.dma_start(slot_token.rearrange("(p n) o -> p (n o)", p=P), zeros_i).then_inc(w_loaded["table"], 16)

            def load_experts(e):
                uv = stage[:, 0:DC * 2 * R].rearrange("p (c h r) -> p c h r", c=DC, h=2)
                sp.dma_start(uv[:, :, 0, :], wu_v[e]).then_inc(stage_loaded, 16)
                sp.dma_start(uv[:, :, 1, :], wv_v[e]).then_inc(stage_loaded, 16)
                sp.dma_start(stage[:, 2 * D:3 * D], Wo[e]).then_inc(stage_loaded, 16)

            def body(b, batch):
                nxt, prv = b + 1, b + (-1)
                if nxt.within(NB) and not (isinstance(nxt.j, int) and nxt.n == 0):
                    ge(sp, x1_ready, 2 * (nxt.n - 2) + 2)
                    sp.dma_start(xin[:, nxt.p, :, :], x_blk[nxt.n]).then_inc(x_loaded[nxt.p], 16)
                if b.within(NB):
                    ge(sp, s_done, b.n - 1)
                    sp.dma_start(mraw[:, b.p, :, :], m_blk[b.n - batch * NB_G]).then_inc(m_loaded[b.p], 16)
                if prv.within(NB):
                    ge(sp, x1_ready, 2 * prv.n + 2)
                    sp.dma_start(x1_blk[prv.n], x1[:, :, :]).then_inc(x1_stored[prv.p], 16)
                    ge(sp, z_ready, 2 * prv.n + 2)
                    sp.dma_start(z_blk[prv.n], z[:, :, :]).then_inc(z_stored[prv.p], 16)
                if isinstance(b.j, int) and b.n == -1:
                    sp.wait_ge(v_done, 2)
                    load_experts(0)
                elif b.p == 1 and b.within(NB - 2):
                    ge(sp, stage_lo, 3 * (b.j + 1))
                    load_experts(b.j + 1)

            block_steps(sp, body)

            def store_out(n, q, k):
                sp.wait_ge(comb2, n + 3)
                sp.dma_start(out_tile[n], xg[q]).then_inc(out_stored[q], 16)

            def load_x1(n, q, k):
                ge(sp, out_stored[q], 16 * (k + 1))
                sp.dma_start(xg[q], x1_tile[n]).then_inc(xg_loaded[q], 16)

            y_tile = [y.rearrange("(n p) d -> n p d", p=P) for y in y_dram]

            def tile_body(t, comb, g):
                if comb is not None:
                    i, q = comb
                    load_x1(2 * i + q, q, i)
                sp.wait_ge(y_ready, t.n + 1)
                sp.dma_start(y_tile[g][t.n - g * TILES_G], ysb[t.p]).then_inc(y_stored[t.p], 16)
                if comb is not None:
                    store_out(2 * i + q, q, i)

            first = TILES_G // 2
            with sp.Fori(0, first) as i:
                for p in range(2):
                    tile_body(Step(i, p), None, 0)
            for n in range(2 * first, 2 * first + 2):
                tile_body(Step(n // 2, n % 2), None, n // TILES_G)
            with sp.Fori(0, SEQ // P // 2) as i:
                for p in range(4):
                    tile_body(Step(2 * i + first + 1 + p // 2, p % 2), (i, p // 2) if p % 2 else None, 1)
            for n in range(2 * (first + 1) + 2 * (SEQ // P), TILES):
                tile_body(Step(n // 2, n % 2), None, n // TILES_G)
            with sp.Fori(0, TILES_B // 4) as i:
                for q in range(4):
                    load_x1(TILES_B + 4 * i + q, q, i + used(q))
                for q in range(4):
                    store_out(TILES_B + 4 * i + q, q, i + used(q))
            for q in range(4):
                sp.wait_ge(out_stored[q], 16 * (TILES_B // 4 + used(q) + 1))
            for q in range(2):
                sp.wait_ge(y_stored[q], 16 * TILES // 2)
                sp.wait_ge(x1_stored[q], 16 * NB // 2)
                sp.wait_ge(z_stored[q], 16 * NB // 2)

        @block.gpsimd
        def _(pool):
            nc.gpsimd.memset(zeros_i, 0).then_inc(const_ready, 1)
            nc.gpsimd.memset(ident[:, :], 0.0).then_inc(pool_step, 1)
            nc.gpsimd.memset(before[:, :], 1.0).then_inc(pool_step, 1)
            nc.gpsimd.memset(upto_e[:, :, :], 1.0).then_inc(pool_step, 1)
            pool.wait_ge(pool_step, 3)
            nc.gpsimd.affine_select(out=ident[:, :], in_=ident[:, :], compare_op=ALU.not_equal, fill=1.0,
                                    base=0, pattern=[[-1, P]], channel_multiplier=1).then_inc(const_ready, 1)
            nc.gpsimd.affine_select(out=before[:, :], in_=before[:, :], compare_op=ALU.is_gt, fill=0.0,
                                    base=0, pattern=[[1, P]], channel_multiplier=-1).then_inc(const_ready, 1)
            nc.gpsimd.affine_select(out=upto_e[:, :, :], in_=upto_e[:, :, :], compare_op=ALU.is_ge, fill=0.0,
                                    base=0, pattern=[[1, E], [-1, E]], channel_multiplier=0).then_inc(const_ready, 1)
            nc.gpsimd.memset(ones[:, :], 1.0).then_inc(const_ready, 1)
            nc.gpsimd.memset(ones_row[:, :], 1.0).then_inc(const_ready, 1)
            nc.gpsimd.memset(minus_half[:, :], -0.5).then_inc(const_ready, 1)
            nc.gpsimd.iota(iota_i[:, :, :, :], [[0, TPB], [0, 2], [1, E]], base=0, channel_multiplier=0).then_inc(const_ready, 1)
            nc.gpsimd.iota(base_i[:, :], [[CAP, E]], base=0, channel_multiplier=0).then_inc(const_ready, 1)
            nc.gpsimd.iota(tile_i[:, :], [[0, 1]], base=0, channel_multiplier=P).then_inc(const_ready, 1)
            for q in range(2):
                nc.gpsimd.iota(tokid[:, q, :], [[P, TPB]], base=q * BT, channel_multiplier=1).then_inc(tokid_moved, 1)

            def body(b, batch):
                prv, nxt, old = b + (-1), b + 1, b + (-2)
                if prv.within(NB):
                    ge(pool, stats2, 5 * prv.n + 5)
                    ge(pool, z_ready, 2 * prv.n)
                    nc.gpsimd.tensor_tensor(rstd2[:, :], ve2[:, :], minus_half[:, :], ALU.pow).then_inc(rstd2_ready, 1)
                if nxt.within(NB):
                    ge(pool, stats1, 5 * nxt.n + 5)
                    ge(pool, xn_ready, 2 * nxt.n)
                    nc.gpsimd.tensor_tensor(rstd1[:, :], ve1[:, :], minus_half[:, :], ALU.pow).then_inc(rstd1_ready, 1)
                if old.within(NB):
                    if isinstance(old.j, int) and old.n == 0:
                        pool.wait_ge(w_loaded["table"], 16)
                    ge(pool, place, PLACE_STEPS * old.n + 5)
                    ge(pool, tokid_moved, old.n + 1)
                    pass_held(pool, "pool")
                    for t in range(TPB):
                        for k in range(2):
                            pool.indirect_dma_start(
                                out=slot_token, out_offset=bass.IndirectOffsetOnAxis(ap=dest[:, old.p, t, k:k + 1], axis=0),
                                in_=tokid[:, old.p, t:t + 1], in_offset=None).then_inc(token_scattered[old.p], 16)
                if b.within(NB):
                    for n, (dst, src) in enumerate(expert_parts(b)):
                        ge(pool, stage_hi, 3 * b.j + b.p + n + 1)
                        pass_held(pool, "pool")
                        nc.gpsimd.tensor_tensor(dst(LO), src, dst(HI), ALU.subtract).then_inc(stage_lo, 1)
                if (b + (-3)).within(NB):
                    o = b + (-3)
                    ge(pool, token_scattered[o.p], 16 * 4 * (o.j + 1))
                    pass_held(pool, "pool")
                    nc.gpsimd.tensor_scalar(tokid[:, o.p, :], tokid[:, o.p, :], 2 * BT, None, ALU.add).then_inc(tokid_moved, 1)

            block_steps(pool, body)

            def gather_rows(g):
                for q in range(2):
                    pool.wait_ge(token_scattered[q], 16 * 4 * NB_G // 2 * (g + 1))
                pool.wait_ge(plan, PLAN_STEPS * g + SCHED_STEPS)
                ge(pool, rows_float, g)
                pool.indirect_dma_start(out=slot_rows[0:TILES_G, :], out_offset=None,
                                        in_=slot_token.rearrange("(a b) o -> a (b o)", b=P),
                                        in_offset=bass.IndirectOffsetOnAxis(ap=table_row[0:TILES_G, g:g + 1], axis=0)
                                        ).then_inc(rows_gathered, 16)

            gather_rows(0)

            def gather(t, g):
                if not t.within(TILES):
                    return
                n = t.n - g * TILES_G
                ge(pool, z_gathered[t.p], 16 * t.j)
                pass_held(pool, "pool")
                nc.gpsimd.tensor_copy(idx[:, t.p:t.p + 1], idx_all[g][:, n:n + 1] if isinstance(n, int)
                                      else idx_all[g][:, bass.ds(n, 1)]).then_inc(idx_ready, 1)
                ge(pool, idx_ready, t.n + 1)
                ge(pool, g_turned, t.n - 1)
                pass_held(pool, "pool")
                pool.indirect_dma_start(out=zg[t.p], out_offset=None, in_=z_dram,
                                        in_offset=bass.IndirectOffsetOnAxis(ap=idx[:, t.p:t.p + 1], axis=0)
                                        ).then_inc(z_gathered[t.p], 16)

            def gather_y(n, q, k, g):
                ge(pool, cidx_ready, n + 1)
                ge(pool, comb2, n + 1 if g == 0 else n - 1)
                pass_held(pool, "pool")
                for kk_, (buf, s) in enumerate(((y1g[q], y1_gathered[q]), (y2g[q], y2_gathered[q]))):
                    pool.indirect_dma_start(out=buf, out_offset=None, in_=y_dram[g],
                                            in_offset=bass.IndirectOffsetOnAxis(ap=cidx[:, q, kk_:kk_ + 1], axis=0)
                                            ).then_inc(s, 16)

            for q in range(2):
                pool.wait_ge(z_stored[q], 16 * NB // 2)
            pool.wait_ge(xn_turned, 2 * NB)
            pool.wait_ge(sched_ready, 2)
            gather(Step(0, 0), 0)
            gather(Step(0, 1), 0)
            gather_rows(1)

            def tile_body(t, comb, g):
                gather(t + 2, g)
                if comb is not None:
                    i, q = comb
                    gather_y(2 * i + q, q, i, 0)

            first = TILES_G // 2
            with pool.Fori(0, first - 1) as i:
                for p in range(2):
                    tile_body(Step(i, p), None, 0)
            pool.wait_ge(sched_ready, 4)
            for n in range(2 * first - 2, 2 * first + 2):
                tile_body(Step(n // 2, n % 2), None, (n + 2) // TILES_G)
            pool.wait_ge(y_stored[0], 16 * (first + 1))
            pool.wait_ge(y_stored[1], 16 * first)
            with pool.Fori(0, SEQ // P // 2) as i:
                for p in range(4):
                    tile_body(Step(2 * i + first + 1 + p // 2, p % 2), (i, p // 2) if p % 2 else None, 1)
            for n in range(2 * (first + 1) + 2 * (SEQ // P), TILES):
                tile_body(Step(n // 2, n % 2), None, 1)
            for q in range(2):
                pool.wait_ge(y_stored[q], 16 * TILES // 2)
            with pool.Fori(0, TILES_B // 4) as i:
                for q in range(4):
                    gather_y(TILES_B + 4 * i + q, q, i, 1)

        @block.scalar
        def _(act):
            def copy(o, i, s):
                nc.scalar.activation(o, i, ACT.Copy).then_inc(s, 1)

            for g in range(NBATCH):
                act.wait_ge(ctx_turned, g + 1)
                copy(ctxT[:, :, g * KEYS:(g + 1) * KEYS], psT[g][:, :].rearrange("p (c k) -> p c k", c=DC), ctxT_ready)
            act.wait_ge(w_loaded["wq"], 16)
            for c in range(DC):
                copy(wq[:, HI, c, :], wraw[:, c * D:(c + 1) * D], wq_hi)
            act.wait_ge(w_loaded["small"], 64)
            for m in range(DC):
                act.wait_ge(k_done, m + 1)
                dst = lg if m % 2 == 0 else tl
                ge(act, k_lo, m - 1)
                nc.scalar.activation(dst[:, :], psQ[m % 2][:, 0:BT], ACT.Relu,
                                     bias=bk_sb[:, m:m + 1]).then_inc(k_relu, 1)
                act.wait_ge(k_relu, m + 1)
                copy(kpT[:, HI, m, :], dst[:, :], k_hi)
            for g in range(NBATCH):
                act.wait_ge(v_done, g + 1)
                act.wait_ge(k_done, DC)
                nc.scalar.activation(z[:, g, :], ps_out[g][:, :], ACT.Relu).then_inc(v_relu, 1)
                act.wait_ge(v_relu, g + 1)
                copy(vp[:, HI, g, :], z[:, g, :], v_hi)

            def body(b, batch):
                nxt, prv = b + 1, b + (-1)

                def queries(m):
                    ge(act, q_done, 4 * b.n + m + 1)
                    ge(act, qp_lo, 4 * b.n + m - 1)
                    nc.scalar.activation(tq[:, m % 2, :], psQ[m % 2][:, 0:BT], ACT.Relu,
                                         bias=bq_sb[:, m:m + 1]).then_inc(qp_relu, 1)
                    ge(act, qp_relu, 4 * b.n + m + 1)
                    ge(act, s_done, b.n)
                    copy(qpT[:, HI, m, :], tq[:, m % 2, :], qp_hi)

                def turned_z(t):
                    ge(act, z_turned, 2 * prv.n + t + 1)
                    ge(act, gate_done, prv.n)
                    copy(zT[:, :, t * P:(t + 1) * P], psZ[:, :].rearrange("p (c k) -> p c k", c=DC), zT_ready)

                def norm2(t):
                    if t == 0:
                        ge(act, nmr2_ready, prv.n + 1)
                        ge(act, z_turned, 2 * prv.n)
                        if (prv + (-1)).within(NB):
                            last = prv + (-1)
                            ge(act, z_stored[last.p], 16 * (last.j + 1))
                    nc.scalar.activation(z[:, t, :], x1[:, t, :], ACT.Identity, bias=nmr2[:, t:t + 1],
                                         scale=rstd2[:, t:t + 1]).then_inc(z_ready, 1)

                def norm1(t):
                    if t == 0:
                        ge(act, nmr1_ready, nxt.n + 1)
                        ge(act, xn_turned, 2 * nxt.n)
                    nc.scalar.activation(xn[:, t, :], xin[:, nxt.p, t, :], ACT.Identity, bias=nmr1[:, t:t + 1],
                                         scale=rstd1[:, t:t + 1]).then_inc(xn_ready, 1)

                if b.within(NB):
                    queries(0)
                    queries(1)
                if prv.within(NB):
                    norm2(0)
                if b.within(NB):
                    queries(2)
                if prv.within(NB):
                    norm2(1)
                if b.within(NB):
                    queries(3)
                if prv.within(NB):
                    turned_z(0)
                if nxt.within(NB):
                    norm1(0)
                    norm1(1)
                if b.within(NB):
                    ge(act, s_done, b.n + 1)
                    ge(act, lg_step, 3 * b.n)
                    nc.scalar.activation(tl[:, :], psS[:, 0:BT], ACT.Relu, scale=SCALE).then_inc(s_relu, 1)
                if prv.within(NB):
                    turned_z(1)
                if nxt.within(NB):
                    for t in range(TPB):
                        ge(act, xn_turned, 2 * nxt.n + t + 1)
                        ge(act, q_done, 4 * nxt.n)
                        copy(qT[:, HI, :, t * P:(t + 1) * P], psT[t][:, :].rearrange("p (c k) -> p c k", c=DC), qT_hi)
                if prv.within(NB):
                    ge(act, gate_done, prv.n + 1)
                    ge(act, logit_turned, prv.n)
                    copy(logT[:, :], ps_log, logT_ready)
                if b.within(NB):
                    for dst, src in expert_parts(b):
                        ge(act, stage_loaded, 48 * (b.j + 1))
                        pass_held(act, "act")
                        copy(dst(HI), src, stage_hi)

            block_steps(act, body)
            act.wait_ge(route, ROUTE_STEPS * NB)
            nc.scalar.activation(e_all[:, :], gap_all[:, :], ACT.Exp).then_inc(gap_exp, 1)

            def turned_g(t):
                ge(act, g_turned, t.n + 1)
                ge(act, uv_done, t.n - 1)
                copy(zgT[t.p][:, :, 0:P], psT[t.p][:, :].rearrange("p (c k) -> p c k", c=DC), gT_hi)

            def turned_s(t):
                ge(act, s_turned, t.n + 1)
                ge(act, y_done, t.n - 1)
                copy(sT[t.p][:, HI, :], psST[:, 0:P], sT_hi)

            def take_y(t):
                ge(act, y_done, t.n + 1)
                if not isinstance(t.j, int) or t.n >= 2:
                    ge(act, y_stored[t.p], 16 * t.j)
                copy(ysb[t.p], ps_out[t.p][:, :], y_ready)

            turned_g(Step(0, 0))

            def tile_body(t, comb, last=False):
                ge(act, uv_done, t.n + 1)
                ge(act, s_ready, t.n - 1)
                nc.scalar.activation(sil[:, t.p, :], psQ[t.p][:, 0:R], ACT.Silu).then_inc(silu_done, 1)
                if (t + 1).within(TILES):
                    turned_g(t + 1)
                if (t + (-1)).within(TILES):
                    take_y(t + (-1))
                turned_s(t)

            for n in range(4):
                tile_body(Step(n // 2, n % 2), None)
            with act.Fori(2, TILES // 2 - 1) as i:
                for p in range(2):
                    tile_body(Step(i, p), None)
            tile_body(Step(TILES // 2 - 1, 0), None)
            tile_body(Step(TILES // 2 - 1, 1), None)
            take_y(Step(TILES // 2 - 1, 1))

        @block.vector
        def _(dve):
            def sub(o, a, b, s):
                nc.vector.tensor_tensor(o, a, b, ALU.subtract).then_inc(s, 1)

            dve.sem_inc(comb2, 2)
            dve.wait_ge(const_ready, 10)
            nc.vector.tensor_copy(iota_f[:, :, :, :], iota_i[:, :, :, :]).then_inc(conv_ready, 1)
            nc.vector.tensor_copy(base0[:, :], base_i[:, :]).then_inc(conv_ready, 1)
            nc.vector.tensor_copy(base[:, :], base_i[:, :]).then_inc(conv_ready, 1)
            nc.vector.tensor_copy(tile_s[:, :], tile_i[:, :]).then_inc(conv_ready, 1)
            dve.wait_ge(conv_ready, 4)

            def setup_splits():
                for c in range(DC):
                    dve.wait_ge(wq_hi, c + 1)
                    sub(wq[:, LO, c, :], wraw[:, c * D:(c + 1) * D], wq[:, HI, c, :], wq_ready)
                for m in range(DC):
                    dve.wait_ge(k_hi, m + 1)
                    sub(kpT[:, LO, m, :], (lg if m % 2 == 0 else tl)[:, :], kpT[:, HI, m, :], k_lo)
                for g in range(NBATCH):
                    dve.wait_ge(v_hi, g + 1)
                    sub(vp[:, LO, g, :], z[:, g, :], vp[:, HI, g, :], v_lo)

            def make_plan(g):
                n0 = PLAN_STEPS * g
                step = [n0]

                def link(ins):
                    ins.then_inc(plan, 1)
                    step[0] += 1
                    dve.wait_ge(plan, step[0])

                start = float(g * E * CAP)
                link(nc.vector.scalar_tensor_tensor(cnt[:, :], base[:, :], P - 1 - start, base0[:, :], ALU.add, ALU.subtract))
                link(nc.vector.tensor_copy(cnt_i[:, :], cnt[:, :]))
                link(nc.vector.tensor_scalar(len_i[:, :], cnt_i[:, :], LOG_P, LOG_P,
                                             ALU.logical_shift_right, ALU.logical_shift_left))
                link(nc.vector.tensor_copy(length[:, :], len_i[:, :]))
                link(nc.vector.tensor_tensor(lens[:, :, :], upto_e[:, :, :],
                                             length[:, :].unsqueeze(1).broadcast_to([P, E, E]), ALU.mult))
                link(nc.vector.tensor_reduce(cum[:, :], lens[:, :, :], AX.X, ALU.add))
                link(nc.vector.tensor_scalar(past[:, :], cum[:, :], tile_s[:, 0:1], None, ALU.is_le))
                link(nc.vector.tensor_tensor(pastc[:, :], past[:, :], cum[:, :], ALU.mult))
                link(nc.vector.tensor_reduce(exp_f[:, :], past[:, :], AX.X, ALU.add))
                link(nc.vector.tensor_reduce(prev_f[:, :], pastc[:, :], AX.X, ALU.max))
                link(nc.vector.tensor_tensor(off_f[:, :], tile_s[:, :], prev_f[:, :], ALU.subtract))
                link(nc.vector.scalar_tensor_tensor(row_f[:, :], exp_f[:, :], float(CAP), off_f[:, :], ALU.mult, ALU.add))
                link(nc.vector.tensor_scalar(over_f[:, :], exp_f[:, :], float(E), float(DUMMY), ALU.is_ge, ALU.mult))
                link(nc.vector.scalar_tensor_tensor(row2_f[:, :], row_f[:, :], start, over_f[:, :], ALU.add, ALU.add))
                link(nc.vector.tensor_scalar(table_row[:, g:g + 1], row2_f[:, :], float(DUMMY), 1.0 / P, ALU.min, ALU.mult))
                link(nc.vector.tensor_scalar(expc_f[:, g:g + 1], exp_f[:, :], float(E - 1), None, ALU.min))
                ex = expert_all[:, g * TILES_B:(g + 1) * TILES_B, :].rearrange("p n k -> p (n k)")
                sl = dest_all[:, g * TILES_B:(g + 1) * TILES_B, :].rearrange("p n k -> p (n k)")
                rw = row_all[:, g * TILES_B:(g + 1) * TILES_B, :].rearrange("p n k -> p (n k)")
                wide = [P, 2 * TILES_B, E]
                link(nc.vector.tensor_tensor(before_e[:, :], cum[:, :], length[:, :], ALU.subtract))
                link(nc.vector.scalar_tensor_tensor(shift_e[:, :], before_e[:, :], -start, base0[:, :], ALU.add, ALU.subtract))
                link(nc.vector.tensor_tensor(plan_big[0], iota_f[:, 0, 0, :].unsqueeze(1).broadcast_to(wide),
                                             ex.unsqueeze(2).broadcast_to(wide), ALU.is_equal))
                link(nc.vector.tensor_tensor(plan_big[1], plan_big[0], shift_e[:, :].unsqueeze(1).broadcast_to(wide), ALU.mult))
                link(nc.vector.tensor_reduce(shift_t[:, :], plan_big[1], AX.X, ALU.add))
                link(nc.vector.tensor_tensor(rw, sl, shift_t[:, :], ALU.add))

            def add_attention(b):
                for t in range(TPB):
                    ge(dve, o_done, 2 * b.n + t + 1)
                    if t == 0:
                        ge(dve, z_ready, 2 * b.n)
                        last = b + (-1)
                        if last.within(NB):
                            ge(dve, x1_stored[last.p], 16 * (last.j + 1))
                    nc.vector.scalar_tensor_tensor(x1[:, t, :], ps_out[t][:, :], 0.0, xin[:, b.p, t, :],
                                                   ALU.max, ALU.add).then_inc(x1_ready, 1)

            class Norm:

                def __init__(self, b, src, st, mv, ve, nmr, rstd, s, rstd_ready, nmr_ready, used):
                    self.b, self.src, self.st, self.mv, self.ve, self.nmr, self.rstd = b, src, st, mv, ve, nmr, rstd
                    self.s, self.rstd_ready, self.nmr_ready, self.used = s, rstd_ready, nmr_ready, used

                def sums(self, t):
                    nc.vector.bn_stats(self.st[:, t, :], self.src(t)).then_inc(self.s, 1)

                def moments(self, t):
                    ge(dve, self.s, 5 * self.b.n + 2 * t + 1)
                    pass_held(dve, "dve")
                    nc.vector.bn_aggr(self.mv[:, t, :], self.st[:, t, :]).then_inc(self.s, 1)

                def variance(self):
                    ge(dve, self.s, 5 * self.b.n + 4)
                    nc.vector.tensor_scalar(self.ve[:, :], self.mv[:, :, 1], EPS, None, ALU.add).then_inc(self.s, 1)

                def shift(self):
                    ge(dve, self.rstd_ready, self.b.n + 1)
                    ge(dve, self.used, 2 * self.b.n)
                    nc.vector.scalar_tensor_tensor(self.nmr[:, :], self.mv[:, :, 0], -1.0, self.rstd[:, :],
                                                   ALU.mult, ALU.mult).then_inc(self.nmr_ready, 1)

            class Choose:

                def __init__(self, b):
                    self.b, self.n = b, ROUTE_STEPS * b.n

                def logits(self):
                    ge(dve, logit_turned, self.b.n + 1)
                    nc.vector.tensor_copy(logit[:, :, :], ps_logit).then_inc(route, 1)

                def values(self):
                    ge(dve, route, self.n + 1)
                    pass_held(dve, "dve")
                    for t in range(TPB):
                        nc.vector.max(top_v[:, t, :], logit[:, t, :]).then_inc(route, 1)

                def indices(self):
                    ge(dve, route, self.n + 3)
                    pass_held(dve, "dve")
                    for t in range(TPB):
                        nc.vector.max_index(top_i[:, t, :], top_v[:, t, :], logit[:, t, :]).then_inc(route, 1)

                def floats(self):
                    b = self.b
                    gap = gap_all[:, 2 * b.n:2 * b.n + 2] if isinstance(b.j, int) else gap_all[:, bass.ds(b.n * 2, 2)]
                    nc.vector.tensor_tensor(gap, top_v[:, :, 1], top_v[:, :, 0], ALU.subtract).then_inc(route, 1)
                    ge(dve, route, self.n + 5)
                    nc.vector.tensor_copy(top_f[:, :, :], top_i[:, :, 0:2]).then_inc(route, 1)

                def one_hot(self):
                    ge(dve, route, self.n + 7)
                    nc.vector.tensor_tensor(onehot[:, :, :, :], iota_f[:, :, :, :],
                                            top_f[:, :, :].unsqueeze(3).broadcast_to([P, TPB, 2, E]),
                                            ALU.is_equal).then_inc(route, 1)

                def both(self):
                    b = self.b
                    ge(dve, route, self.n + 8)
                    ge(dve, rank_done, b.n)
                    nc.vector.tensor_tensor(chosen[:, :, :], onehot[:, :, 0, :], onehot[:, :, 1, :], ALU.add).then_inc(route, 1)
                    ea = (expert_all[:, 2 * b.n:2 * b.n + 2, :] if isinstance(b.j, int)
                          else expert_all[:, bass.ds(b.n * 2, 2), :])
                    nc.vector.tensor_copy(ea, top_f[:, :, :]).then_inc(route, 1)

            class Place:

                def __init__(self, b):
                    self.b, self.n = b, PLACE_STEPS * b.n

                def ranks(self):
                    ge(dve, rank_done, self.b.n + 1)
                    nc.vector.tensor_tensor(pos[:, :, :], ps_pos, base[:, :].unsqueeze(1).broadcast_to([P, TPB, E]),
                                            ALU.add).then_inc(place, 1)

                def picked(self):
                    ge(dve, place, self.n + 1)
                    nc.vector.tensor_tensor(posk[:, :, :, :], onehot[:, :, :, :],
                                            pos[:, :, :].unsqueeze(2).broadcast_to([P, TPB, 2, E]), ALU.mult).then_inc(place, 1)
                    nc.vector.tensor_tensor(base[:, :], base[:, :], ps_tot, ALU.add).then_inc(place, 1)

                def slots(self):
                    ge(dve, place, self.n + 3)
                    nc.vector.tensor_reduce(destf[:, :, :], posk[:, :, :, :], AX.X, ALU.add).then_inc(place, 1)

                def write(self):
                    b, n = self.b, self.n
                    ge(dve, place, n + 4)
                    if (b + (-2)).within(NB):
                        ge(dve, token_scattered[b.p], 16 * 4 * b.j)
                    nc.vector.tensor_copy(dest[:, b.p, :, :], destf[:, :, :]).then_inc(place, 1)
                    da = (dest_all[:, 2 * b.n:2 * b.n + 2, :] if isinstance(b.j, int)
                          else dest_all[:, bass.ds(b.n * 2, 2), :])
                    nc.vector.tensor_copy(da, destf[:, :, :]).then_inc(place, 1)
                    if isinstance(b.j, int) and b.n % NB_G == NB_G - 1:
                        dve.wait_ge(place, n + PLACE_STEPS)
                        dve.wait_ge(route, ROUTE_STEPS * (b.n + 1))
                        make_plan(b.n // NB_G)
                        if b.n == NB_G - 1:
                            nc.vector.tensor_scalar(base[:, :], base0[:, :], float(E * CAP), None, ALU.add).then_inc(regroup, 1)
                            dve.wait_ge(regroup, 1)

            def body(b, batch):
                nxt, prv, old = b + 1, b + (-1), b + (-2)
                b_in, nxt_in, prv_in, old_in = (s.within(NB) for s in (b, nxt, prv, old))
                norm2 = Norm(prv, lambda t: x1[:, t, :], st2, mv2, ve2, nmr2, rstd2, stats2, rstd2_ready, nmr2_ready, z_ready)
                norm1 = Norm(nxt, lambda t: xin[:, nxt.p, t, :], st1, mv1, ve1, nmr1, rstd1, stats1, rstd1_ready,
                             nmr1_ready, xn_ready)
                choose, put = Choose(old), Place(old)

                def low(m):
                    ge(dve, qp_hi, 4 * b.n + m + 1)
                    ge(dve, s_done, b.n)
                    sub(qpT[:, LO, m, :], tq[:, m % 2, :], qpT[:, HI, m, :], qp_lo)

                if prv_in:
                    add_attention(prv)
                if old_in:
                    choose.logits()
                if prv_in:
                    ge(dve, rstd2_ready, prv.n)
                    ge(dve, x1_ready, 2 * prv.n + 1)
                    norm2.sums(0)
                if old_in:
                    choose.values()
                if prv_in:
                    norm2.moments(0)
                    ge(dve, x1_ready, 2 * prv.n + 2)
                    norm2.sums(1)
                if old_in:
                    choose.indices()
                if prv_in:
                    norm2.moments(1)
                if b_in:
                    low(0)
                if prv_in:
                    norm2.variance()
                if old_in:
                    choose.floats()
                if nxt_in:
                    ge(dve, x_loaded[nxt.p], 16 * (nxt.j + 1))
                    ge(dve, rstd1_ready, nxt.n)
                    norm1.sums(0)
                if old_in:
                    choose.one_hot()
                if nxt_in:
                    norm1.moments(0)
                if prv_in:
                    norm2.shift()
                if b_in:
                    low(1)
                if old_in:
                    choose.both()
                if nxt_in:
                    norm1.sums(1)
                if b_in:
                    low(2)
                if nxt_in:
                    norm1.moments(1)
                if old_in:
                    put.ranks()
                if nxt_in:
                    norm1.variance()
                if b_in:
                    low(3)
                if old_in:
                    put.picked()
                if nxt_in:
                    norm1.shift()
                if isinstance(b.j, int) and b.n == -1:
                    setup_splits()
                if old_in:
                    put.slots()
                    put.write()
                if b_in:
                    n = 3 * b.n
                    ge(dve, s_relu, b.n + 1)
                    nc.vector.tensor_tensor(lg[:, :], tl[:, :], ps_mask, ALU.add).then_inc(lg_step, 1)
                    ge(dve, lg_step, n + 1)
                    ge(dve, o_done, 2 * b.n)
                    nc.vector.tensor_copy(lgT[:, HI, :], lg[:, :]).then_inc(lg_step, 1)
                    ge(dve, lg_step, n + 2)
                    sub(lgT[:, LO, :], lg[:, :], lgT[:, HI, :], lg_step)
                if nxt_in:
                    for t in range(TPB):
                        ge(dve, qT_hi, 2 * nxt.n + t + 1)
                        ge(dve, q_done, 4 * nxt.n)
                        sub(qT[:, LO, :, t * P:(t + 1) * P], psT[t][:, :].rearrange("p (c k) -> p c k", c=DC),
                            qT[:, HI, :, t * P:(t + 1) * P], qT_lo)

            block_steps(dve, body)
            dve.wait_ge(gap_exp, 1)
            nc.vector.tensor_scalar(den_all[:, :], e_all[:, :], 1.0, None, ALU.add).then_inc(weight, 1)
            dve.wait_ge(weight, 1)
            nc.vector.reciprocal(w_all[:, 0, :], den_all[:, :]).then_inc(weight, 1)
            dve.wait_ge(weight, 2)
            nc.vector.tensor_tensor(w_all[:, 1, :], e_all[:, :], w_all[:, 0, :], ALU.mult).then_inc(weight, 1)
            dve.wait_ge(weight, 3)

            def turned_g(t):
                ge(dve, gT_hi, t.n + 1)
                ge(dve, uv_done, t.n - 1)
                sub(zgT[t.p][:, :, P:2 * P], psT[t.p][:, :].rearrange("p (c k) -> p c k", c=DC),
                    zgT[t.p][:, :, 0:P], gT_lo)

            def take_idx(n, q):
                if isinstance(n, int):
                    src = row_all[:, n, :]
                else:
                    src = row_all[:, bass.ds(n, 1), :].rearrange("p n k -> p (n k)")
                nc.vector.tensor_copy(cidx[:, q, :], src).then_inc(cidx_ready, 1)

            def combine(n, q, k):
                w = [w_all[:, j, bass.ds(n, 1)] for j in range(2)]
                ge(dve, xg_loaded[q], 16 * (k + 1))
                ge(dve, y1_gathered[q], 16 * (k + 1))
                nc.vector.scalar_tensor_tensor(y1g[q], y1g[q], w[0], xg[q], ALU.mult, ALU.add).then_inc(comb1, 1)
                ge(dve, y2_gathered[q], 16 * (k + 1))
                ge(dve, comb1, n + 1)
                nc.vector.scalar_tensor_tensor(xg[q], y2g[q], w[1], y1g[q], ALU.mult, ALU.add).then_inc(comb2, 1)

            def make_sched(g):
                dve.wait_ge(rows_gathered, 16 * (g + 1))
                nc.vector.tensor_copy(slot_rows_f[0:TILES_G, :], slot_rows[0:TILES_G, :]).then_inc(rows_float, 1)

            def keep_sched(g):
                dve.wait_ge(rows_turned, g + 1)
                nc.vector.tensor_copy(idx_all[g][:, :], psG[:, 0:TILES_G]).then_inc(sched_ready, 1)
                nc.vector.tensor_copy(sched_exp[:, g * TILES_G:(g + 1) * TILES_G], psG[0:1, P:P + TILES_G]).then_inc(sched_ready, 1)

            make_sched(0)
            keep_sched(0)
            turned_g(Step(0, 0))

            def tile_body(t, comb):
                if isinstance(t.j, int) and t.n == 0:
                    make_sched(1)
                if isinstance(t.j, int) and t.n == 1:
                    keep_sched(1)
                if comb is not None:
                    i, q = comb
                    take_idx(2 * i + q, q)
                ge(dve, silu_done, t.n + 1)
                ge(dve, s_turned, t.n - 1)
                nc.vector.tensor_tensor(s_tok[:, t.p, :], sil[:, t.p, :], psQ[t.p][:, R:2 * R], ALU.mult).then_inc(s_ready, 1)
                if (t + 1).within(TILES):
                    turned_g(t + 1)
                ge(dve, sT_hi, t.n + 1)
                ge(dve, y_done, t.n - 1)
                sub(sT[t.p][:, LO, :], psST[:, 0:P], sT[t.p][:, HI, :], sT_lo)
                if comb is not None:
                    combine(2 * i + q, q, i)

            tile_steps(dve, tile_body)
            with dve.Fori(0, TILES_B // 4) as i:
                for q in range(4):
                    take_idx(TILES_B + 4 * i + q, q)
                for q in range(4):
                    combine(TILES_B + 4 * i + q, q, i + used(q))

        @block.tensor
        def _(pe):
            def turn(o, i, n=P):
                return pe.transpose(o, i, ident[0:n, 0:n])

            def three(o, w, a, first, last):
                pe.matmul(o, w[LO], a[HI], start=first, stop=False)
                pe.matmul(o, w[HI], a[LO], start=False, stop=False)
                return pe.matmul(o, w[HI], a[HI], start=False, stop=last)

            pe.wait_ge(const_ready, 10)
            pe.wait_ge(w_loaded["ctx"], 16)
            for g in range(NBATCH):
                for c in range(DC):
                    ins = turn(psT[g][:, c * P:(c + 1) * P], ctx_raw[:, g, c * P:(c + 1) * P])
                ins.then_inc(ctx_turned, 1)
            pe.wait_ge(ctxT_ready, 2)
            pe.wait_ge(w_loaded["wk0"], 16)
            pe.wait_ge(w_loaded["wk1"], 16)
            for m in range(DC):
                ge(pe, k_relu, m - 1)
                for c in range(DC):
                    w = z if c < 2 else x1
                    ins = pe.matmul(psQ[m % 2][:, 0:BT], w[:, c % 2, m * P:(m + 1) * P],
                                    ctxT[:, c, :], start=(c == 0), stop=(c == DC - 1))
                ins.then_inc(k_done, 1)
            pe.wait_ge(w_loaded["wv"], 32)
            pe.wait_ge(w_loaded["small"], 64)
            for g in range(NBATCH):
                pe.matmul(ps_out[g][:, :], ones_row[:, :], bv_sb[:, :], start=True, stop=False)
                for c in range(DC):
                    w = stage[:, c * D:(c + 1) * D] if c < 3 else tq[:, :, :].rearrange("p a t -> p (a t)")
                    ins = pe.matmul(ps_out[g][:, :], ctxT[:, c, g * KEYS:(g + 1) * KEYS], w, start=False, stop=(c == DC - 1))
                ins.then_inc(v_done, 1)

            def queries(b):
                ge(pe, qT_lo, 2 * b.n + 2)
                if isinstance(b.j, int) and b.n == 0:
                    pe.wait_ge(wq_ready, DC)
                    pe.wait_ge(k_relu, DC)
                for m in range(DC):
                    ge(pe, qp_relu, 4 * b.n + m - 1)
                    for c in range(DC):
                        ins = three(psQ[m % 2][:, 0:BT],
                                    [wq[:, h, c, m * P:(m + 1) * P] for h in range(2)],
                                    [qT[:, h, c, :] for h in range(2)], c == 0, c == DC - 1)
                    ins.then_inc(q_done, 1)

            def ranks(b):
                ge(pe, route, ROUTE_STEPS * b.n + 9)
                ge(pe, place, PLACE_STEPS * (b.n - 1) + 3)
                for t in range(TPB):
                    for u in range(t):
                        pe.matmul(ps_pos[:, t, :], ones[:, :], chosen[:, u, :], start=(u == 0), stop=False)
                    pe.matmul(ps_pos[:, t, :], before[:, :], chosen[:, t, :], start=(t == 0), stop=True)
                for t in range(TPB):
                    ins = pe.matmul(ps_tot, ones[:, :], chosen[:, t, :], start=(t == 0), stop=(t == TPB - 1))
                ins.then_inc(rank_done, 1)

            def turn_z(b, t):
                ge(pe, z_ready, 2 * b.n + t + 1)
                ge(pe, zT_ready, 2 * b.n + t)
                for c in range(DC):
                    ins = turn(psZ[:, c * P:(c + 1) * P], z[:, t, c * P:(c + 1) * P])
                ins.then_inc(z_turned, 1)

            def scores(b, batch):
                ge(pe, m_loaded[b.p], 16 * (b.j + 1))
                ge(pe, x1_ready, 2 * b.n)
                if isinstance(b.j, int) and b.n == 0:
                    pe.wait_ge(k_lo, DC)
                    pe.wait_ge(v_relu, 2)
                for t in range(TPB):
                    turn(ps_mask[:, t * P:(t + 1) * P], mraw[:, b.p, t, :])
                ge(pe, qp_lo, 4 * b.n + 4)
                for c in range(DC):
                    ins = three(psS[:, 0:BT], [kpT[:, h, c, batch * KEYS:(batch + 1) * KEYS] for h in range(2)],
                                [qpT[:, h, c, :] for h in range(2)], c == 0, c == DC - 1)
                ins.then_inc(s_done, 1)

            def turn_x(b):
                ge(pe, xn_ready, 2 * b.n + 2)
                ge(pe, qT_lo, 2 * b.n)
                for t in range(TPB):
                    for c in range(DC):
                        ins = turn(psT[t][:, c * P:(c + 1) * P], xn[:, t, c * P:(c + 1) * P])
                    ins.then_inc(xn_turned, 1)

            def gates(b):
                ge(pe, zT_ready, 2 * b.n + 2)
                ge(pe, logT_ready, b.n)
                ge(pe, place, PLACE_STEPS * (b.n - 1) + 3)
                for c in range(DC):
                    ins = pe.matmul(ps_log, gw[:, c, :], zT[:, c, :], start=(c == 0), stop=(c == DC - 1))
                ins.then_inc(gate_done, 1)

            def attend(b, batch):
                ge(pe, lg_step, 3 * b.n + 3)
                ge(pe, x1_ready, 2 * b.n)
                if isinstance(b.j, int) and b.n == 0:
                    pe.wait_ge(v_lo, 2)
                for t in range(TPB):
                    three(ps_out[t][:, :], [lgT[:, h, t * P:(t + 1) * P] for h in range(2)],
                          [vp[:, h, batch, :] for h in range(2)], True, True).then_inc(o_done, 1)

            def turn_logits(b):
                ge(pe, logT_ready, b.n + 1)
                ge(pe, route, ROUTE_STEPS * (b.n - 1) + 1)
                pass_held(pe, "pe")
                for t in range(TPB):
                    ins = turn(ps_logit[:, t, :], logT[:, t * P:(t + 1) * P], E)
                ins.then_inc(logit_turned, 1)

            def body(b, batch):
                nxt, prv, old = b + 1, b + (-1), b + (-2)
                if b.within(NB):
                    queries(b)
                if old.within(NB):
                    ranks(old)
                if prv.within(NB):
                    turn_z(prv, 0)
                if b.within(NB):
                    scores(b, batch)
                if prv.within(NB):
                    turn_z(prv, 1)
                if nxt.within(NB):
                    turn_x(nxt)
                if prv.within(NB):
                    gates(prv)
                if b.within(NB):
                    attend(b, batch)
                if prv.within(NB):
                    turn_logits(prv)

            block_steps(pe, body)

            def turn_g(t):
                ge(pe, z_gathered[t.p], 16 * (t.j + 1))
                ge(pe, gT_lo, t.n - 1)
                for c in range(DC):
                    ins = turn(psT[t.p][:, c * P:(c + 1) * P], zg[t.p][:, c * P:(c + 1) * P])
                ins.then_inc(g_turned, 1)

            def expert(t):
                return pe.value_load(sched_exp[0:1, bass.ds(t.n, 1)], min_val=0, max_val=E - 1)

            def up(t):
                e = expert(t)
                ge(pe, gT_lo, t.n + 1)
                ge(pe, s_ready, t.n - 1)
                for c in range(DC):
                    w = [wuv[:, bass.ds(e, 1), h, 2 * R * c:2 * R * (c + 1)].rearrange("p e n -> p (e n)") for h in range(2)]
                    a = [zgT[t.p][:, c, h * P:(h + 1) * P] for h in range(2)]
                    ins = three(psQ[t.p][:, 0:2 * R], a, w, c == 0, c == DC - 1)
                ins.then_inc(uv_done, 1)

            def down(t):
                e = expert(t)
                ge(pe, sT_lo, t.n + 1)
                ge(pe, y_ready, t.n - 1)
                w = [wo[:, bass.ds(e, 1), h, :].rearrange("p e n -> p (e n)") for h in range(2)]
                three(ps_out[t.p][:, :], [sT[t.p][:, h, :] for h in range(2)], w, True, True).then_inc(y_done, 1)

            def turn_s(t):
                ge(pe, s_ready, t.n + 1)
                ge(pe, sT_lo, t.n - 1)
                turn(psST[:, 0:P], s_tok[:, t.p, :]).then_inc(s_turned, 1)

            pe.wait_ge(place, PLACE_STEPS * NB)
            pe.wait_ge(stage_lo, 3 * E)
            pe.wait_ge(x1_ready, 2 * NB)

            def turn_sched(g):
                pe.wait_ge(rows_float, g + 1)
                pe.wait_ge(plan, PLAN_STEPS * g + SCHED_STEPS)
                ge(pe, sched_ready, 2 * g)
                turn(psG[:, 0:TILES_G], slot_rows_f[0:TILES_G, :], TILES_G)
                turn(psG[0:1, P:2 * P], expc_f[:, g:g + 1]).then_inc(rows_turned, 1)

            turn_sched(0)
            pe.wait_ge(sched_ready, 2)
            turn_g(Step(0, 0))

            def tile_body(t):
                up(t)
                if (t + 1).within(TILES):
                    turn_g(t + 1)
                if (t + (-1)).within(TILES):
                    down(t + (-1))
                turn_s(t)

            tile_body(Step(0, 0))
            turn_sched(1)
            tile_body(Step(0, 1))
            pe.wait_ge(sched_ready, 4)
            with pe.Fori(1, TILES // 2 - 1) as i:
                for p in range(2):
                    tile_body(Step(i, p))
            tile_body(Step(TILES // 2 - 1, 0))
            tile_body(Step(TILES // 2 - 1, 1))
            down(Step(TILES // 2 - 1, 1))


_INS = ['x', 'ctx_1024', 'mask_1xSxS2_ff0', 'L0_xattn_kernel_q', 'L0_xattn_kernel_k', 'L0_xattn_kernel_v',
        'L0_xattn_bias_q', 'L0_xattn_bias_k', 'L0_xattn_bias_v', 'L0_ffn_gate_w', 'L0_ffn_Wu', 'L0_ffn_Wv', 'L0_ffn_Wo']
_OUTS = [((NBATCH, SEQ, D), 'float32')]


def kernel(**inputs):
    import numpy as _np
    import concourse.bacc as _bacc
    from concourse import mybir as _mybir
    from concourse.bass_utils import run_bass_kernel_spmd as _run

    nc = _bacc.Bacc("TRN2", target_bir_lowering=False, num_devices=1)
    arrays, args = {}, []
    for name in _INS:
        a = _np.ascontiguousarray(inputs[name])
        arrays[f"in_{name}_dram"] = a
        args.append(nc.dram_tensor(f"in_{name}_dram", a.shape, _mybir.dt.from_np(a.dtype), kind="ExternalInput").ap())
    for i, (shape, dtype) in enumerate(_OUTS):
        dt = _mybir.dt.from_np(_np.dtype(dtype))
        args.append(nc.dram_tensor(f"out_{i}_dram", shape, dt, kind="ExternalOutput").ap())
    moe_block(nc, *args)
    r = _run(nc, [arrays], core_ids=[0])
    return r.results[0]["out_0_dram"]
```

```python
import numpy as np
import concourse.bass as bass
from concourse import mybir
from contextlib import ExitStack

F32 = mybir.dt.float32
F32R = mybir.dt.float32r
BF16 = mybir.dt.bfloat16
I32 = mybir.dt.int32
U32 = mybir.dt.uint32
ALU = mybir.AluOpType
ACT = mybir.ActivationFunctionType
AX = mybir.AxisListType

P = 128
LOG_P = 7
D = 512
DC = D // P
NBATCH, SEQ = 2, 2048
KEYS = 128
E, R = 8, 128
TOK = NBATCH * SEQ
TPB = 2
BT = TPB * P
NB = TOK // BT
NB_G = NB // NBATCH
NTILE = TOK // P
TILES_B = SEQ // P
CAP = SEQ
DUMMY = E * CAP
NSLOT = DUMMY + P
TILES_G = 2 * SEQ // P + E - 1
TILES = NBATCH * TILES_G
SHARED = 3
SCALE = float(np.float32(1.0) / np.sqrt(np.float32(D)))
EPS = 1e-5
HI, LO = 0, 1


def ge(eng, sem, value):
    if isinstance(value, int) and value <= 0:
        return
    eng.wait_ge(sem, value)


class Step:

    def __init__(self, j, p):
        self.j, self.p = j, p

    @property
    def n(self):
        return 2 * self.j + self.p

    def __add__(self, k):
        q = self.p + k
        return Step(self.j + q // 2, q % 2)

    def within(self, count):
        return not isinstance(self.j, int) or 0 <= self.n < count


def block_steps(eng, body):
    def straight(a, b):
        for n in range(a, b):
            body(Step(n // 2, n % 2), min(max(n // NB_G, 0), 1))

    def looped(a, b, batch):
        with eng.Fori(0, (b - a) // 2) as i:
            for p in range(2):
                body(Step(i, a % 2) + (2 * (a // 2) + p), batch)

    straight(0, 4)
    looped(4, NB_G, 0)
    straight(NB_G, NB_G + 3)
    looped(NB_G + 3, NB - 1, 1)
    straight(NB - 1, NB)


class Tile:

    def __init__(self, j, p):
        self.j, self.p, self.r = j, p, p % 2

    @property
    def n(self):
        return 4 * self.j + self.p

    @property
    def pair(self):
        return 2 * self.j + self.p // 2

    def __add__(self, k):
        q = self.p + k
        return Tile(self.j + q // 4, q % 4)

    def within(self, count):
        return not isinstance(self.j, int) or 0 <= self.n < count


def tile_steps(eng, body, fours=1, enter=None):
    def straight(a, b):
        if enter and a < b:
            enter()
        for n in range(a, b):
            body(Tile(n // 4, n % 4), None, n // TILES_G)

    def looped(a, b, batch):
        with eng.Fori(0, (b - a) // fours) as i:
            if enter:
                enter()
            for p in range(4 * fours):
                k = i * fours + p // 4
                body(Tile(k + a, p % 4), k if batch else None, batch)

    full = TILES_G // 4 + 1
    begin = full + 1
    comb = SEQ // P // 2
    last = full - 1 if fours == 1 else full
    straight(SHARED, 16)
    looped(4, last, 0)
    straight(4 * last, 4 * begin)
    looped(begin, begin + comb - fours, 1)
    for k in range(comb - fours, comb):
        if enter:
            enter()
        for p in range(4):
            body(Tile(k + begin, p), k, 1)
    straight(4 * (begin + comb), TILES)


def moe_block(nc, x, ctx_in, mask, kq, kk, kv, bq, bk, bv, gate_w, Wu, Wv, Wo, out):
    ctx = ExitStack()
    with ctx:
        def sb(name, shape, dt=F32):
            return ctx.enter_context(nc.sbuf_tensor(name, shape, dt))

        def bank(name):
            return ctx.enter_context(nc.psum_tensor(name, [P, 512], F32))

        def sem(name):
            return ctx.enter_context(nc.semaphore(name))

        def pair(name):
            return [sem(f"{name}{i}") for i in range(2)]

        def dram(name, shape, dt=F32):
            return nc.dram_tensor(name, shape, dt, kind="Internal").ap()

        z_dram = [dram(f"z_dram{g}", [SEQ, D]) for g in range(NBATCH)]
        x1_dram = dram("x1_dram", [TOK, D])
        y_dram = [dram(f"y_dram{g}", [TILES_G * P, D]) for g in range(NBATCH)]
        slot_token = [dram(f"slot_token{g}", [NSLOT, 1], I32) for g in range(NBATCH)]

        wq = sb("wq", [P, 2, DC, D], F32R)
        wuv = sb("wuv", [P, E, 2, DC * 2 * R], F32R)
        wo = sb("wo", [P, E, 2, D], F32R)
        kpT = sb("kpT", [P, 2, DC, NBATCH * KEYS], F32R)
        vp = sb("vp", [P, 2, NBATCH, D], F32R)
        qT = sb("qT", [P, 2, DC, BT], F32R)
        qpT = sb("qpT", [P, 2, DC, BT], F32R)
        lgT = sb("lgT", [P, 2, BT], F32R)
        zgT = [qT[:, h, :, :] for h in range(2)]
        sT = [lgT[:, i, :].rearrange("p (h t) -> p h t", h=2) for i in range(2)]
        xin = sb("xin", [P, 2, TPB, D])
        x1 = sb("x1", [P, TPB, D])
        xn = sb("xn", [P, TPB, D])
        z = sb("z", [P, TPB, D])
        zT_ctxT = sb("zT_ctxT", [P, 2, DC, BT])
        zT, ctxT = zT_ctxT[:, 0, :, :], zT_ctxT[:, 1, :, :]
        stage = sb("stage", [P, 3 * D])
        tq = sb("tq", [P, 2, BT])
        wraw = sb("wraw", [P, 4 * D])
        mraw = sb("mraw", [P, 2, TPB, KEYS])
        tl = sb("tl", [P, BT])
        lg = sb("lg", [P, BT])
        gate_work = sb("gate_work", [P, 2, 2, R])
        sil, s_tok = gate_work[:, 0, :, :], gate_work[:, 1, :, :]
        zeros_i = gate_work[:, :, :, :].rearrange("p a b r -> p (a b r)")[:, 0:NSLOT // P].bitcast(I32)
        wk_raw = z[:, :, :].rearrange("p t d -> p (t d)")
        zg = [xn[:, i, :] for i in range(2)] + [stage[:, i * D:(i + 1) * D] for i in range(2)]
        ysb = [xin[:, i // 2, i % 2, :] for i in range(4)]
        plan_big = [wraw[:, (2 + i) * D:(2 + i) * D + 2 * TILES_B * E].rearrange("p (n e) -> p n e", e=E) for i in range(2)]
        y1g = [wraw[:, i * D:(i + 1) * D] for i in range(2)] + [xin[:, 0, i, :] for i in range(2)]
        y2g = [wraw[:, (2 + i) * D:(3 + i) * D] for i in range(2)] + [xin[:, 1, i, :] for i in range(2)]
        xg = [x1[:, i, :] for i in range(2)] + [z[:, i, :] for i in range(2)]
        def as_tiles(part):
            return part.rearrange("p a b k -> p (a b k)").rearrange("p (n d) -> p n d", d=D)

        x1_first = as_tiles(wq[:, :, :, :]).bitcast(F32)
        x1_kept = [as_tiles(qpT[:, :, :, :]).bitcast(F32), as_tiles(kpT[:, :, :, :]).bitcast(F32),
                   as_tiles(vp[:, :, :, :]).bitcast(F32), as_tiles(zT_ctxT[:, :, :, :])]
        ctx_raw = zT[:, :, :].rearrange("p c t -> p (c t)").rearrange("p (b d) -> p b d", b=NBATCH)
        ident = sb("ident", [P, P])
        before = sb("before", [P, P], BF16)
        ones = sb("ones", [P, P], BF16)
        ones_row = sb("ones_row", [1, P])
        gw = sb("gw", [P, DC, E])
        bq_sb = sb("bq_sb", [P, DC])
        bk_sb = sb("bk_sb", [P, DC])
        bv_sb = sb("bv_sb", [1, D])
        st1 = sb("st1", [P, TPB, 6])
        mv1 = sb("mv1", [P, TPB, 2])
        rstd1 = sb("rstd1", [P, TPB])
        st2 = sb("st2", [P, TPB, 6])
        mv2 = sb("mv2", [P, TPB, 2])
        rstd2 = sb("rstd2", [P, TPB])
        nmr1 = sb("nmr1", [P, TPB])
        nmr2 = sb("nmr2", [P, TPB])
        ve1 = sb("ve1", [P, TPB])
        ve2 = sb("ve2", [P, TPB])
        minus_half = sb("minus_half", [P, TPB])
        logT = sb("logT", [E, BT])
        logit = sb("logit", [P, TPB, E])
        top_v = sb("top_v", [P, TPB, 8])
        top_i = sb("top_i", [P, TPB, 8], U32)
        top_f = sb("top_f", [P, TPB, 2])
        iota_i = sb("iota_i", [P, TPB, 2, E], I32)
        iota_f = sb("iota_f", [P, TPB, 2, E])
        onehot = sb("onehot", [P, TPB, 2, E])
        chosen = sb("chosen", [P, TPB, E], BF16)
        base_i = sb("base_i", [P, E], I32)
        base0 = sb("base0", [P, E])
        base = sb("base", [P, E])
        pos = sb("pos", [P, TPB, E])
        posk = sb("posk", [P, TPB, 2, E])
        destf = sb("destf", [P, TPB, 2])
        dest = sb("dest", [P, 2, TPB, 2], U32)
        dest_all = sb("dest_all", [P, NTILE, 2])
        expert_all = sb("expert_all", [P, NTILE, 2])
        row_all = sb("row_all", [P, NTILE, 2], U32)
        before_e = sb("before_e", [P, E])
        shift_e = sb("shift_e", [P, E])
        shift_t = sb("shift_t", [P, TILES_B * 2])
        cidx = sb("cidx", [P, 4, 2], U32)
        gap_all = sb("gap_all", [P, NTILE])
        e_all = sb("e_all", [P, NTILE])
        den_all = sb("den_all", [P, NTILE])
        w_all = sb("w_all", [P, 2, NTILE])
        tokid = sb("tokid", [P, 2, TPB], I32)
        upto_e = sb("upto_e", [P, E, E])
        tile_i = sb("tile_i", [P, 1], I32)
        tile_s = sb("tile_s", [P, 1])
        cnt = sb("cnt", [P, E])
        cnt_i = sb("cnt_i", [P, E], I32)
        len_i = sb("len_i", [P, E], I32)
        length = sb("length", [P, E])
        cum = sb("cum", [P, E])
        past = sb("past", [P, E])
        pastc = sb("pastc", [P, E])
        exp_f, prev_f, off_f, row_f, over_f, row2_f = (sb(f"plan{i}", [P, 1]) for i in range(6))
        expc_f = sb("expc_f", [P, NBATCH])
        lens = sb("lens", [P, E, E])
        table_row = sb("table_row", [P, NBATCH], U32)
        slot_rows = sb("slot_rows", [P, P], I32)
        slot_rows_f = sb("slot_rows_f", [P, P])
        idx_all = sb("idx_all", [P, TILES], U32)
        sched_exp = sb("sched_exp", [1, TILES], I32)
        idx = sb("idx", [P, 4], U32)

        psT = [bank(f"psT{i}") for i in range(2)]
        psQ = [bank(f"psQ{i}") for i in range(2)]
        psS = bank("psS")
        psO = bank("psO")
        psZ = bank("psZ")
        psG = bank("psG")
        ps_out = [psO, psS]
        ps_sched = [psT[0], psG]
        ps_mask = psS[:, BT:2 * BT]
        ps_log = psG[0:E, 0:BT]
        ps_logit = psG[:, BT:BT + TPB * E].rearrange("p (t e) -> p t e", e=E)
        ps_pos = psG[:, BT + 32:BT + 32 + TPB * E].rearrange("p (t e) -> p t e", e=E)
        ps_tot = psG[:, BT + 64:BT + 64 + E]
        psST = [psQ[i][:, 2 * R:2 * R + P] for i in range(2)]

        const_ready = sem("const_ready")
        pool_step = sem("pool_step")
        conv_ready = sem("conv_ready")
        w_loaded = {k: sem(f"load_{k}") for k in ("ctx", "wk0", "wk1", "wq", "wv", "small", "table")}
        ctxT_ready = sem("ctxT_ready")
        ctx_turned = sem("ctx_turned")
        wq_hi = sem("wq_hi")
        wq_ready = sem("wq_ready")
        k_done = sem("k_done")
        k_relu = sem("k_relu")
        k_hi = sem("k_hi")
        k_lo = sem("k_lo")
        v_done = sem("v_done")
        v_relu = sem("v_relu")
        v_hi = sem("v_hi")
        v_lo = sem("v_lo")
        x_loaded = pair("x_loaded")
        m_loaded = pair("m_loaded")
        stats1 = sem("stats1")
        rstd1_ready = sem("rstd1_ready")
        xn0_ready = sem("xn0_ready")
        xn1_ready = sem("xn1_ready")
        xn_turned = sem("xn_turned")
        qT_hi = sem("qT_hi")
        qT_lo = sem("qT_lo")
        q_done = sem("q_done")
        qp_relu = sem("qp_relu")
        qp_hi = sem("qp_hi")
        qp_lo = sem("qp_lo")
        s_done = sem("s_done")
        s_relu = sem("s_relu")
        lg_step = sem("lg_step")
        o_done = sem("o_done")
        x1_ready = sem("x1_ready")
        stats2 = sem("stats2")
        rstd2_ready = sem("rstd2_ready")
        nmr2_ready = sem("nmr2_ready")
        z_ready = sem("z_ready")
        x1_stored = pair("x1_stored")
        z_stored = pair("z_stored")
        z_turned = sem("z_turned")
        zT_ready = sem("zT_ready")
        gate_done = sem("gate_done")
        logT_ready = sem("logT_ready")
        logit_turned = sem("logit_turned")
        route = sem("route")
        rank_done = sem("rank_done")
        place = sem("place")
        token_scattered = pair("token_scattered") 
        tokid_moved = sem("tokid_moved")
        stage_loaded = sem("stage_loaded")
        stage_hi = sem("stage_hi")
        stage_lo = sem("stage_lo")
        rows_gathered = sem("rows_gathered")
        rows_float = sem("rows_float")
        rows_turned = sem("rows_turned")
        sched_ready = sem("sched_ready")
        idx_ready = sem("idx_ready")
        nmr1_ready = sem("nmr1_ready")
        regroup = sem("regroup")
        plan = sem("plan")
        gap_exp = sem("gap_exp")
        weight = sem("weight")
        z_gathered = [sem(f"z_gathered{i}") for i in range(4)]
        x1_back = sem("x1_back")
        g_turned = sem("g_turned")
        gT_hi = sem("gT_hi")
        gT_lo = sem("gT_lo")
        uv_done = sem("uv_done")
        silu_done = sem("silu_done")
        s_ready = sem("s_ready")
        s_turned = sem("s_turned")
        sT_hi = sem("sT_hi")
        sT_lo = sem("sT_lo")
        y_done = sem("y_done")
        y_ready = sem("y_ready")
        y_stored = [sem(f"y_stored{i}") for i in range(4)]
        cidx_ready = sem("cidx_ready")
        y1_gathered = [sem(f"y1_gathered{i}") for i in range(4)]
        y2_gathered = [sem(f"y2_gathered{i}") for i in range(4)]
        xg_loaded = [sem(f"xg_loaded{i}") for i in range(4)]
        comb1 = sem("comb1")
        comb2 = sem("comb2")
        out_stored = [sem(f"out_stored{i}") for i in range(4)]
        held = {e: sem(f"held_{e}") for e in ("pool", "dve", "act", "sp", "pe")}

        ROUTE_STEPS, PLACE_STEPS, PLAN_STEPS, SCHED_STEPS = 10, 6, 22, 16

        x_blk = x.rearrange("g (b t p) d -> (g b) p t d", t=TPB, p=P)
        x1_blk = x1_dram.rearrange("(b t p) d -> b p t d", t=TPB, p=P)
        z_blk = [zd.rearrange("(b t p) d -> b p t d", t=TPB, p=P) for zd in z_dram]
        m_blk = mask.rearrange("o (b t p) k -> (o b) p t k", t=TPB, p=P)
        x1_tile = x1_dram.rearrange("(n p) d -> n p d", p=P)
        out_tile = out.rearrange("g (n p) d -> (g n) p d", p=P)
        wu_v = Wu.rearrange("e (c p) r -> e p c r", p=P)
        wv_v = Wv.rearrange("e (c p) r -> e p c r", p=P)
        w_v = {k: w.rearrange("a b (c p) n -> p (a b c) n", p=P) for k, w in (("q", kq), ("k", kk), ("v", kv))}

        def used(q):
            return TILES_B // 2 if q < 2 else 0

        def group_of(b, batch):
            return b.n // NB_G if isinstance(b.j, int) else batch

        def pass_held(eng, name):
            eng.sem_inc(held[name], 1)

        def expert_parts(b):
            def uv(lo, hi):
                if isinstance(b.j, int):
                    return lambda h: wuv[:, b.j, h, lo:hi]
                return lambda h: wuv[:, bass.ds(b.j, 1), h, lo:hi].rearrange("p e n -> p (e n)")

            def o(h):
                if isinstance(b.j, int):
                    return wo[:, b.j, h, :]
                return wo[:, bass.ds(b.j, 1), h, :].rearrange("p e n -> p (e n)")

            cut = 3 * D // 2
            if b.p == 0:
                return [(uv(0, cut), stage[:, 0:cut])]
            return [(uv(cut, 2 * D), stage[:, cut:2 * D]), (o, stage[:, 2 * D:3 * D])]

        block = ctx.enter_context(nc.Block())

        @block.sync
        def _(sp):
            for q in range(4):
                sp.sem_inc(out_stored[q], 16)
                sp.sem_inc(y_stored[q], 16)
            sp.dma_start(ctx_raw, ctx_in.rearrange("b k d -> k b d")).then_inc(w_loaded["ctx"], 16)
            sp.dma_start(wk_raw.rearrange("p (c n) -> p c n", c=2), w_v["k"][:, 0:2, :]).then_inc(w_loaded["wk0"], 16)
            sp.dma_start(x1[:, :, :], w_v["k"][:, 2:4, :]).then_inc(w_loaded["wk1"], 16)
            sp.dma_start(xin[:, 0, :, :], x_blk[0]).then_inc(x_loaded[0], 16)
            with nc.allow_non_contiguous_dma("small biases"):
                sp.dma_start(bq_sb[:, :], bq.rearrange("(m p) -> p m", p=P)).then_inc(w_loaded["small"], 16)
                sp.dma_start(bk_sb[:, :], bk.rearrange("(m p) -> p m", p=P)).then_inc(w_loaded["small"], 16)
                sp.dma_start(gw[:, :, :], gate_w.rearrange("(c p) e -> p c e", p=P)).then_inc(w_loaded["small"], 16)
            sp.dma_start(bv_sb[:, :], bv.rearrange("(a n) -> a n", a=1)).then_inc(w_loaded["small"], 16)
            sp.dma_start(wraw[:, :].rearrange("p (c n) -> p c n", c=DC), w_v["q"]).then_inc(w_loaded["wq"], 16)
            sp.dma_start(stage[:, 0:3 * D].rearrange("p (c n) -> p c n", c=3), w_v["v"][:, 0:3, :]).then_inc(w_loaded["wv"], 16)
            sp.wait_ge(const_ready, 1)
            for g in range(NBATCH):
                sp.dma_start(slot_token[g].rearrange("(p n) o -> p (n o)", p=P), zeros_i).then_inc(w_loaded["table"], 16)
            sp.wait_ge(wq_ready, 1)
            sp.dma_start(wraw[:, 0:D], w_v["v"][:, 3, :]).then_inc(w_loaded["wv"], 16)

            def load_experts(e):
                uv = stage[:, 0:DC * 2 * R].rearrange("p (c h r) -> p c h r", c=DC, h=2)
                sp.dma_start(uv[:, :, 0, :], wu_v[e]).then_inc(stage_loaded, 16)
                sp.dma_start(uv[:, :, 1, :], wv_v[e]).then_inc(stage_loaded, 16)
                sp.dma_start(stage[:, 2 * D:3 * D], Wo[e]).then_inc(stage_loaded, 16)

            def body(b, batch):
                nxt, prv = b + 1, b + (-1)
                if nxt.within(NB):
                    ge(sp, x1_ready, 2 * (nxt.n - 2) + 2)
                    sp.dma_start(xin[:, nxt.p, :, :], x_blk[nxt.n]).then_inc(x_loaded[nxt.p], 16)
                if b.within(NB):
                    ge(sp, s_done, b.n - 1)
                    sp.dma_start(mraw[:, b.p, :, :], m_blk[b.n - batch * NB_G]).then_inc(m_loaded[b.p], 16)
                if prv.within(NB):
                    ge(sp, x1_ready, 2 * prv.n + 2)
                    sp.dma_start(x1_blk[prv.n], x1[:, :, :]).then_inc(x1_stored[prv.p], 16)
                if b.p == 0 and b.within(NB) and not (isinstance(b.j, int) and b.n == 0):
                    ge(sp, stage_lo, 3 * b.j)
                    load_experts(b.j)
                if prv.within(NB):
                    ge(sp, z_ready, 2 * prv.n + 2)
                    g = group_of(prv, batch)
                    sp.dma_start(z_blk[g][prv.n - g * NB_G], z[:, :, :]).then_inc(z_stored[prv.p], 16)
                if isinstance(b.j, int) and b.n == 0:
                    sp.wait_ge(v_done, 2)
                    load_experts(0)

            block_steps(sp, body)
            body(Step(NB // 2, 0), 1)

            def store_out(n, q, k):
                sp.wait_ge(comb2, n + 3)
                sp.dma_start(out_tile[n], xg[q]).then_inc(out_stored[q], 16)

            def load_x1(n, q, k):
                ge(sp, out_stored[q], 16 * (k + 1))
                sp.dma_start(xg[q], x1_tile[n]).then_inc(xg_loaded[q], 16)

            y_tile = [y.rearrange("(n p) d -> n p d", p=P) for y in y_dram]

            def tile_body(t, comb, g):
                if comb is not None and t.p == 1:
                    load_x1(2 * comb + 1, 1, comb)
                if comb is not None and t.p == 3:
                    store_out(2 * comb, 0, comb)
                sp.wait_ge(y_ready, t.n + 1)
                sp.dma_start(y_tile[g][t.n - g * TILES_G], ysb[t.p]).then_inc(y_stored[t.p], 16)
                if comb is not None and t.p == 3:
                    store_out(2 * comb + 1, 1, comb)
                if isinstance(t.j, int) and t.n in x1_parts:
                    k = x1_parts.index(t.n)
                    if k < 2:
                        dst = x1_first[:, 4 * k:4 * (k + 1), :]
                        src = x1_dram[8 * k * P:8 * (k + 1) * P, :].rearrange("(n two p) d -> p n two d", two=2, p=P)[:, :, 0, :]
                    else:
                        n0 = TILES_B + 4 * (k - 2)
                        dst, src = x1_kept[k - 2], x1_tile[n0:n0 + 4].rearrange("n p d -> p n d")
                    sp.dma_start(dst, src).then_inc(x1_back, 16)

            x1_parts = [5, 7, 9, 11, 13, 15]
            for n in range(SHARED):
                tile_body(Tile(0, n), None, 0)
            sp.wait_ge(q_done, 4 * NB)
            sp.wait_ge(s_done, NB)
            sp.wait_ge(o_done, 2 * NB)
            sp.wait_ge(gate_done, NB)
            for q in range(2):
                sp.wait_ge(x1_stored[q], 16 * NB // 2)
            tile_steps(sp, tile_body)
            with sp.Fori(0, 4) as i:
                for q in range(4):
                    sp.wait_ge(comb2, TILES_B + 4 * i + q + 3)
                    sp.dma_start(out_tile[TILES_B + 4 * q + i], xg[q]).then_inc(out_stored[q], 16)
            for q in range(4):
                sp.wait_ge(out_stored[q], 16 * (TILES_B // 4 + used(q) + 1))
                sp.wait_ge(y_stored[q], 16 * ((TILES + 3 - q) // 4 + 1))
            for q in range(2):
                sp.wait_ge(x1_stored[q], 16 * NB // 2)
                sp.wait_ge(z_stored[q], 16 * NB // 2)

        @block.gpsimd
        def _(pool):
            nc.gpsimd.memset(zeros_i, 0).then_inc(const_ready, 1)
            nc.gpsimd.memset(ident[:, :], 0.0).then_inc(pool_step, 1)
            nc.gpsimd.memset(before[:, :], 1.0).then_inc(pool_step, 1)
            nc.gpsimd.memset(upto_e[:, :, :], 1.0).then_inc(pool_step, 1)
            pool.wait_ge(pool_step, 3)
            nc.gpsimd.affine_select(out=ident[:, :], in_=ident[:, :], compare_op=ALU.not_equal, fill=1.0,
                                    base=0, pattern=[[-1, P]], channel_multiplier=1).then_inc(const_ready, 1)
            nc.gpsimd.affine_select(out=before[:, :], in_=before[:, :], compare_op=ALU.is_gt, fill=0.0,
                                    base=0, pattern=[[1, P]], channel_multiplier=-1).then_inc(const_ready, 1)
            nc.gpsimd.affine_select(out=upto_e[:, :, :], in_=upto_e[:, :, :], compare_op=ALU.is_ge, fill=0.0,
                                    base=0, pattern=[[1, E], [-1, E]], channel_multiplier=0).then_inc(const_ready, 1)
            nc.gpsimd.memset(ones[:, :], 1.0).then_inc(const_ready, 1)
            nc.gpsimd.memset(ones_row[:, :], 1.0).then_inc(const_ready, 1)
            nc.gpsimd.memset(minus_half[:, :], -0.5).then_inc(const_ready, 1)
            nc.gpsimd.iota(iota_i[:, :, :, :], [[0, TPB], [0, 2], [1, E]], base=0, channel_multiplier=0).then_inc(const_ready, 1)
            nc.gpsimd.iota(base_i[:, :], [[CAP, E]], base=0, channel_multiplier=0).then_inc(const_ready, 1)
            nc.gpsimd.iota(tile_i[:, :], [[0, 1]], base=0, channel_multiplier=P).then_inc(const_ready, 1)
            for q in range(2):
                nc.gpsimd.iota(tokid[:, q, :], [[P, TPB]], base=q * BT, channel_multiplier=1).then_inc(tokid_moved, 1)

            def gather_rows(g):
                for q in range(2):
                    pool.wait_ge(token_scattered[q], 16 * 4 * NB_G // 2 * (g + 1))
                pool.wait_ge(plan, PLAN_STEPS * g + SCHED_STEPS)
                ge(pool, rows_float, g)
                pool.indirect_dma_start(out=slot_rows[0:TILES_G, :], out_offset=None,
                                        in_=slot_token[g].rearrange("(a b) o -> a (b o)", b=P),
                                        in_offset=bass.IndirectOffsetOnAxis(ap=table_row[0:TILES_G, g:g + 1], axis=0)
                                        ).then_inc(rows_gathered, 16)

            def gather(t, g):
                if not t.within(TILES):
                    return
                ge(pool, g_turned, t.n - 3)
                pass_held(pool, "pool")
                nc.gpsimd.tensor_copy(idx[:, t.p:t.p + 1], idx_all[:, t.n:t.n + 1] if isinstance(t.j, int)
                                      else idx_all[:, bass.ds(t.n, 1)]).then_inc(idx_ready, 1)
                ge(pool, idx_ready, t.n + 1)
                pass_held(pool, "pool")
                pool.indirect_dma_start(out=zg[t.p], out_offset=None, in_=z_dram[g],
                                        in_offset=bass.IndirectOffsetOnAxis(ap=idx[:, t.p:t.p + 1], axis=0)
                                        ).then_inc(z_gathered[t.p], 16)

            def scatter(old, batch, tiles=range(TPB)):
                if isinstance(old.j, int) and old.n == 0:
                    pool.wait_ge(w_loaded["table"], 32)
                g = group_of(old, batch)
                ge(pool, place, PLACE_STEPS * old.n + 5)
                ge(pool, tokid_moved, old.n + 1)
                pass_held(pool, "pool")
                for t in tiles:
                    for k in range(2):
                        pool.indirect_dma_start(
                            out=slot_token[g], out_offset=bass.IndirectOffsetOnAxis(ap=dest[:, old.p, t, k:k + 1], axis=0),
                            in_=tokid[:, old.p, t:t + 1], in_offset=None).then_inc(token_scattered[old.p], 16)

            def move_on(b):
                ge(pool, token_scattered[b.p], 16 * 4 * (b.j + 1))
                pass_held(pool, "pool")
                nc.gpsimd.tensor_scalar(tokid[:, b.p, :], tokid[:, b.p, :], 2 * BT, None, ALU.add).then_inc(tokid_moved, 1)

            def rstd2_of(b):
                ge(pool, stats2, 5 * b.n + 5)
                ge(pool, z_ready, 2 * b.n)
                nc.gpsimd.tensor_tensor(rstd2[:, :], ve2[:, :], minus_half[:, :], ALU.pow).then_inc(rstd2_ready, 1)

            def body(b, batch):
                prv, nxt, old = b + (-1), b + 1, b + (-3)
                if prv.within(NB):
                    rstd2_of(prv)
                if nxt.within(NB):
                    ge(pool, stats1, 5 * nxt.n + 5)
                    ge(pool, xn0_ready, nxt.n)
                    ge(pool, xn1_ready, nxt.n)
                    nc.gpsimd.tensor_tensor(rstd1[:, :], ve1[:, :], minus_half[:, :], ALU.pow).then_inc(rstd1_ready, 1)
                last = isinstance(b.j, int) and b.n == NB - 1
                if last:
                    for q in range(2):
                        pool.wait_ge(z_stored[q], 16 * NB_G // 2)
                    pool.wait_ge(xn_turned, 2 * NB)
                    pool.wait_ge(sched_ready, 2)
                    gather(Tile(0, 0), 0)
                    gather(Tile(0, 1), 0)
                elif old.within(NB):
                    scatter(old, batch)
                if b.within(NB):
                    for n, (dst, src) in enumerate(expert_parts(b)):
                        ge(pool, stage_hi, 3 * b.j + b.p + n + 1)
                        pass_held(pool, "pool")
                        nc.gpsimd.tensor_tensor(dst(LO), src, dst(HI), ALU.subtract).then_inc(stage_lo, 1)
                if last:
                    pool.wait_ge(stage_lo, 3 * E)
                    gather(Tile(0, 2), 0)
                if (b + (-4)).within(NB):
                    move_on(b + (-4))
                if isinstance(b.j, int) and b.n == NB_G + 2:
                    gather_rows(0)

            def gather_tail(n, tile, q):
                ge(pool, comb2, n - 1)
                gather_rows_of(row_all[:, tile, :], q, 1)

            def gather_y(n, q, g):
                ge(pool, comb2, n + 1)
                pass_held(pool, "pool")
                nc.gpsimd.tensor_copy(cidx[:, q, :], row_all[:, bass.ds(n, 1), :].rearrange("p n k -> p (n k)")).then_inc(cidx_ready, 1)
                ge(pool, cidx_ready, n + 1)
                pass_held(pool, "pool")
                gather_rows_of(cidx[:, q, :], q, g)

            def gather_rows_of(row, q, g):
                for kk_, (buf, s) in enumerate(((y1g[q], y1_gathered[q]), (y2g[q], y2_gathered[q]))):
                    pool.indirect_dma_start(out=buf, out_offset=None, in_=y_dram[g],
                                            in_offset=bass.IndirectOffsetOnAxis(ap=row[:, kk_:kk_ + 1], axis=0)
                                            ).then_inc(s, 16)

            halves = [1, 2, 3, 4, 7, 8, 9, 10]

            def tile_body(t, comb, g):
                nxt = t + 3
                if isinstance(t.j, int):
                    g = nxt.n // TILES_G
                if isinstance(t.j, int) and nxt.n == TILES_G:
                    for q in range(2):
                        pool.wait_ge(z_stored[q], 16 * NB // 2)
                    pool.wait_ge(sched_ready, 4)
                gather(nxt, g)
                if isinstance(t.j, int) and t.n in halves:
                    if t.n == 3:
                        move_on(Step(NB // 2 - 2, 0))
                    block, half = divmod(halves.index(t.n), 2)
                    k = NB - 4 + block
                    scatter(Step(k // 2, k % 2), 1, [half])
                if isinstance(t.j, int) and t.n == 5:
                    move_on(Step(NB // 2 - 2, 1))
                if isinstance(t.j, int) and t.n == 12:
                    gather_rows(1)
                if isinstance(t.j, int) and t.n == TILES_G + 4:
                    for q in range(4):
                        pool.wait_ge(y_stored[q], 16 * ((TILES_G + 3 - q) // 4 + 1))
                if comb is not None and t.p < 2:
                    gather_y(2 * comb + t.p, t.p, 0)

            body(Step(-1, 1), 0)
            block_steps(pool, body)
            rstd2_of(Step(NB // 2 - 1, 1))
            tile_body(Tile(0, 0), None, 0)
            tile_body(Tile(0, 1), None, 0)
            tile_body(Tile(0, 2), None, 0)
            tile_steps(pool, tile_body)
            for q in range(4):
                pool.wait_ge(y_stored[q], 16 * ((TILES + 3 - q) // 4 + 1))
            for i in range(TILES_B // 4):
                for q in range(4):
                    gather_tail(TILES_B + 4 * i + q, TILES_B + 4 * q + i, q)

        @block.scalar
        def _(act):
            def copy(o, i, s):
                nc.scalar.activation(o, i, ACT.Copy).then_inc(s, 1)

            for g in range(NBATCH):
                act.wait_ge(ctx_turned, g + 1)
                copy(ctxT[:, :, g * KEYS:(g + 1) * KEYS], psT[g][:, :].rearrange("p (c k) -> p c k", c=DC), ctxT_ready)
            def split_key(m):
                act.wait_ge(k_done, m + 1)
                dst = lg if m % 2 == 0 else tl
                ge(act, k_lo, m - 1)
                nc.scalar.activation(dst[:, :], psQ[m % 2][:, 0:BT], ACT.Relu,
                                     bias=bk_sb[:, m:m + 1]).then_inc(k_relu, 1)
                act.wait_ge(k_relu, m + 1)
                copy(kpT[:, HI, m, :], dst[:, :], k_hi)

            def split_values():
                for g in range(NBATCH):
                    act.wait_ge(v_done, g + 1)
                    act.wait_ge(k_done, DC)
                    nc.scalar.activation(z[:, g, :], ps_out[g][:, :], ACT.Relu).then_inc(v_relu, 1)
                    act.wait_ge(v_relu, g + 1)
                    copy(vp[:, HI, g, :], z[:, g, :], v_hi)

            def norm1(b, t):
                ge(act, nmr1_ready, b.n + 1)
                ge(act, xn_turned, 2 * b.n)
                nc.scalar.activation(xn[:, t, :], xin[:, b.p, t, :], ACT.Identity, bias=nmr1[:, t:t + 1],
                                     scale=rstd1[:, t:t + 1]).then_inc(xn1_ready, 1)

            def turned_x(b):
                for t in range(TPB):
                    ge(act, xn_turned, 2 * b.n + t + 1)
                    ge(act, q_done, 4 * b.n)
                    copy(qT[:, HI, :, t * P:(t + 1) * P], psT[t][:, :].rearrange("p (c k) -> p c k", c=DC), qT_hi)

            def turned_g(t):
                ge(act, g_turned, t.n + 1)
                copy(zgT[t.r][:, :, 0:P], psT[t.r][:, :].rearrange("p (c k) -> p c k", c=DC), gT_hi)

            def turned_s(t):
                ge(act, s_turned, t.n + 1)
                copy(sT[t.r][:, HI, :], psST[t.r], sT_hi)

            def take_y(t):
                ge(act, y_done, t.n + 1)
                ge(act, y_stored[t.p], 16 * (t.j + 1))
                copy(ysb[t.p], ps_out[t.r][:, :], y_ready)

            def tile_body(t, comb, g):
                if isinstance(t.j, int) and t.n == TILES_G - 3:
                    act.wait_ge(route, ROUTE_STEPS * NB)
                    nc.scalar.activation(e_all[:, :], gap_all[:, :], ACT.Exp).then_inc(gap_exp, 1)
                ge(act, uv_done, t.n + 1)
                nc.scalar.activation(sil[:, t.r, :], psQ[t.r][:, 0:R], ACT.Silu).then_inc(silu_done, 1)
                if (t + 2).within(TILES):
                    turned_g(t + 2)
                if (t + (-1)).within(TILES):
                    take_y(t + (-1))
                turned_s(t)

            def turned_z(b, t):
                ge(act, z_turned, 2 * b.n + t + 1)
                ge(act, gate_done, b.n)
                copy(zT[:, :, t * P:(t + 1) * P], psZ[:, :].rearrange("p (c k) -> p c k", c=DC), zT_ready)

            def norm2(prv, t):
                if t == 0:
                    ge(act, nmr2_ready, prv.n + 1)
                    ge(act, z_turned, 2 * prv.n)
                    if (prv + (-1)).within(NB):
                        last = prv + (-1)
                        ge(act, z_stored[last.p], 16 * (last.j + 1))
                nc.scalar.activation(z[:, t, :], x1[:, t, :], ACT.Identity, bias=nmr2[:, t:t + 1],
                                     scale=rstd2[:, t:t + 1]).then_inc(z_ready, 1)

            def gate_logits(b):
                ge(act, gate_done, b.n + 1)
                ge(act, logit_turned, b.n)
                copy(logT[:, :], ps_log, logT_ready)

            def body(b, batch):
                nxt, prv, old = b + 1, b + (-1), b + (-2)

                def queries(m):
                    ge(act, q_done, 4 * b.n + m + 1)
                    ge(act, qp_lo, 4 * b.n + m - 1)
                    nc.scalar.activation(tq[:, m % 2, :], psQ[m % 2][:, 0:BT], ACT.Relu,
                                         bias=bq_sb[:, m:m + 1]).then_inc(qp_relu, 1)
                    ge(act, qp_relu, 4 * b.n + m + 1)
                    ge(act, s_done, b.n)
                    copy(qpT[:, HI, m, :], tq[:, m % 2, :], qp_hi)

                if old.within(NB):
                    turned_z(old, 1)
                if b.within(NB):
                    for m in range(DC):
                        queries(m)
                if prv.within(NB):
                    norm2(prv, 0)
                if old.within(NB):
                    gate_logits(old)
                if nxt.within(NB):
                    norm1(nxt, 1)
                if isinstance(b.j, int) and b.n == 0:
                    split_values()
                if b.within(NB):
                    ge(act, s_done, b.n + 1)
                    ge(act, lg_step, 3 * b.n)
                    nc.scalar.activation(tl[:, :], psS[:, 0:BT], ACT.Relu, scale=SCALE).then_inc(s_relu, 1)
                if nxt.within(NB):
                    turned_x(nxt)
                else:
                    act.wait_ge(q_done, 4 * NB)
                    turned_g(Tile(0, 0))
                    turned_g(Tile(0, 1))
                if prv.within(NB):
                    norm2(prv, 1)
                    turned_z(prv, 0)
                if b.within(NB):
                    for dst, src in expert_parts(b):
                        ge(act, stage_loaded, 48 * (b.j + 1))
                        pass_held(act, "act")
                        copy(dst(HI), src, stage_hi)

            act.wait_ge(w_loaded["small"], 64)
            norm1(Step(0, 0), 1)
            split_key(0)
            split_key(1)
            turned_x(Step(0, 0))
            act.wait_ge(w_loaded["wq"], 16)
            for c in range(DC):
                copy(wq[:, HI, c, :], wraw[:, c * D:(c + 1) * D], wq_hi)
            split_key(2)
            split_key(3)
            block_steps(act, body)
            act.wait_ge(s_done, NB)
            act.wait_ge(o_done, 2 * NB)
            last = Step(NB // 2 - 1, 1)
            turned_z(last + (-1), 1)
            gate_logits(last + (-1))
            norm2(last, 0)
            norm2(last, 1)
            turned_z(last, 0)
            tile_body(Tile(0, 0), None, 0)
            turned_z(last, 1)
            tile_body(Tile(0, 1), None, 0)
            gate_logits(last)
            tile_body(Tile(0, 2), None, 0)
            tile_steps(act, tile_body)
            take_y(Tile(TILES // 4, TILES % 4) + (-1))

        @block.vector
        def _(dve):
            def sub(o, a, b, s):
                nc.vector.tensor_tensor(o, a, b, ALU.subtract).then_inc(s, 1)

            dve.sem_inc(comb2, 2)
            dve.wait_ge(const_ready, 10)
            nc.vector.tensor_copy(iota_f[:, :, :, :], iota_i[:, :, :, :]).then_inc(conv_ready, 1)
            nc.vector.tensor_copy(base0[:, :], base_i[:, :]).then_inc(conv_ready, 1)
            nc.vector.tensor_copy(base[:, :], base_i[:, :]).then_inc(conv_ready, 1)
            nc.vector.tensor_copy(tile_s[:, :], tile_i[:, :]).then_inc(conv_ready, 1)
            dve.wait_ge(conv_ready, 4)

            def split_key(m):
                dve.wait_ge(k_hi, m + 1)
                sub(kpT[:, LO, m, :], (lg if m % 2 == 0 else tl)[:, :], kpT[:, HI, m, :], k_lo)

            planned = [0]

            def link(ins):
                ins.then_inc(plan, 1)
                planned[0] += 1
                dve.wait_ge(plan, planned[0])

            def plan_lengths(g):
                link(nc.vector.scalar_tensor_tensor(cnt[:, :], base[:, :], float(P - 1), base0[:, :], ALU.add, ALU.subtract))
                link(nc.vector.tensor_copy(cnt_i[:, :], cnt[:, :]))
                link(nc.vector.tensor_scalar(len_i[:, :], cnt_i[:, :], LOG_P, LOG_P,
                                             ALU.logical_shift_right, ALU.logical_shift_left))
                link(nc.vector.tensor_copy(length[:, :], len_i[:, :]))
                link(nc.vector.tensor_tensor(lens[:, :, :], upto_e[:, :, :],
                                             length[:, :].unsqueeze(1).broadcast_to([P, E, E]), ALU.mult))
                link(nc.vector.tensor_reduce(cum[:, :], lens[:, :, :], AX.X, ALU.add))
                if g == 0:
                    nc.vector.tensor_copy(base[:, :], base0[:, :]).then_inc(regroup, 1)
                    dve.wait_ge(regroup, 1)

            def plan_experts(g):
                link(nc.vector.tensor_scalar(past[:, :], cum[:, :], tile_s[:, 0:1], None, ALU.is_le))
                link(nc.vector.tensor_tensor(pastc[:, :], past[:, :], cum[:, :], ALU.mult))
                link(nc.vector.tensor_reduce(exp_f[:, :], past[:, :], AX.X, ALU.add))
                link(nc.vector.tensor_reduce(prev_f[:, :], pastc[:, :], AX.X, ALU.max))

            def plan_slots(g):
                link(nc.vector.tensor_tensor(off_f[:, :], tile_s[:, :], prev_f[:, :], ALU.subtract))
                link(nc.vector.scalar_tensor_tensor(row_f[:, :], exp_f[:, :], float(CAP), off_f[:, :], ALU.mult, ALU.add))
                link(nc.vector.tensor_scalar(over_f[:, :], exp_f[:, :], float(E), float(DUMMY), ALU.is_ge, ALU.mult))
                link(nc.vector.tensor_tensor(row2_f[:, :], row_f[:, :], over_f[:, :], ALU.add))
                link(nc.vector.tensor_scalar(table_row[:, g:g + 1], row2_f[:, :], float(DUMMY), 1.0 / P, ALU.min, ALU.mult))
                link(nc.vector.tensor_scalar(expc_f[:, g:g + 1], exp_f[:, :], float(E - 1), None, ALU.min))

            def plan_rows(g):
                ex = expert_all[:, g * TILES_B:(g + 1) * TILES_B, :].rearrange("p n k -> p (n k)")
                sl = dest_all[:, g * TILES_B:(g + 1) * TILES_B, :].rearrange("p n k -> p (n k)")
                rw = row_all[:, g * TILES_B:(g + 1) * TILES_B, :].rearrange("p n k -> p (n k)")
                wide = [P, 2 * TILES_B, E]
                link(nc.vector.tensor_tensor(before_e[:, :], cum[:, :], length[:, :], ALU.subtract))
                link(nc.vector.tensor_tensor(shift_e[:, :], before_e[:, :], base0[:, :], ALU.subtract))
                link(nc.vector.tensor_tensor(plan_big[0], iota_f[:, 0, 0, :].unsqueeze(1).broadcast_to(wide),
                                             ex.unsqueeze(2).broadcast_to(wide), ALU.is_equal))
                link(nc.vector.tensor_tensor(plan_big[1], plan_big[0], shift_e[:, :].unsqueeze(1).broadcast_to(wide), ALU.mult))
                link(nc.vector.tensor_reduce(shift_t[:, :], plan_big[1], AX.X, ALU.add))
                link(nc.vector.tensor_tensor(rw, sl, shift_t[:, :], ALU.add))

            def add_attention(b):
                for t in range(TPB):
                    ge(dve, o_done, 2 * b.n + t + 1)
                    if t == 0:
                        ge(dve, z_ready, 2 * b.n)
                        last = b + (-1)
                        if last.within(NB):
                            ge(dve, x1_stored[last.p], 16 * (last.j + 1))
                    nc.vector.scalar_tensor_tensor(x1[:, t, :], ps_out[t][:, :], 0.0, xin[:, b.p, t, :],
                                                   ALU.max, ALU.add).then_inc(x1_ready, 1)

            class Norm:

                def __init__(self, b, src, st, mv, ve, nmr, rstd, s, rstd_ready, nmr_ready, used, uses):
                    self.b, self.src, self.st, self.mv, self.ve, self.nmr, self.rstd = b, src, st, mv, ve, nmr, rstd
                    self.s, self.rstd_ready, self.nmr_ready = s, rstd_ready, nmr_ready
                    self.used, self.uses = used, uses

                def sums(self, t):
                    nc.vector.bn_stats(self.st[:, t, :], self.src(t)).then_inc(self.s, 1)

                def moments(self, t):
                    ge(dve, self.s, 5 * self.b.n + 2 * t + 1)
                    pass_held(dve, "dve")
                    nc.vector.bn_aggr(self.mv[:, t, :], self.st[:, t, :]).then_inc(self.s, 1)

                def variance(self):
                    ge(dve, self.s, 5 * self.b.n + 4)
                    nc.vector.tensor_scalar(self.ve[:, :], self.mv[:, :, 1], EPS, None, ALU.add).then_inc(self.s, 1)

                def shift(self):
                    ge(dve, self.rstd_ready, self.b.n + 1)
                    ge(dve, self.used, self.uses * self.b.n)
                    nc.vector.scalar_tensor_tensor(self.nmr[:, :], self.mv[:, :, 0], -1.0, self.rstd[:, :],
                                                   ALU.mult, ALU.mult).then_inc(self.nmr_ready, 1)

            class Choose:

                def __init__(self, b):
                    self.b, self.n = b, ROUTE_STEPS * b.n

                def all(self):
                    self.logits()
                    self.values()
                    self.indices()
                    self.floats()
                    self.one_hot()
                    self.both()

                def logits(self):
                    ge(dve, logit_turned, self.b.n + 1)
                    nc.vector.tensor_copy(logit[:, :, :], ps_logit).then_inc(route, 1)

                def values(self):
                    ge(dve, route, self.n + 1)
                    pass_held(dve, "dve")
                    for t in range(TPB):
                        nc.vector.max(top_v[:, t, :], logit[:, t, :]).then_inc(route, 1)

                def indices(self):
                    ge(dve, route, self.n + 3)
                    pass_held(dve, "dve")
                    for t in range(TPB):
                        nc.vector.max_index(top_i[:, t, :], top_v[:, t, :], logit[:, t, :]).then_inc(route, 1)

                def floats(self):
                    b = self.b
                    gap = gap_all[:, 2 * b.n:2 * b.n + 2] if isinstance(b.j, int) else gap_all[:, bass.ds(b.n * 2, 2)]
                    nc.vector.tensor_tensor(gap, top_v[:, :, 1], top_v[:, :, 0], ALU.subtract).then_inc(route, 1)
                    ge(dve, route, self.n + 5)
                    nc.vector.tensor_copy(top_f[:, :, :], top_i[:, :, 0:2]).then_inc(route, 1)

                def one_hot(self):
                    ge(dve, route, self.n + 7)
                    nc.vector.tensor_tensor(onehot[:, :, :, :], iota_f[:, :, :, :],
                                            top_f[:, :, :].unsqueeze(3).broadcast_to([P, TPB, 2, E]),
                                            ALU.is_equal).then_inc(route, 1)

                def both(self):
                    b = self.b
                    ge(dve, route, self.n + 8)
                    ge(dve, rank_done, b.n)
                    nc.vector.tensor_tensor(chosen[:, :, :], onehot[:, :, 0, :], onehot[:, :, 1, :], ALU.add).then_inc(route, 1)
                    ea = (expert_all[:, 2 * b.n:2 * b.n + 2, :] if isinstance(b.j, int)
                          else expert_all[:, bass.ds(b.n * 2, 2), :])
                    nc.vector.tensor_copy(ea, top_f[:, :, :]).then_inc(route, 1)

            class Place:

                def __init__(self, b):
                    self.b, self.n = b, PLACE_STEPS * b.n

                def ranks(self):
                    ge(dve, rank_done, self.b.n + 1)
                    nc.vector.tensor_tensor(pos[:, :, :], ps_pos, base[:, :].unsqueeze(1).broadcast_to([P, TPB, E]),
                                            ALU.add).then_inc(place, 1)

                def picked(self):
                    ge(dve, place, self.n + 1)
                    nc.vector.tensor_tensor(posk[:, :, :, :], onehot[:, :, :, :],
                                            pos[:, :, :].unsqueeze(2).broadcast_to([P, TPB, 2, E]), ALU.mult).then_inc(place, 1)
                    nc.vector.tensor_tensor(base[:, :], base[:, :], ps_tot, ALU.add).then_inc(place, 1)

                def slots(self):
                    ge(dve, place, self.n + 3)
                    nc.vector.tensor_reduce(destf[:, :, :], posk[:, :, :, :], AX.X, ALU.add).then_inc(place, 1)

                def write(self):
                    b, n = self.b, self.n
                    ge(dve, place, n + 4)
                    ge(dve, tokid_moved, b.n + 1)
                    nc.vector.tensor_copy(dest[:, b.p, :, :], destf[:, :, :]).then_inc(place, 1)
                    da = (dest_all[:, 2 * b.n:2 * b.n + 2, :] if isinstance(b.j, int)
                          else dest_all[:, bass.ds(b.n * 2, 2), :])
                    nc.vector.tensor_copy(da, destf[:, :, :]).then_inc(place, 1)

            def turned_g(t):
                ge(dve, gT_hi, t.n + 1)
                sub(zgT[t.r][:, :, P:2 * P], psT[t.r][:, :].rearrange("p (c k) -> p c k", c=DC),
                    zgT[t.r][:, :, 0:P], gT_lo)

            def combine(n, q, k, x1_tile_sb, w_at):
                w = [w_all[:, j, bass.ds(w_at, 1)] for j in range(2)]
                ge(dve, y1_gathered[q], 16 * (k + 1))
                nc.vector.scalar_tensor_tensor(y1g[q], y1g[q], w[0], x1_tile_sb, ALU.mult, ALU.add).then_inc(comb1, 1)
                ge(dve, y2_gathered[q], 16 * (k + 1))
                ge(dve, comb1, n + 1)
                nc.vector.scalar_tensor_tensor(xg[q], y2g[q], w[1], y1g[q], ALU.mult, ALU.add).then_inc(comb2, 1)

            def weights():
                dve.wait_ge(gap_exp, 1)
                nc.vector.tensor_scalar(den_all[:, :], e_all[:, :], 1.0, None, ALU.add).then_inc(weight, 1)
                dve.wait_ge(weight, 1)
                nc.vector.reciprocal(w_all[:, 0, :], den_all[:, :]).then_inc(weight, 1)
                dve.wait_ge(weight, 2)
                nc.vector.tensor_tensor(w_all[:, 1, :], e_all[:, :], w_all[:, 0, :], ALU.mult).then_inc(weight, 1)
                dve.wait_ge(weight, 3)

            def make_sched(g):
                dve.wait_ge(rows_gathered, 16 * (g + 1))
                nc.vector.tensor_copy(slot_rows_f[0:TILES_G, :], slot_rows[0:TILES_G, :]).then_inc(rows_float, 1)

            def keep_sched(g):
                dve.wait_ge(rows_turned, g + 1)
                bank = ps_sched[g]
                nc.vector.tensor_scalar(idx_all[:, g * TILES_G:(g + 1) * TILES_G], bank[:, 0:TILES_G],
                                        float(-g * SEQ), 0.0, ALU.add, ALU.max).then_inc(sched_ready, 1)
                nc.vector.tensor_copy(sched_exp[:, g * TILES_G:(g + 1) * TILES_G], bank[0:1, P:P + TILES_G]).then_inc(sched_ready, 1)

            def tile_body(t, comb, g):
                if isinstance(t.j, int) and t.n == 5:
                    put = Place(Step(NB // 2 - 1, 1))
                    Place(Step(NB // 2 - 1, 0)).write()
                    put.ranks()
                    put.picked()
                    put.slots()
                if isinstance(t.j, int) and t.n == 6:
                    Place(Step(NB // 2 - 1, 1)).write()
                    dve.wait_ge(place, PLACE_STEPS * NB)
                    dve.wait_ge(route, ROUTE_STEPS * NB)
                if isinstance(t.j, int) and t.n == 7:
                    plan_lengths(1)
                if isinstance(t.j, int) and t.n == 8:
                    plan_experts(1)
                if isinstance(t.j, int) and t.n == 9:
                    plan_slots(1)
                if isinstance(t.j, int) and t.n == 10:
                    plan_rows(1)
                if isinstance(t.j, int) and t.n == TILES_G - 1:
                    weights()
                    dve.wait_ge(x1_back, 16 * 6)
                if isinstance(t.j, int) and t.n == 14:
                    make_sched(1)
                if isinstance(t.j, int) and t.n == 15:
                    keep_sched(1)
                ge(dve, silu_done, t.n + 1)
                nc.vector.tensor_tensor(s_tok[:, t.r, :], sil[:, t.r, :], psQ[t.r][:, R:2 * R], ALU.mult).then_inc(s_ready, 1)
                if (t + 2).within(TILES):
                    turned_g(t + 2)
                ge(dve, sT_hi, t.n + 1)
                sub(sT[t.r][:, LO, :], psST[t.r], sT[t.r][:, HI, :], sT_lo)
                if comb is not None and t.p >= 2:
                    q = t.p - 2
                    if q == 0:
                        ge(dve, out_stored[0], 16 * (comb + 1))
                        mine = x1_first[:, bass.ds(comb, 1), :].rearrange("p n d -> p (n d)")
                    else:
                        ge(dve, xg_loaded[1], 16 * (comb + 1))
                        mine = xg[1]
                    combine(2 * comb + q, q, comb, mine, 2 * comb + q)

            def norm1_of(b):
                return Norm(b, lambda t: xin[:, b.p, t, :], st1, mv1, ve1, nmr1, rstd1, stats1, rstd1_ready,
                            nmr1_ready, xn1_ready, 1)

            def norm_x(b):
                ge(dve, xn_turned, 2 * b.n)
                nc.vector.tensor_scalar(xn[:, 0, :], xin[:, b.p, 0, :], mv1[:, 0, 0:1], rstd1[:, 0:1],
                                        ALU.subtract, ALU.mult).then_inc(xn0_ready, 1)

            def turned_x(b, t):
                ge(dve, qT_hi, 2 * b.n + t + 1)
                ge(dve, q_done, 4 * b.n)
                sub(qT[:, LO, :, t * P:(t + 1) * P], psT[t][:, :].rearrange("p (c k) -> p c k", c=DC),
                    qT[:, HI, :, t * P:(t + 1) * P], qT_lo)

            def norm2_of(b):
                return Norm(b, lambda t: x1[:, t, :], st2, mv2, ve2, nmr2, rstd2, stats2, rstd2_ready, nmr2_ready, z_ready, 2)

            def body(b, batch):
                nxt, prv, old, third = b + 1, b + (-1), b + (-2), b + (-3)
                b_in, nxt_in, prv_in, old_in, third_in = (s.within(NB) for s in (b, nxt, prv, old, third))
                norm2 = norm2_of(prv)
                norm1 = norm1_of(nxt)
                choose, put = Choose(old), Place(third)

                def low(m):
                    ge(dve, qp_hi, 4 * b.n + m + 1)
                    ge(dve, s_done, b.n)
                    sub(qpT[:, LO, m, :], tq[:, m % 2, :], qpT[:, HI, m, :], qp_lo)

                if not nxt_in:
                    make_sched(0)
                if prv_in:
                    add_attention(prv)
                    if not nxt_in:
                        keep_sched(0)
                    ge(dve, rstd2_ready, prv.n)
                    ge(dve, x1_ready, 2 * prv.n + 1)
                    norm2.sums(0)
                if third_in:
                    put.ranks()
                if prv_in:
                    norm2.moments(0)
                    ge(dve, x1_ready, 2 * prv.n + 2)
                    norm2.sums(1)
                if third_in:
                    put.picked()
                if prv_in:
                    norm2.moments(1)
                if third_in:
                    put.slots()
                if prv_in:
                    norm2.variance()
                if b_in:
                    low(0)
                ends_group = isinstance(third.j, int) and third.n == NB_G - 1
                if third_in:
                    put.write()
                if ends_group:
                    dve.wait_ge(place, PLACE_STEPS * NB_G)
                    dve.wait_ge(route, ROUTE_STEPS * NB_G)
                    plan_lengths(0)
                if b_in:
                    low(1)
                if prv_in:
                    norm2.shift()
                if ends_group:
                    plan_experts(0)
                if nxt_in:
                    ge(dve, x_loaded[nxt.p], 16 * (nxt.j + 1))
                    ge(dve, rstd1_ready, nxt.n)
                    norm1.sums(0)
                if b_in:
                    low(2)
                if nxt_in:
                    norm1.moments(0)
                    norm1.sums(1)
                if b_in:
                    low(3)
                if nxt_in:
                    norm1.moments(1)
                    norm1.variance()
                if ends_group:
                    plan_slots(0)
                if nxt_in:
                    norm1.shift()
                    norm_x(nxt)
                if isinstance(b.j, int) and b.n == 0:
                    for g in range(NBATCH):
                        dve.wait_ge(v_hi, g + 1)
                        sub(vp[:, LO, g, :], z[:, g, :], vp[:, HI, g, :], v_lo)
                if b_in:
                    ge(dve, s_relu, b.n + 1)
                    nc.vector.tensor_tensor(lg[:, :], tl[:, :], ps_mask, ALU.add).then_inc(lg_step, 1)
                if old_in:
                    choose.logits()
                if b_in:
                    ge(dve, lg_step, 3 * b.n + 1)
                    ge(dve, o_done, 2 * b.n)
                    nc.vector.tensor_copy(lgT[:, HI, :], lg[:, :]).then_inc(lg_step, 1)
                if old_in:
                    choose.values()
                if b_in:
                    ge(dve, lg_step, 3 * b.n + 2)
                    sub(lgT[:, LO, :], lg[:, :], lgT[:, HI, :], lg_step)
                if old_in:
                    choose.indices()
                for t in range(TPB):
                    if nxt_in:
                        turned_x(nxt, t)
                    else:
                        turned_g(Tile(0, t))
                    if old_in and t == 0:
                        choose.floats()
                        choose.one_hot()
                if old_in:
                    choose.both()
                if ends_group:
                    plan_rows(0)

            first = Step(0, 0)
            norm1 = norm1_of(first)
            dve.wait_ge(x_loaded[0], 16)
            norm1.sums(0)
            norm1.moments(0)
            norm1.sums(1)
            norm1.moments(1)
            norm1.variance()
            norm1.shift()
            norm_x(first)
            split_key(0)
            split_key(1)
            for t in range(TPB):
                turned_x(first, t)
            for c in range(DC):
                dve.wait_ge(wq_hi, c + 1)
                sub(wq[:, LO, c, :], wraw[:, c * D:(c + 1) * D], wq[:, HI, c, :], wq_ready)
            split_key(2)
            split_key(3)
            block_steps(dve, body)
            last = Step(NB // 2 - 1, 1)
            norm2, put = norm2_of(last), Place(last + (-2))
            add_attention(last)
            ge(dve, rstd2_ready, last.n)
            dve.wait_ge(x1_ready, 2 * last.n + 1)
            norm2.sums(0)
            put.ranks()
            norm2.moments(0)
            dve.wait_ge(x1_ready, 2 * last.n + 2)
            norm2.sums(1)
            put.picked()
            norm2.moments(1)
            put.slots()
            norm2.variance()
            put.write()
            norm2.shift()
            tile_body(Tile(0, 0), None, 0)
            Choose(last + (-1)).all()
            tile_body(Tile(0, 1), None, 0)
            put = Place(last + (-1))
            put.ranks()
            put.picked()
            put.slots()
            Choose(last).all()
            tile_body(Tile(0, 2), None, 0)
            tile_steps(dve, tile_body)
            with dve.Fori(0, 4) as i:
                for q in range(4):
                    dve.wait_ge(out_stored[q], 16 * (i + used(q) + 1))
                    combine(TILES_B + 4 * i + q, q, i + used(q),
                            x1_kept[q][:, bass.ds(i, 1), :].rearrange("p n d -> p (n d)"), TILES_B + 4 * q + i)

        @block.tensor
        def _(pe):
            def turn(o, i, n=P):
                return pe.transpose(o, i, ident[0:n, 0:n])

            def three(o, w, a, first, last):
                pe.matmul(o, w[LO], a[HI], start=first, stop=False)
                pe.matmul(o, w[HI], a[LO], start=False, stop=False)
                return pe.matmul(o, w[HI], a[HI], start=False, stop=last)

            pe.wait_ge(const_ready, 10)
            pe.wait_ge(w_loaded["ctx"], 16)
            for g in range(NBATCH):
                for c in range(DC):
                    ins = turn(psT[g][:, c * P:(c + 1) * P], ctx_raw[:, g, c * P:(c + 1) * P])
                ins.then_inc(ctx_turned, 1)
            def values():
                pe.wait_ge(w_loaded["wv"], 32)
                pe.wait_ge(w_loaded["small"], 64)
                for g in range(NBATCH):
                    pe.matmul(ps_out[g][:, :], ones_row[:, :], bv_sb[:, :], start=True, stop=False)
                    for c in range(DC):
                        w = stage[:, c * D:(c + 1) * D] if c < 3 else wraw[:, 0:D]
                        ins = pe.matmul(ps_out[g][:, :], ctxT[:, c, g * KEYS:(g + 1) * KEYS], w, start=False, stop=(c == DC - 1))
                    ins.then_inc(v_done, 1)

            def queries(b):
                ge(pe, qT_lo, 2 * b.n + 2)
                if isinstance(b.j, int) and b.n == 0:
                    pe.wait_ge(wq_ready, DC)
                    pe.wait_ge(k_relu, DC)
                for m in range(DC):
                    ge(pe, qp_relu, 4 * b.n + m - 1)
                    for c in range(DC):
                        ins = three(psQ[m % 2][:, 0:BT],
                                    [wq[:, h, c, m * P:(m + 1) * P] for h in range(2)],
                                    [qT[:, h, c, :] for h in range(2)], c == 0, c == DC - 1)
                    ins.then_inc(q_done, 1)

            def ranks(b):
                ge(pe, route, ROUTE_STEPS * b.n + 9)
                ge(pe, place, PLACE_STEPS * (b.n - 1) + 3)
                for t in range(TPB):
                    for u in range(t):
                        pe.matmul(ps_pos[:, t, :], ones[:, :], chosen[:, u, :], start=(u == 0), stop=False)
                    pe.matmul(ps_pos[:, t, :], before[:, :], chosen[:, t, :], start=(t == 0), stop=True)
                for t in range(TPB):
                    ins = pe.matmul(ps_tot, ones[:, :], chosen[:, t, :], start=(t == 0), stop=(t == TPB - 1))
                ins.then_inc(rank_done, 1)

            def turn_z(b, t):
                ge(pe, z_ready, 2 * b.n + t + 1)
                ge(pe, zT_ready, 2 * b.n + t)
                for c in range(DC):
                    ins = turn(psZ[:, c * P:(c + 1) * P], z[:, t, c * P:(c + 1) * P])
                ins.then_inc(z_turned, 1)

            def turn_masks(b):
                ge(pe, m_loaded[b.p], 16 * (b.j + 1))
                ge(pe, x1_ready, 2 * b.n)
                if isinstance(b.j, int) and b.n == 0:
                    pe.wait_ge(k_lo, DC)
                    pe.wait_ge(v_relu, 2)
                for t in range(TPB):
                    turn(ps_mask[:, t * P:(t + 1) * P], mraw[:, b.p, t, :])

            def scores(b, batch):
                ge(pe, qp_lo, 4 * b.n + 4)
                for c in range(DC):
                    ins = three(psS[:, 0:BT], [kpT[:, h, c, batch * KEYS:(batch + 1) * KEYS] for h in range(2)],
                                [qpT[:, h, c, :] for h in range(2)], c == 0, c == DC - 1)
                ins.then_inc(s_done, 1)

            def turn_x(b):
                ge(pe, qT_lo, 2 * b.n)
                for t in range(TPB):
                    ge(pe, (xn0_ready, xn1_ready)[t], b.n + 1)
                    if t == 0:
                        pass_held(pe, "pe")
                    for c in range(DC):
                        ins = turn(psT[t][:, c * P:(c + 1) * P], xn[:, t, c * P:(c + 1) * P])
                    ins.then_inc(xn_turned, 1)

            def gates(b):
                ge(pe, zT_ready, 2 * b.n + 2)
                ge(pe, logT_ready, b.n)
                ge(pe, place, PLACE_STEPS * (b.n - 1) + 3)
                for c in range(DC):
                    ins = pe.matmul(ps_log, gw[:, c, :], zT[:, c, :], start=(c == 0), stop=(c == DC - 1))
                ins.then_inc(gate_done, 1)

            def attend(b, batch):
                ge(pe, lg_step, 3 * b.n + 3)
                ge(pe, x1_ready, 2 * b.n)
                if isinstance(b.j, int) and b.n == 0:
                    pe.wait_ge(v_lo, 2)
                for t in range(TPB):
                    three(ps_out[t][:, :], [lgT[:, h, t * P:(t + 1) * P] for h in range(2)],
                          [vp[:, h, batch, :] for h in range(2)], True, True).then_inc(o_done, 1)

            def turn_logits(b):
                ge(pe, logT_ready, b.n + 1)
                ge(pe, route, ROUTE_STEPS * (b.n - 1) + 1)
                pass_held(pe, "pe")
                for t in range(TPB):
                    ins = turn(ps_logit[:, t, :], logT[:, t * P:(t + 1) * P], E)
                ins.then_inc(logit_turned, 1)

            def turn_g(t):
                ge(pe, z_gathered[t.p], 16 * (t.j + 1))
                for c in range(DC):
                    ins = turn(psT[t.r][:, c * P:(c + 1) * P], zg[t.p][:, c * P:(c + 1) * P])
                ins.then_inc(g_turned, 1)

            def load_expert(t):
                return pe.value_load(sched_exp[0:1, bass.ds(t.n, 1)], min_val=0, max_val=E - 1)

            def up(t, e):
                ge(pe, gT_lo, t.n + 1)
                for c in range(DC):
                    w = [wuv[:, bass.ds(e, 1), h, 2 * R * c:2 * R * (c + 1)].rearrange("p e n -> p (e n)") for h in range(2)]
                    a = [zgT[t.r][:, c, h * P:(h + 1) * P] for h in range(2)]
                    ins = three(psQ[t.r][:, 0:2 * R], a, w, c == 0, c == DC - 1)
                ins.then_inc(uv_done, 1)

            def down(t, e):
                ge(pe, sT_lo, t.n + 1)
                ge(pe, y_ready, t.n - 1)
                w = [wo[:, bass.ds(e, 1), h, :].rearrange("p e n -> p (e n)") for h in range(2)]
                three(ps_out[t.r][:, :], [sT[t.r][:, h, :] for h in range(2)], w, True, True).then_inc(y_done, 1)

            def turn_s(t):
                ge(pe, s_ready, t.n + 1)
                turn(psST[t.r], s_tok[:, t.r, :]).then_inc(s_turned, 1)

            def turn_sched(g):
                pe.wait_ge(rows_float, g + 1)
                pe.wait_ge(plan, PLAN_STEPS * g + SCHED_STEPS)
                ge(pe, qT_lo, 2 * NB)
                ge(pe, place, PLACE_STEPS * g * NB)
                bank = ps_sched[g]
                turn(bank[:, 0:TILES_G], slot_rows_f[0:TILES_G, :], TILES_G)
                turn(bank[0:1, P:2 * P], expc_f[:, g:g + 1]).then_inc(rows_turned, 1)

            expert = {}

            def expert_of(t):
                if t.p not in expert:
                    expert[t.p] = load_expert(t)
                return expert[t.p]

            def tile_body(t, comb, g):
                last, nxt = t + (-1), t + 1
                if (t + 2).within(TILES):
                    turn_g(t + 2)
                if last.within(TILES):
                    down(last, expert_of(last))
                    del expert[last.p]
                if nxt.within(TILES):
                    expert_of(nxt)
                turn_s(t)
                if isinstance(t.j, int) and t.n == 14:
                    turn_sched(1)
                if isinstance(t.j, int) and t.n == 15:
                    pe.wait_ge(sched_ready, 4)
                if nxt.within(TILES):
                    up(nxt, expert_of(nxt))

            def body(b, batch):
                nxt, prv, old = b + 1, b + (-1), b + (-2)
                if not nxt.within(NB):
                    turn_sched(0)
                    pe.wait_ge(sched_ready, 2)
                if b.within(NB):
                    queries(b)
                if old.within(NB):
                    gates(old)
                if isinstance(b.j, int) and b.n == 0:
                    values()
                if b.within(NB):
                    turn_masks(b)
                    scores(b, batch)
                if nxt.within(NB):
                    turn_x(nxt)
                else:
                    turn_g(Tile(0, 0))
                    turn_g(Tile(0, 1))
                if old.within(NB):
                    turn_logits(old)
                if prv.within(NB):
                    turn_z(prv, 0)
                if b.within(NB):
                    attend(b, batch)
                if prv.within(NB):
                    turn_z(prv, 1)
                if old.within(NB):
                    ranks(old)

            pe.wait_ge(ctxT_ready, 2)
            pe.wait_ge(w_loaded["wk0"], 16)
            pe.wait_ge(w_loaded["wk1"], 16)
            for m in range(DC):
                ge(pe, k_relu, m - 1)
                for c in range(DC):
                    w = z if c < 2 else x1
                    ins = pe.matmul(psQ[m % 2][:, 0:BT], w[:, c % 2, m * P:(m + 1) * P],
                                    ctxT[:, c, :], start=(c == 0), stop=(c == DC - 1))
                ins.then_inc(k_done, 1)
                if m == 1:
                    turn_x(Step(0, 0))
            block_steps(pe, body)
            last = Step(NB // 2 - 1, 1)
            gates(last + (-1))
            pe.wait_ge(stage_lo, 3 * E)
            up(Tile(0, 0), load_expert(Tile(0, 0)))
            turn_logits(last + (-1))
            turn_z(last, 0)
            tile_body(Tile(0, 0), None, 0)
            turn_z(last, 1)
            ranks(last + (-1))
            pe.wait_ge(x1_ready, 2 * NB)
            tile_body(Tile(0, 1), None, 0)
            gates(last)
            turn_logits(last)
            tile_body(Tile(0, 2), None, 0)
            ranks(last)
            tile_steps(pe, tile_body, fours=2, enter=expert.clear)
            last = Tile(TILES // 4, TILES % 4) + (-1)
            down(last, expert_of(last))


_INS = ['x', 'ctx_1024', 'mask_1xSxS2_ff0', 'L0_xattn_kernel_q', 'L0_xattn_kernel_k', 'L0_xattn_kernel_v',
        'L0_xattn_bias_q', 'L0_xattn_bias_k', 'L0_xattn_bias_v', 'L0_ffn_gate_w', 'L0_ffn_Wu', 'L0_ffn_Wv', 'L0_ffn_Wo']
_OUTS = [((NBATCH, SEQ, D), 'float32')]


def kernel(**inputs):
    import numpy as _np
    import concourse.bacc as _bacc
    from concourse import mybir as _mybir
    from concourse.bass_utils import run_bass_kernel_spmd as _run

    nc = _bacc.Bacc("TRN2", target_bir_lowering=False, num_devices=1)
    arrays, args = {}, []
    for name in _INS:
        a = _np.ascontiguousarray(inputs[name])
        arrays[f"in_{name}_dram"] = a
        args.append(nc.dram_tensor(f"in_{name}_dram", a.shape, _mybir.dt.from_np(a.dtype), kind="ExternalInput").ap())
    for i, (shape, dtype) in enumerate(_OUTS):
        dt = _mybir.dt.from_np(_np.dtype(dtype))
        args.append(nc.dram_tensor(f"out_{i}_dram", shape, dt, kind="ExternalOutput").ap())
    moe_block(nc, *args)
    r = _run(nc, [arrays], core_ids=[0])
    return r.results[0]["out_0_dram"]
```
